# Optimizing a Trainium2 kernel written in Bass

```python
import numpy as np
import jax
import jax.numpy as jnp

def _softmax(x, axis=-1):
    return jax.nn.softmax(x, axis=axis)

def _gelu(x):
    return jax.nn.gelu(x, approximate=True)

def _silu(x):
    return jax.nn.silu(x)

def _sigmoid(x):
    return jax.nn.sigmoid(x)

def _layernorm(x, axis=-1, eps=1e-05):
    m = jnp.mean(x, axis=axis, keepdims=True)
    v = jnp.var(x, axis=axis, keepdims=True)
    return (x - m) / jnp.sqrt(v + eps)

def _scatter_add(tgt, idx, src, axis=0):
    return tgt.at[idx].add(src)

def _segment_sum(src, seg, n):
    return jax.ops.segment_sum(src, seg, n)
kernel_name = 'mk_decoder_postln_d2_seqx_r8_d24c43'

def setup_inputs(seed: int=0):
    np.random.seed(seed)
    _w = jnp.asarray

    def _rec_inputs():
        import jax
        import jax.numpy as jnp
        _rk = jax.random.key(seed)
        x = -0.0003929 + 0.9999 * jax.random.normal(jax.random.fold_in(_rk, 1), (8, 256, 256), jnp.float32)
        _lenS = 256 - jax.random.randint(jax.random.fold_in(_rk, 7), (8,), 0, max(1, 256 // 4) + 1, jnp.int32)
        _lenS2 = 64 - jax.random.randint(jax.random.fold_in(_rk, 8), (8,), 0, max(1, 64 // 4) + 1, jnp.int32)
        _ctx_1024P = jax.random.normal(jax.random.fold_in(_rk, 11), (8, 16, 128), jnp.float32)
        _ctx_1024c = jax.random.dirichlet(jax.random.fold_in(_rk, 511), 0.3 * jnp.ones((16,), jnp.float32), (8, 64))
        _ctx_1024t = jnp.einsum('bsk,bkd->bsd', _ctx_1024c, _ctx_1024P)
        _ctx_1024t = _ctx_1024t * jax.lax.rsqrt(jnp.mean(jnp.square(_ctx_1024t)) + 1e-12) * 0.953939
        ctx_1024 = -0.000494167 + 1.00018 * (_ctx_1024t + 0.3 * jax.random.normal(jax.random.fold_in(_rk, 611), (8, 64, 128), jnp.float32))
        _validS = jnp.arange(256)[None, :] < _lenS[:, None]
        _validS2 = jnp.arange(64)[None, :] < _lenS2[:, None]
        _causal = jnp.tril(jnp.ones((256, 256), dtype=bool))
        mask_BxS2_bf1 = jnp.ones((8, 64), dtype=bool)
        return (x, ctx_1024, mask_BxS2_bf1)
    x, ctx_1024, mask_BxS2_bf1 = _rec_inputs()

    def _L0_attn_setup():
        import jax, jax.numpy as jnp
        import numpy as np
        EPS = 1e-06

        def rmsnorm(x, w):
            return x * jax.lax.rsqrt(jnp.mean(x * x, axis=-1, keepdims=True) + EPS) * w

        def rope(x, freqs):
            xr = x.reshape(x.shape[:-1] + (-1, 2))
            c, s = (jnp.cos(freqs), jnp.sin(freqs))
            x0, x1 = (xr[..., 0], xr[..., 1])
            return jnp.stack([x0 * c - x1 * s, x0 * s + x1 * c], axis=-1).reshape(x.shape)
        B_, L, D = (2, 256, 256)
        Din, H, P, N = (512, 64, 64, 128)
        key = jax.random.key(seed)
        ks = jax.random.split(key, 10)
        sd = lambda fan: 1.0 / np.sqrt(fan)
        f32 = jnp.float32
        return {'x': jax.random.normal(ks[0], (B_, L, D), f32), 'Wx': (jax.random.normal(ks[1], (Din, D)) * sd(D)).astype(f32), 'Wz': (jax.random.normal(ks[2], (Din, D)) * sd(D)).astype(f32), 'WB': (jax.random.normal(ks[3], (H * N, D)) * sd(D)).astype(f32), 'WC': (jax.random.normal(ks[4], (H * N, D)) * sd(D)).astype(f32), 'Wdt': jax.random.uniform(ks[5], (H, D), f32, -0.0001, 0.0001), 'Wlam': (jax.random.normal(ks[6], (H, D)) * sd(D)).astype(f32), 'Wth': (jax.random.normal(ks[7], (H * (N // 2), D)) * sd(D)).astype(f32), 'A_log': jnp.log(jnp.linspace(1.0, N, H)).astype(f32), 'Bn_w': jnp.ones((N,), f32), 'Cn_w': jnp.ones((N,), f32), 'B_bias': jnp.ones((H, N), f32), 'C_bias': jnp.ones((H, N), f32), 'Wout': (jax.random.normal(ks[8], (D, Din)) * sd(Din)).astype(f32)}
    _L0_attn_all = _L0_attn_setup()
    _L0_attn_in = {k: v for k, v in _L0_attn_all.items() if k in ('Wx', 'Wz', 'WB', 'WC', 'Wdt', 'Wlam', 'Wth', 'A_log', 'Bn_w', 'Cn_w', 'B_bias', 'C_bias', 'Wout')}
    del _L0_attn_all

    def _L0_xattn_setup():
        import jax, jax.numpy as jnp
        import numpy as np
        N_HEADS = 16
        N_KV_HEADS = 8
        HEAD_DIM = 128
        D_TEXT = 256
        D_VISION = 128
        GROUPS = N_HEADS // N_KV_HEADS
        key = jax.random.key(seed)
        ks = jax.random.split(key, 6)
        B, T_text, T_vis = (4, 256, 72)
        text_hidden = jax.random.normal(ks[0], (B, T_text, D_TEXT), dtype=jnp.float32)
        vision_tokens = jax.random.normal(ks[1], (B, T_vis, D_VISION), dtype=jnp.float32)
        vision_mask = jnp.ones((B, T_vis), dtype=bool)
        s = 0.02
        Wq = jax.random.normal(ks[2], (D_TEXT, N_HEADS * HEAD_DIM), dtype=jnp.float32) * s
        Wk = jax.random.normal(ks[3], (D_VISION, N_KV_HEADS * HEAD_DIM), dtype=jnp.float32) * s
        Wv = jax.random.normal(ks[4], (D_VISION, N_KV_HEADS * HEAD_DIM), dtype=jnp.float32) * s
        Wo = jax.random.normal(ks[5], (N_HEADS * HEAD_DIM, D_TEXT), dtype=jnp.float32) * s
        return {'text_hidden': text_hidden, 'vision_tokens': vision_tokens, 'vision_mask': vision_mask, 'Wq': Wq, 'Wk': Wk, 'Wv': Wv, 'Wo': Wo}
    _L0_xattn_all = _L0_xattn_setup()
    _L0_xattn_in = {k: v for k, v in _L0_xattn_all.items() if k in ('Wq', 'Wk', 'Wv', 'Wo')}
    del _L0_xattn_all

    def _L0_ffn_setup():
        import jax, jax.numpy as jnp
        import numpy as np
        HIDDEN = 256
        INTER = 1024
        SCALE = 64.0

        def fwht(x):
            orig_shape = x.shape
            n = orig_shape[-1]
            x = x.reshape(-1, n)
            h = 1
            while h < n:
                x = x.reshape(-1, n // (2 * h), 2, h)
                a, b = (x[:, :, 0, :], x[:, :, 1, :])
                x = jnp.stack([a + b, a - b], axis=2).reshape(-1, n)
                h *= 2
            return (x / jnp.sqrt(jnp.asarray(n, x.dtype))).reshape(orig_shape)
        key = jax.random.key(seed)
        ks = jax.random.split(key, 8)
        inp = jax.random.normal(ks[0], (4, 256, HIDDEN), dtype=jnp.float32)
        SU_ug = jnp.where(jax.random.bernoulli(ks[1], 0.5, (HIDDEN,)), 1.0, -1.0).astype(jnp.float32)
        SU_dp = jnp.where(jax.random.bernoulli(ks[2], 0.5, (INTER,)), 1.0, -1.0).astype(jnp.float32)
        Wscale_ug = jax.random.uniform(ks[3], (2 * INTER,), jnp.float32, 0.5, 1.5)
        Wscale_dp = jax.random.uniform(ks[4], (HIDDEN,), jnp.float32, 0.5, 1.5)
        W_up = jax.random.normal(ks[5], (INTER, HIDDEN), dtype=jnp.float32) * 0.02
        W_gate = jax.random.normal(ks[6], (INTER, HIDDEN), dtype=jnp.float32) * 0.02
        W_down = jax.random.normal(ks[7], (HIDDEN, INTER), dtype=jnp.float32) * 0.02
        return {'input': inp, 'SU_ug': SU_ug, 'SU_dp': SU_dp, 'Wscale_ug': Wscale_ug, 'Wscale_dp': Wscale_dp, 'W_up': W_up, 'W_gate': W_gate, 'W_down': W_down}
    _L0_ffn_all = _L0_ffn_setup()
    _L0_ffn_in = {k: v for k, v in _L0_ffn_all.items() if k in ('SU_ug', 'SU_dp', 'Wscale_ug', 'Wscale_dp', 'W_up', 'W_gate', 'W_down')}
    del _L0_ffn_all

    def _L1_attn_setup():
        import jax, jax.numpy as jnp
        import numpy as np
        from jax import lax
        B, T = (2, 256)
        HID = 256
        H, K, KC = (16, 128, 4)
        D = H * K
        EPS = 1e-05
        SCALE = K ** (-0.5)

        def causal_conv_silu(x, w, b):
            xp = jnp.pad(jnp.swapaxes(x, 1, 2), ((0, 0), (0, 0), (KC - 1, 0)))
            y = lax.conv_general_dilated(xp, w[:, None, :], (1,), 'VALID', feature_group_count=D)
            return jax.nn.silu(jnp.swapaxes(y, 1, 2) + b)

        def l2norm(x):
            return x * lax.rsqrt(jnp.sum(x * x, -1, keepdims=True) + 1e-06)

        def kda_scan(q, k, v, g, beta):
            qT, kT, vT, gT, bT = (jnp.moveaxis(a, 1, 0) for a in (q, k, v, g, beta))
            S0 = jnp.zeros((q.shape[0], H, K, K), q.dtype)

            def step(S, inp):
                qt, kt, vt, gt, bt = inp
                S = S * jnp.exp(gt)[..., None]
                vd = (vt - jnp.einsum('bhkv,bhk->bhv', S, kt)) * bt[..., None]
                S = S + kt[..., None] * vd[:, :, None, :]
                return (S, jnp.einsum('bhkv,bhk->bhv', S, qt))
            _, o = lax.scan(step, S0, (qT, kT, vT, gT, bT))
            return jnp.moveaxis(o, 0, 1)

        def _forward(x, Wq, Wk, Wv, conv_q_w, conv_q_b, conv_k_w, conv_k_b, conv_v_w, conv_v_b, Wfa, Wfb, A_log, dt_bias, Wb, Wga, Wgb, o_norm_w, Wo):
            b, t = x.shape[:2]
            q = causal_conv_silu(x @ Wq, conv_q_w, conv_q_b).reshape(b, t, H, K)
            k = causal_conv_silu(x @ Wk, conv_k_w, conv_k_b).reshape(b, t, H, K)
            v = causal_conv_silu(x @ Wv, conv_v_w, conv_v_b).reshape(b, t, H, K)
            g = jax.nn.softplus(x @ Wfa @ Wfb + dt_bias).reshape(b, t, H, K)
            g = -jnp.exp(A_log)[None, None, :, None] * g
            beta = jax.nn.sigmoid(x @ Wb)
            q = l2norm(q) * SCALE
            k = l2norm(k)
            o = kda_scan(q, k, v, g, beta)
            gate = (x @ Wga @ Wgb).reshape(b, t, H, K)
            var = jnp.mean(o * o, -1, keepdims=True)
            o = o * lax.rsqrt(var + EPS) * o_norm_w * jax.nn.sigmoid(gate)
            return o.reshape(b, t, D) @ Wo
        key = jax.random.key(seed)
        ks = jax.random.split(key, 16)
        s = 0.02
        f32 = jnp.float32
        return {'x': jax.random.normal(ks[0], (B, T, HID), f32), 'Wq': jax.random.normal(ks[1], (HID, D), f32) * s, 'Wk': jax.random.normal(ks[2], (HID, D), f32) * s, 'Wv': jax.random.normal(ks[3], (HID, D), f32) * s, 'conv_q_w': jax.random.normal(ks[4], (D, KC), f32) * 0.2, 'conv_q_b': jnp.zeros((D,), f32), 'conv_k_w': jax.random.normal(ks[5], (D, KC), f32) * 0.2, 'conv_k_b': jnp.zeros((D,), f32), 'conv_v_w': jax.random.normal(ks[6], (D, KC), f32) * 0.2, 'conv_v_b': jnp.zeros((D,), f32), 'Wfa': jax.random.normal(ks[7], (HID, K), f32) * s, 'Wfb': jax.random.normal(ks[8], (K, D), f32) * s, 'A_log': jnp.log(jax.random.uniform(ks[9], (H,), f32, 1.0, 16.0)), 'dt_bias': jnp.zeros((D,), f32), 'Wb': jax.random.normal(ks[10], (HID, H), f32) * s, 'Wga': jax.random.normal(ks[11], (HID, K), f32) * s, 'Wgb': jax.random.normal(ks[12], (K, D), f32) * s, 'o_norm_w': jnp.ones((K,), f32), 'Wo': jax.random.normal(ks[13], (D, HID), f32) * s}
    _L1_attn_all = _L1_attn_setup()
    _L1_attn_in = {k: v for k, v in _L1_attn_all.items() if k in ('Wq', 'Wk', 'Wv', 'conv_q_w', 'conv_q_b', 'conv_k_w', 'conv_k_b', 'conv_v_w', 'conv_v_b', 'Wfa', 'Wfb', 'A_log', 'dt_bias', 'Wb', 'Wga', 'Wgb', 'o_norm_w', 'Wo')}
    del _L1_attn_all

    def _L1_xattn_setup():
        import jax, jax.numpy as jnp
        import numpy as np
        EPS = 1e-05

        def rmsnorm(x, g, eps=EPS):
            var = jnp.mean(jnp.square(x), axis=-1, keepdims=True)
            return x * jax.lax.rsqrt(var + eps) * g
        key = jax.random.key(seed)
        ks = jax.random.split(key, 8)
        B, Sq, Skv = (2, 512, 64)
        dim, cdim, H, D = (256, 128, 16, 128)
        inner = H * D
        s = lambda f: 1.0 / np.sqrt(f)
        return {'hidden_states': jax.random.normal(ks[0], (B, Sq, dim), jnp.float32), 'encoder_hidden_states': jax.random.normal(ks[1], (B, Skv, cdim), jnp.float32), 'Wq': jax.random.normal(ks[2], (dim, inner), jnp.float32) * s(dim), 'Wk': jax.random.normal(ks[3], (cdim, inner), jnp.float32) * s(cdim), 'Wv': jax.random.normal(ks[4], (cdim, inner), jnp.float32) * s(cdim), 'Wo': jax.random.normal(ks[5], (inner, dim), jnp.float32) * s(inner), 'gq': jnp.ones((D,), jnp.float32), 'gk': jnp.ones((D,), jnp.float32)}
    _L1_xattn_all = _L1_xattn_setup()
    _L1_xattn_in = {k: v for k, v in _L1_xattn_all.items() if k in ('Wq', 'Wk', 'Wv', 'Wo', 'gq', 'gk')}
    del _L1_xattn_all

    def _L1_ffn_setup():
        import jax, jax.numpy as jnp
        import numpy as np
        DIM = 256
        HID = 704
        ZERO_POINT = 128.0

        def _qlinear(x, wq, scale):
            W = (wq.astype(jnp.float32) - ZERO_POINT) * scale[:, None]
            return jnp.einsum('bsd,hd->bsh', x, W)
        key = jax.random.key(seed)
        ks = jax.random.split(key, 7)
        B, S = (4, 256)
        sg = jax.random.uniform(ks[1], (HID,)) * (0.02 / np.sqrt(DIM)) + 0.0001
        su = jax.random.uniform(ks[3], (HID,)) * (0.02 / np.sqrt(DIM)) + 0.0001
        sd = jax.random.uniform(ks[5], (DIM,)) * (0.02 / np.sqrt(HID)) + 0.0001
        return {'x': jax.random.normal(ks[0], (B, S, DIM), dtype=jnp.float32), 'wq_gate': jax.random.randint(ks[2], (HID, DIM), 0, 32, dtype=jnp.int32), 's_gate': sg, 'wq_up': jax.random.randint(ks[4], (HID, DIM), 0, 32, dtype=jnp.int32), 's_up': su, 'wq_down': jax.random.randint(ks[6], (DIM, HID), 0, 32, dtype=jnp.int32), 's_down': sd}
    _L1_ffn_all = _L1_ffn_setup()
    _L1_ffn_in = {k: v for k, v in _L1_ffn_all.items() if k in ('wq_gate', 's_gate', 'wq_up', 's_up', 'wq_down', 's_down')}
    del _L1_ffn_all
    return {'x': x, 'ctx_1024': ctx_1024, 'mask_BxS2_bf1': mask_BxS2_bf1, 'L0_attn_Wx': _L0_attn_in['Wx'], 'L0_attn_Wz': _L0_attn_in['Wz'], 'L0_attn_WB': _L0_attn_in['WB'], 'L0_attn_WC': _L0_attn_in['WC'], 'L0_attn_Wdt': _L0_attn_in['Wdt'], 'L0_attn_Wlam': _L0_attn_in['Wlam'], 'L0_attn_Wth': _L0_attn_in['Wth'], 'L0_attn_A_log': _L0_attn_in['A_log'], 'L0_attn_Bn_w': _L0_attn_in['Bn_w'], 'L0_attn_Cn_w': _L0_attn_in['Cn_w'], 'L0_attn_B_bias': _L0_attn_in['B_bias'], 'L0_attn_C_bias': _L0_attn_in['C_bias'], 'L0_attn_Wout': _L0_attn_in['Wout'], 'L0_xattn_Wq': _L0_xattn_in['Wq'], 'L0_xattn_Wk': _L0_xattn_in['Wk'], 'L0_xattn_Wv': _L0_xattn_in['Wv'], 'L0_xattn_Wo': _L0_xattn_in['Wo'], 'L0_ffn_SU_ug': _L0_ffn_in['SU_ug'], 'L0_ffn_SU_dp': _L0_ffn_in['SU_dp'], 'L0_ffn_Wscale_ug': _L0_ffn_in['Wscale_ug'], 'L0_ffn_Wscale_dp': _L0_ffn_in['Wscale_dp'], 'L0_ffn_W_up': _L0_ffn_in['W_up'], 'L0_ffn_W_gate': _L0_ffn_in['W_gate'], 'L0_ffn_W_down': _L0_ffn_in['W_down'], 'L1_attn_Wq': _L1_attn_in['Wq'], 'L1_attn_Wk': _L1_attn_in['Wk'], 'L1_attn_Wv': _L1_attn_in['Wv'], 'L1_attn_conv_q_w': _L1_attn_in['conv_q_w'], 'L1_attn_conv_q_b': _L1_attn_in['conv_q_b'], 'L1_attn_conv_k_w': _L1_attn_in['conv_k_w'], 'L1_attn_conv_k_b': _L1_attn_in['conv_k_b'], 'L1_attn_conv_v_w': _L1_attn_in['conv_v_w'], 'L1_attn_conv_v_b': _L1_attn_in['conv_v_b'], 'L1_attn_Wfa': _L1_attn_in['Wfa'], 'L1_attn_Wfb': _L1_attn_in['Wfb'], 'L1_attn_A_log': _L1_attn_in['A_log'], 'L1_attn_dt_bias': _L1_attn_in['dt_bias'], 'L1_attn_Wb': _L1_attn_in['Wb'], 'L1_attn_Wga': _L1_attn_in['Wga'], 'L1_attn_Wgb': _L1_attn_in['Wgb'], 'L1_attn_o_norm_w': _L1_attn_in['o_norm_w'], 'L1_attn_Wo': _L1_attn_in['Wo'], 'L1_xattn_Wq': _L1_xattn_in['Wq'], 'L1_xattn_Wk': _L1_xattn_in['Wk'], 'L1_xattn_Wv': _L1_xattn_in['Wv'], 'L1_xattn_Wo': _L1_xattn_in['Wo'], 'L1_xattn_gq': _L1_xattn_in['gq'], 'L1_xattn_gk': _L1_xattn_in['gk'], 'L1_ffn_wq_gate': _L1_ffn_in['wq_gate'], 'L1_ffn_s_gate': _L1_ffn_in['s_gate'], 'L1_ffn_wq_up': _L1_ffn_in['wq_up'], 'L1_ffn_s_up': _L1_ffn_in['s_up'], 'L1_ffn_wq_down': _L1_ffn_in['wq_down'], 'L1_ffn_s_down': _L1_ffn_in['s_down']}

def reference(x, ctx_1024, mask_BxS2_bf1, L0_attn_Wx, L0_attn_Wz, L0_attn_WB, L0_attn_WC, L0_attn_Wdt, L0_attn_Wlam, L0_attn_Wth, L0_attn_A_log, L0_attn_Bn_w, L0_attn_Cn_w, L0_attn_B_bias, L0_attn_C_bias, L0_attn_Wout, L0_xattn_Wq, L0_xattn_Wk, L0_xattn_Wv, L0_xattn_Wo, L0_ffn_SU_ug, L0_ffn_SU_dp, L0_ffn_Wscale_ug, L0_ffn_Wscale_dp, L0_ffn_W_up, L0_ffn_W_gate, L0_ffn_W_down, L1_attn_Wq, L1_attn_Wk, L1_attn_Wv, L1_attn_conv_q_w, L1_attn_conv_q_b, L1_attn_conv_k_w, L1_attn_conv_k_b, L1_attn_conv_v_w, L1_attn_conv_v_b, L1_attn_Wfa, L1_attn_Wfb, L1_attn_A_log, L1_attn_dt_bias, L1_attn_Wb, L1_attn_Wga, L1_attn_Wgb, L1_attn_o_norm_w, L1_attn_Wo, L1_xattn_Wq, L1_xattn_Wk, L1_xattn_Wv, L1_xattn_Wo, L1_xattn_gq, L1_xattn_gk, L1_ffn_wq_gate, L1_ffn_s_gate, L1_ffn_wq_up, L1_ffn_s_up, L1_ffn_wq_down, L1_ffn_s_down):
    import jax
    import jax.numpy as jnp

    def _L0_attn_ref(x, Wx, Wz, WB, WC, Wdt, Wlam, Wth, A_log, Bn_w, Cn_w, B_bias, C_bias, Wout):
        import jax, jax.numpy as jnp
        import numpy as np
        EPS = 1e-06

        def rmsnorm(x, w):
            return x * jax.lax.rsqrt(jnp.mean(x * x, axis=-1, keepdims=True) + EPS) * w

        def rope(x, freqs):
            xr = x.reshape(x.shape[:-1] + (-1, 2))
            c, s = (jnp.cos(freqs), jnp.sin(freqs))
            x0, x1 = (xr[..., 0], xr[..., 1])
            return jnp.stack([x0 * c - x1 * s, x0 * s + x1 * c], axis=-1).reshape(x.shape)
        B_, L, D = x.shape
        H = A_log.shape[0]
        N = B_bias.shape[1]
        Din = Wx.shape[0]
        P = Din // H
        xp = x @ Wx.T
        z = x @ Wz.T
        Bm = (x @ WB.T).reshape(B_, L, H, N)
        Cm = (x @ WC.T).reshape(B_, L, H, N)
        Bm = rmsnorm(Bm, Bn_w) + B_bias
        Cm = rmsnorm(Cm, Cn_w) + C_bias
        dt = jax.nn.softplus(x @ Wdt.T)
        lam = jax.nn.sigmoid(x @ Wlam.T)
        theta = (x @ Wth.T).reshape(B_, L, H, N // 2)
        theta_cumsum = jnp.cumsum(theta * dt[..., None], axis=1)
        Bm = rope(Bm, theta_cumsum)
        Cm = rope(Cm, theta_cumsum)
        xh = xp.reshape(B_, L, H, P)
        A = -jnp.exp(A_log)
        alpha = jnp.exp(dt * A)
        beta = (1.0 - lam) * dt * alpha
        gamma = lam * dt

        def step(carry, inputs):
            h, B_prev, x_prev = carry
            Bt, Ct, xt, at, bt, gt = inputs
            h = at[..., None, None] * h + jnp.einsum('bh,bhn,bhp->bhnp', bt, B_prev, x_prev) + jnp.einsum('bh,bhn,bhp->bhnp', gt, Bt, xt)
            yt = jnp.einsum('bhn,bhnp->bhp', Ct, h)
            return ((h, Bt, xt), yt)
        h0 = jnp.zeros((B_, H, N, P), x.dtype)
        carry0 = (h0, jnp.zeros((B_, H, N), x.dtype), jnp.zeros((B_, H, P), x.dtype))
        seq = (Bm.transpose(1, 0, 2, 3), Cm.transpose(1, 0, 2, 3), xh.transpose(1, 0, 2, 3), alpha.transpose(1, 0, 2), beta.transpose(1, 0, 2), gamma.transpose(1, 0, 2))
        _, ys = jax.lax.scan(step, carry0, seq)
        y = ys.transpose(1, 0, 2, 3).reshape(B_, L, H * P)
        y = y * jax.nn.silu(z)
        return y @ Wout.T

    def _L0_xattn_ref(text_hidden, vision_tokens, vision_mask, Wq, Wk, Wv, Wo):
        import jax, jax.numpy as jnp
        import numpy as np
        N_HEADS = 16
        N_KV_HEADS = 8
        HEAD_DIM = 128
        D_TEXT = 256
        D_VISION = 128
        GROUPS = N_HEADS // N_KV_HEADS
        B, T_text, _ = text_hidden.shape
        T_vis = vision_tokens.shape[1]
        scale = jnp.float32(np.sqrt(HEAD_DIM))
        q = (text_hidden @ Wq).reshape(B, T_text, N_HEADS, HEAD_DIM).transpose(0, 2, 1, 3)
        k = (vision_tokens @ Wk).reshape(B, T_vis, N_KV_HEADS, HEAD_DIM).transpose(0, 2, 1, 3)
        v = (vision_tokens @ Wv).reshape(B, T_vis, N_KV_HEADS, HEAD_DIM).transpose(0, 2, 1, 3)
        k = jnp.repeat(k, GROUPS, axis=1)
        v = jnp.repeat(v, GROUPS, axis=1)
        scores = jnp.einsum('bhtd,bhsd->bhts', q, k) / scale
        mask = vision_mask[:, None, None, :]
        scores = jnp.where(mask, scores, -jnp.inf)
        attn = jax.nn.softmax(scores, axis=-1)
        attn = jnp.nan_to_num(attn, nan=0.0)
        out = jnp.einsum('bhts,bhsd->bhtd', attn, v)
        out = out.transpose(0, 2, 1, 3).reshape(B, T_text, N_HEADS * HEAD_DIM)
        return out @ Wo

    def _L0_ffn_ref(input, SU_ug, SU_dp, Wscale_ug, Wscale_dp, W_up, W_gate, W_down):
        import jax, jax.numpy as jnp
        import numpy as np
        HIDDEN = 256
        INTER = 1024
        SCALE = 64.0

        def fwht(x):
            orig_shape = x.shape
            n = orig_shape[-1]
            x = x.reshape(-1, n)
            h = 1
            while h < n:
                x = x.reshape(-1, n // (2 * h), 2, h)
                a, b = (x[:, :, 0, :], x[:, :, 1, :])
                x = jnp.stack([a + b, a - b], axis=2).reshape(-1, n)
                h *= 2
            return (x / jnp.sqrt(jnp.asarray(n, x.dtype))).reshape(orig_shape)
        n = SU_ug.shape[0]
        x = input.reshape(-1, n)
        x = fwht(x * SU_ug) / SCALE
        x_up = x @ W_up.T * (Wscale_ug[:INTER] * SCALE)
        x_gate = x @ W_gate.T * (Wscale_ug[INTER:] * SCALE)
        x = jax.nn.silu(x_gate) * x_up
        x = fwht(x * SU_dp) / SCALE
        x = x @ W_down.T * (Wscale_dp * SCALE)
        return x.reshape(input.shape)

    def _L1_attn_ref(x, Wq, Wk, Wv, conv_q_w, conv_q_b, conv_k_w, conv_k_b, conv_v_w, conv_v_b, Wfa, Wfb, A_log, dt_bias, Wb, Wga, Wgb, o_norm_w, Wo):
        import jax, jax.numpy as jnp
        import numpy as np
        from jax import lax
        B, T = (2, 256)
        HID = 256
        H, K, KC = (16, 128, 4)
        D = H * K
        EPS = 1e-05
        SCALE = K ** (-0.5)

        def causal_conv_silu(x, w, b):
            xp = jnp.pad(jnp.swapaxes(x, 1, 2), ((0, 0), (0, 0), (KC - 1, 0)))
            y = lax.conv_general_dilated(xp, w[:, None, :], (1,), 'VALID', feature_group_count=D)
            return jax.nn.silu(jnp.swapaxes(y, 1, 2) + b)

        def l2norm(x):
            return x * lax.rsqrt(jnp.sum(x * x, -1, keepdims=True) + 1e-06)

        def kda_scan(q, k, v, g, beta):
            qT, kT, vT, gT, bT = (jnp.moveaxis(a, 1, 0) for a in (q, k, v, g, beta))
            S0 = jnp.zeros((q.shape[0], H, K, K), q.dtype)

            def step(S, inp):
                qt, kt, vt, gt, bt = inp
                S = S * jnp.exp(gt)[..., None]
                vd = (vt - jnp.einsum('bhkv,bhk->bhv', S, kt)) * bt[..., None]
                S = S + kt[..., None] * vd[:, :, None, :]
                return (S, jnp.einsum('bhkv,bhk->bhv', S, qt))
            _, o = lax.scan(step, S0, (qT, kT, vT, gT, bT))
            return jnp.moveaxis(o, 0, 1)

        def _forward(x, Wq, Wk, Wv, conv_q_w, conv_q_b, conv_k_w, conv_k_b, conv_v_w, conv_v_b, Wfa, Wfb, A_log, dt_bias, Wb, Wga, Wgb, o_norm_w, Wo):
            b, t = x.shape[:2]
            q = causal_conv_silu(x @ Wq, conv_q_w, conv_q_b).reshape(b, t, H, K)
            k = causal_conv_silu(x @ Wk, conv_k_w, conv_k_b).reshape(b, t, H, K)
            v = causal_conv_silu(x @ Wv, conv_v_w, conv_v_b).reshape(b, t, H, K)
            g = jax.nn.softplus(x @ Wfa @ Wfb + dt_bias).reshape(b, t, H, K)
            g = -jnp.exp(A_log)[None, None, :, None] * g
            beta = jax.nn.sigmoid(x @ Wb)
            q = l2norm(q) * SCALE
            k = l2norm(k)
            o = kda_scan(q, k, v, g, beta)
            gate = (x @ Wga @ Wgb).reshape(b, t, H, K)
            var = jnp.mean(o * o, -1, keepdims=True)
            o = o * lax.rsqrt(var + EPS) * o_norm_w * jax.nn.sigmoid(gate)
            return o.reshape(b, t, D) @ Wo
        return _forward(x, Wq, Wk, Wv, conv_q_w, conv_q_b, conv_k_w, conv_k_b, conv_v_w, conv_v_b, Wfa, Wfb, A_log, dt_bias, Wb, Wga, Wgb, o_norm_w, Wo)

    def _L1_xattn_ref(hidden_states, encoder_hidden_states, Wq, Wk, Wv, Wo, gq, gk):
        import jax, jax.numpy as jnp
        import numpy as np
        EPS = 1e-05

        def rmsnorm(x, g, eps=EPS):
            var = jnp.mean(jnp.square(x), axis=-1, keepdims=True)
            return x * jax.lax.rsqrt(var + eps) * g
        B, Sq, _ = hidden_states.shape
        Skv = encoder_hidden_states.shape[1]
        D = gq.shape[0]
        H = Wq.shape[1] // D
        scale = 1.0 / np.sqrt(D)
        q = (hidden_states @ Wq).reshape(B, Sq, H, D)
        k = (encoder_hidden_states @ Wk).reshape(B, Skv, H, D)
        v = (encoder_hidden_states @ Wv).reshape(B, Skv, H, D)
        q = rmsnorm(q, gq)
        k = rmsnorm(k, gk)
        scores = jnp.einsum('bqhd,bkhd->bhqk', q, k) * scale
        attn = jax.nn.softmax(scores, axis=-1)
        out = jnp.einsum('bhqk,bkhd->bqhd', attn, v)
        out = out.reshape(B, Sq, H * D)
        return out @ Wo

    def _L1_ffn_ref(x, wq_gate, s_gate, wq_up, s_up, wq_down, s_down):
        import jax, jax.numpy as jnp
        import numpy as np
        DIM = 256
        HID = 704
        ZERO_POINT = 128.0

        def _qlinear(x, wq, scale):
            W = (wq.astype(jnp.float32) - ZERO_POINT) * scale[:, None]
            return jnp.einsum('bsd,hd->bsh', x, W)
        gate = _qlinear(x, wq_gate, s_gate)
        gate = jax.nn.silu(gate)
        up = _qlinear(x, wq_up, s_up)
        return _qlinear(gate * up, wq_down, s_down)
    x = _layernorm(x + _L0_attn_ref(x, L0_attn_Wx, L0_attn_Wz, L0_attn_WB, L0_attn_WC, L0_attn_Wdt, L0_attn_Wlam, L0_attn_Wth, L0_attn_A_log, L0_attn_Bn_w, L0_attn_Cn_w, L0_attn_B_bias, L0_attn_C_bias, L0_attn_Wout), axis=-1)
    x = _layernorm(x + _L0_xattn_ref(x, ctx_1024, mask_BxS2_bf1, L0_xattn_Wq, L0_xattn_Wk, L0_xattn_Wv, L0_xattn_Wo), axis=-1)
    x = _layernorm(x + _L0_ffn_ref(x, L0_ffn_SU_ug, L0_ffn_SU_dp, L0_ffn_Wscale_ug, L0_ffn_Wscale_dp, L0_ffn_W_up, L0_ffn_W_gate, L0_ffn_W_down), axis=-1)
    x = _layernorm(x + _L1_attn_ref(x, L1_attn_Wq, L1_attn_Wk, L1_attn_Wv, L1_attn_conv_q_w, L1_attn_conv_q_b, L1_attn_conv_k_w, L1_attn_conv_k_b, L1_attn_conv_v_w, L1_attn_conv_v_b, L1_attn_Wfa, L1_attn_Wfb, L1_attn_A_log, L1_attn_dt_bias, L1_attn_Wb, L1_attn_Wga, L1_attn_Wgb, L1_attn_o_norm_w, L1_attn_Wo), axis=-1)
    x = _layernorm(x + _L1_xattn_ref(x, ctx_1024, L1_xattn_Wq, L1_xattn_Wk, L1_xattn_Wv, L1_xattn_Wo, L1_xattn_gq, L1_xattn_gk), axis=-1)
    x = _layernorm(x + _L1_ffn_ref(x, L1_ffn_wq_gate, L1_ffn_s_gate, L1_ffn_wq_up, L1_ffn_s_up, L1_ffn_wq_down, L1_ffn_s_down), axis=-1)
    return x

_drawn_inputs = setup_inputs


def setup_inputs(seed=0):
    import zlib

    import numpy as np

    out = dict(_drawn_inputs(seed))
    spreads = {'L0_attn_Bn_w': (1.0, 0.6),
     'L0_attn_Cn_w': (1.0, 0.6),
     'L0_attn_B_bias': (1.0, 0.6),
     'L0_attn_C_bias': (1.0, 0.6),
     'L1_attn_conv_q_b': (0.0, 0.1),
     'L1_attn_conv_k_b': (0.0, 0.1),
     'L1_attn_conv_v_b': (0.0, 0.277),
     'L1_attn_dt_bias': (0.0, 2.0),
     'L1_attn_o_norm_w': (1.0, 0.6),
     'L1_xattn_gq': (1.0, 0.2),
     'L1_xattn_gk': (1.0, 0.2)}
    factors = {'L0_attn_Wdt': 35.441,
     'L0_attn_Wth': 3.777,
     'L0_xattn_Wq': 8.0,
     'L0_xattn_Wk': 8.0,
     'L0_ffn_Wscale_ug': 4.436,
     'L0_ffn_Wscale_dp': 6.134,
     'L1_attn_Wfa': 8.0,
     'L1_attn_Wfb': 8.0,
     'L1_attn_A_log': 8.0,
     'L1_attn_Wb': 8.0,
     'L1_attn_Wga': 8.0,
     'L1_attn_Wgb': 8.0,
     'L1_ffn_s_gate': 8.0,
     'L1_ffn_s_up': 8.0,
     'L1_ffn_s_down': 8.0}
    for name, (base, spread) in spreads.items():
        noise = np.random.default_rng([zlib.crc32(name.encode()), seed]).standard_normal(out[name].shape)
        drawn = base * np.exp(spread * noise) if base else spread * noise
        out[name] = jnp.asarray(drawn.astype(out[name].dtype))
    for name, factor in factors.items():
        out[name] = (out[name] * factor).astype(out[name].dtype)
    return out
```

```python
from contextlib import ExitStack

import numpy as np

import concourse.bass as bass
from concourse import mybir

F32 = mybir.dt.float32
I32 = mybir.dt.int32
U8 = mybir.dt.uint8
ALU = mybir.AluOpType
ACT = mybir.ActivationFunctionType
AX = mybir.AxisListType

P = 128
B, T, D = 8, 256, 256
TOK = B * T
NT = TOK // P
KD = D // P
SEG = 512
NSEG = TOK // SEG
S2, DC = 64, 128
PI = 3.1415925
HALF_PI = 1.5707963267948966


class Core:

    def __init__(self, nc, ctx):
        self.nc, self.ctx = nc, ctx
        self.held, self.sems = [], ExitStack()
        self.x_tok = self.sbuf("x_tok", [P, NT, D])
        self.x_t = self.sbuf("x_t", [P, KD, TOK])
        self.ident = self.sbuf("ident", [P, P])
        self.ones = self.sbuf("ones", [P, P])
        self.bank = ctx.enter_context(nc.psum_tensor("bank", [P, 8, 512], F32))

    def sbuf(self, name, shape, dt=F32, ctx=None):
        return (ctx or self.ctx).enter_context(self.nc.sbuf_tensor(name, shape, dt))

    def sem(self, name):
        self.held.append(self.sems.enter_context(self.nc.semaphore(name)))
        return self.held[-1]

    def release_sems(self):
        with self.nc.Block() as block:

            @block.sync
            def _(sp):
                for held in self.held:
                    sp.sem_clear(held)

        self.sems.close()
        self.held, self.sems = [], ExitStack()


def load_start(c, x_tok_d, x_t_d, ident_d):
    nc = c.nc
    loaded = c.sem("start_loaded")
    with nc.Block() as block:

        @block.sync
        def _(sp):
            sp.dma_start(c.x_tok[:], x_tok_d).then_inc(loaded, 16)
            sp.dma_start(c.x_t[:], x_t_d).then_inc(loaded, 16)
            sp.dma_start(c.ident[:], ident_d).then_inc(loaded, 16)
            sp.wait_ge(loaded, 48)

        @block.vector
        def _(dve):
            nc.vector.memset(c.ones[:], 1.0)


def layer_norm(c, tag, out_d=None):
    nc = c.nc
    own = ExitStack()
    stats = c.sbuf(tag + "_stats", [P, NT, 6], ctx=own)
    mean_var = c.sbuf(tag + "_mean_var", [P, NT, 2], ctx=own)
    std = c.sbuf(tag + "_std", [P, NT], ctx=own)
    rstd = c.sbuf(tag + "_rstd", [P, NT], ctx=own)
    eps = c.sbuf(tag + "_eps", [P, 1], ctx=own)
    measured, rooted, scaled, turned, copied, stored = (
        c.sem(f"{tag}_{n}") for n in ("measured", "rooted", "scaled", "turned", "copied", "stored"))
    groups = NT // 4 * KD
    with own, nc.Block() as block:

        @block.vector
        def _(dve):
            nc.vector.memset(eps[:], 1e-5).then_inc(measured, 1)
            for t in range(NT):
                nc.vector.bn_stats(stats[:, t, :], c.x_tok[:, t, :]).then_inc(measured, 1)
            for t in range(NT):
                dve.wait_ge(measured, 2 + t)
                nc.vector.bn_aggr(mean_var[:, t, :], stats[:, t, :]).then_inc(measured, 1)
            dve.wait_ge(rooted, 1)
            nc.vector.reciprocal(rstd[:], std[:]).then_inc(rooted, 1)
            dve.wait_ge(rooted, 2)
            for t in range(NT):
                nc.vector.tensor_scalar(c.x_tok[:, t, :], c.x_tok[:, t, :], mean_var[:, t, 0:1],
                                        rstd[:, t:t + 1], ALU.subtract, ALU.mult).then_inc(scaled, 1)

        @block.scalar
        def _(act):
            act.wait_ge(measured, 1 + 2 * NT)
            nc.scalar.activation(std[:], mean_var[:, :, 1], ACT.Sqrt, bias=eps[:, 0:1]).then_inc(rooted, 1)
            if out_d is None:
                for g in range(groups):
                    q, k = divmod(g, KD)
                    act.wait_ge(turned, g + 1)
                    nc.scalar.activation(c.x_t[:, k, SEG * q:SEG * (q + 1)], c.bank[:, g % 4, :],
                                         ACT.Copy).then_inc(copied, 1)

        if out_d is None:

            @block.tensor
            def _(pe):
                for g in range(groups):
                    q, k = divmod(g, KD)
                    pe.wait_ge(scaled, 4 * (q + 1))
                    if g >= 4:
                        pe.wait_ge(copied, g - 3)
                    for j in range(4):
                        last = nc.tensor.transpose(c.bank[:, g % 4, P * j:P * (j + 1)],
                                                   c.x_tok[:, 4 * q + j, P * k:P * (k + 1)], c.ident[:])
                    last.then_inc(turned, 1)
        else:

            @block.sync
            def _(sp):
                for q in range(4):
                    sp.wait_ge(scaled, 4 * (q + 1))
                    sp.dma_start(out_d[:, 4 * q:4 * q + 4, :], c.x_tok[:, 4 * q:4 * q + 4, :]).then_inc(stored, 16)
                sp.wait_ge(stored, 64)



SH, SN, SP_ = 64, 128, 8
DIN = SH * SP_
PAIRS = SH // 2
INV_2PI = 0.15915494309189535
ROUND = 12582912.0
MIX0 = 5
TWO_PI_HI, TWO_PI_LO = 6.28125, 0.0019353071795864769


def ssm(c, w):
    nc = c.nc
    own = ExitStack()
    xh = c.sbuf("xh", [P, NT, DIN], ctx=own)
    y_tok = c.sbuf("y_tok", [P, NT, DIN], ctx=own)
    with own:
        tables = ExitStack()
        dt_t = c.sbuf("dt_t", [SH, TOK], ctx=tables)
        alpha_t = c.sbuf("alpha_t", [SH, TOK], ctx=tables)
        beta_tok = c.sbuf("beta_tok", [P, NT, SH], ctx=tables)
        gamma_tok = c.sbuf("gamma_tok", [P, NT, SH], ctx=tables)
        with tables:
            ssm_gates(c, w, xh, dt_t, alpha_t, beta_tok, gamma_tok)
            ssm_heads(c, w, xh, y_tok, dt_t, alpha_t, beta_tok, gamma_tok)
        ssm_output(c, w, y_tok)


def ssm_gates(c, w, xh, dt_t, alpha_t, beta_tok, gamma_tok):
    nc = c.nc
    own = ExitStack()
    wx = c.sbuf("wx", [P, KD, DIN], ctx=own)
    wdl = c.sbuf("wdl", [P, KD, 2, SH], ctx=own)
    a_log = c.sbuf("a_log", [SH, 1], ctx=own)
    neg_a = c.sbuf("neg_a", [SH, 1], ctx=own)
    tail = c.sbuf("softplus_tail", [SH, SEG], ctx=own)
    low = c.sbuf("softplus_low", [SH, SEG], ctx=own)
    lam = c.sbuf("lam", [SH, SEG], ctx=own)
    rest = c.sbuf("rest", [SH, SEG], ctx=own)
    gamma_t = c.sbuf("gamma_t", [SH, TOK], ctx=own)
    beta_t = c.sbuf("beta_t", [SH, TOK], ctx=own)
    loaded, x_done, x_kept, dl_done, soft, low_done, dt_done, lam_done, gk_done, turned, kept = (
        c.sem("gates_" + n) for n in ("loaded", "x_done", "x_kept", "dl_done", "soft", "low_done", "dt_done", "lam_done",
                                      "gk_done", "turned", "kept"))
    with own, nc.Block() as block:

        @block.sync
        def _(sp):
            sp.dma_start(wdl[:], w["dt_lam"]).then_inc(loaded, 16)
            sp.dma_start(a_log[:], w["A_log"]).then_inc(loaded, 16)
            sp.dma_start(wx[:], w["x"]).then_inc(loaded, 16)

        @block.tensor
        def _(pe):
            pe.wait_ge(loaded, 48)
            for q in range(NSEG):
                if q:
                    pe.wait_ge(lam_done, 2 * q)
                    pe.wait_ge(dt_done, 2 * q)
                for g in range(2):
                    for k in range(KD):
                        last = nc.tensor.matmul(c.bank[0:SH, 4 + g, :], wdl[:, k, g, :],
                                                c.x_t[:, k, SEG * q:SEG * (q + 1)],
                                                start=k == 0, stop=k == KD - 1)
                last.then_inc(dl_done, 1)
            for t in range(NT):
                if t >= 4:
                    pe.wait_ge(x_kept, t - 3)
                for k in range(KD):
                    last = nc.tensor.matmul(c.bank[:, t % 4, :], c.x_t[:, k, P * t:P * (t + 1)], wx[:, k, :],
                                            start=k == 0, stop=k == KD - 1)
                last.then_inc(x_done, 1)
            for g, source in enumerate((beta_t, gamma_t)):
                for half in range(2):
                    pe.wait_ge(gk_done, 4 * NSEG + 1)
                    for t in range(8 * half, 8 * half + 8):
                        last = nc.tensor.transpose(c.bank[:, 4 + 2 * g + half, SH * (t % 8):SH * (t % 8 + 1)],
                                                   source[:, P * t:P * (t + 1)], c.ident[0:SH, 0:SH])
                    last.then_inc(turned, 1)

        @block.scalar
        def _(act):
            act.wait_ge(loaded, 48)
            nc.scalar.activation(neg_a[:], a_log[:], ACT.Exp).then_inc(soft, 1)
            for q in range(NSEG):
                cols = slice(SEG * q, SEG * (q + 1))
                act.wait_ge(dl_done, q + 1)
                if q:
                    act.wait_ge(gk_done, 4 * q + 1)
                nc.scalar.activation(tail[:], c.bank[0:SH, 4, :], ACT.Abs).then_inc(soft, 1)
                act.wait_ge(soft, 4 * q + 2)
                nc.scalar.activation(tail[:], tail[:], ACT.Exp, scale=-1.0).then_inc(soft, 1)
                act.wait_ge(low_done, 2 * q + 2)
                nc.scalar.activation(low[:], low[:], ACT.Ln, bias=1.0).then_inc(soft, 1)
                nc.scalar.activation(lam[:], c.bank[0:SH, 5, :], ACT.Sigmoid).then_inc(lam_done, 1)
                nc.scalar.activation(rest[:], c.bank[0:SH, 5, :], ACT.Sigmoid, scale=-1.0).then_inc(lam_done, 1)
                act.wait_ge(dt_done, 2 * q + 2)
                act.wait_ge(gk_done, 1)
                nc.scalar.activation(alpha_t[:, cols], dt_t[:, cols], ACT.Exp, scale=neg_a[:, 0:1]).then_inc(soft, 1)
            for t in range(NT):
                act.wait_ge(x_done, t + 1)
                nc.scalar.activation(xh[:, t, :], c.bank[:, t % 4, :], ACT.Copy).then_inc(x_kept, 1)
            for j in range(4):
                act.wait_ge(turned, j + 1)
                target = (beta_tok, gamma_tok)[j // 2]
                nc.scalar.activation(target[:, 8 * (j % 2):8 * (j % 2) + 8, :],
                                     c.bank[:, 4 + j, :].rearrange("p (t h) -> p t h", h=SH),
                                     ACT.Copy).then_inc(kept, 1)

        @block.vector
        def _(dve):
            for q in range(NSEG):
                cols = slice(SEG * q, SEG * (q + 1))
                dve.wait_ge(soft, 4 * q + 3)
                nc.vector.tensor_scalar(low[:], tail[:], 1.0, 1.0, ALU.add, ALU.subtract).then_inc(low_done, 1)
                dve.wait_ge(low_done, 2 * q + 1)
                nc.vector.tensor_tensor(tail[:], tail[:], low[:], ALU.subtract).then_inc(low_done, 1)
                dve.wait_ge(low_done, 2 * q + 2)
                dve.wait_ge(soft, 4 * q + 4)
                nc.vector.scalar_tensor_tensor(dt_t[:, cols], c.bank[0:SH, 4, :], 0.0, low[:], ALU.max,
                                               ALU.add).then_inc(dt_done, 1)
                dve.wait_ge(dt_done, 2 * q + 1)
                nc.vector.tensor_tensor(dt_t[:, cols], dt_t[:, cols], tail[:], ALU.add).then_inc(dt_done, 1)
                if q == 0:
                    nc.vector.tensor_scalar(neg_a[:], neg_a[:], -1.0, None, ALU.mult).then_inc(gk_done, 1)
                dve.wait_ge(dt_done, 2 * q + 2)
                dve.wait_ge(lam_done, 2 * q + 2)
                nc.vector.tensor_tensor(gamma_t[:, cols], lam[:], dt_t[:, cols], ALU.mult).then_inc(gk_done, 1)
                nc.vector.tensor_tensor(rest[:], rest[:], dt_t[:, cols], ALU.mult).then_inc(gk_done, 1)
                dve.wait_ge(gk_done, 4 * q + 3)
                dve.wait_ge(soft, 4 * q + 5)
                nc.vector.tensor_tensor(rest[:], rest[:], alpha_t[:, cols], ALU.mult).then_inc(gk_done, 1)
                dve.wait_ge(gk_done, 4 * q + 4)
                b3, r3 = (v.rearrange("h (b t) -> h b t", t=T) for v in (beta_t[:, cols], rest[:, :]))
                nc.vector.memset(b3[:, :, T - 1:T], 0.0)
                nc.vector.tensor_copy(b3[:, :, 0:T - 1], r3[:, :, 1:T]).then_inc(gk_done, 1)


def ssm_heads(c, w, xh, y_tok, dt_t, alpha_t, beta_tok, gamma_tok):
    nc = c.nc
    own = ExitStack()

    def sb(name, shape, dt=F32):
        return c.sbuf(name, shape, dt, ctx=own)

    wp = sb("w_pair", [P, KD, 5, P])
    sel = sb("selectors", [SH, 3, P])
    bias = sb("bc_bias", [P, 4])
    norm_w = sb("bc_norm_w", [P, 4])
    halves = sb("halves", [P, P])
    above = sb("above", [P, P + 1])
    eps = sb("ssm_eps", [P, 1])
    half_pi = sb("ssm_half_pi", [P, 1])
    bet = sb("bet", [P, NT, 2])
    gam = sb("gam", [P, NT, 2])
    dts = sb("dts", [P, SEG])
    ang = sb("ang", [P, SEG])
    turns = sb("turns", [P, SEG])
    red = sb("red", [P, SEG])
    sn = sb("sn", [P, SEG])
    cs = sb("cs", [P, SEG])
    sq = sb("sq", [P, 4, SEG])
    rms = sb("rms", [P, 2, SEG])
    nbc = sb("nbc", [P, 4, SEG])
    pr = sb("pr", [P, 4, SEG])
    pq = sb("pool_products", [P, 2, SEG])
    rot = sb("rot", [P, 2, 4, SEG])
    gdiag = sb("gdiag", [P, 2, 8, P + 1])
    start = sb("start", [P, 3 * P])
    dec = sb("dec", [P, 2, 3 * P])
    mix = sb("mix", [P, 2, 3 * P])
    names = ("const w_loaded th_done dt_kept b_done c_done sq_b sq_c ssq_b ssq_c ln_b ln_c r_b r_c "
             "ang_in ang_done red_k red_done trig cabs n_b n_c aff_b aff_c prod_v rot_v prod_p rot_p "
             "al_done start_done dec_done mix_done s_done y_done y_kept cols_kept gdiag_done set ctr_k").split()
    s = {n: c.sem("ssm_" + n) for n in names}
    with own, nc.Block() as block:

        @block.sync
        def _(sp):
            sp.dma_start(norm_w[:], w["norm_w"]).then_inc(s["const"], 16)
            sp.dma_start(halves[:], w["halves"]).then_inc(s["const"], 16)
            sp.dma_start(above[:], w["above"]).then_inc(s["const"], 16)
            with nc.sync.Fori(0, PAIRS) as i:
                sp.wait_ge(s["y_done"], i * 4 + 1)
                sp.wait_ge(s["rot_p"], i * 8 + 1)
                sp.dma_start(wp[:], w["pair"][bass.ds(i, 1)].rearrange("o p k j m -> p (o k) j m")
                             ).then_inc(s["w_loaded"], 16)
                sp.dma_start(sel[:], w["sel"][bass.ds(i, 1)].rearrange("o p j m -> p (o j) m")
                             ).then_inc(s["w_loaded"], 16)
                sp.dma_start(bias[:], w["bias"][bass.ds(i, 1)].rearrange("o p j -> p (o j)")
                             ).then_inc(s["w_loaded"], 16)

        def project(pe, i, n):
            x = [c.x_t[:, k, SEG * n:SEG * (n + 1)] for k in range(KD)]
            pe.wait_ge(s["ln_b"], i * 4 + n + 1)
            for k in range(KD):
                nc.tensor.matmul(c.bank[:, 4, :], wp[:, k, 0, :], x[k], start=k == 0, stop=k == 1)
            pe.wait_ge(s["ln_c"], i * 4 + n + 1)
            nc.tensor.matmul(c.bank[:, 5, :], sel[:, 0, :], dt_t[:, SEG * n:SEG * (n + 1)], start=True,
                             stop=True).then_inc(s["th_done"], 1)
            for g, (free, done) in enumerate((("n_b", "b_done"), ("n_c", "c_done"))):
                pe.wait_ge(s[free], i * 8 + 2 * n + 2)
                for j in range(2):
                    for k in range(KD):
                        last = nc.tensor.matmul(c.bank[:, 2 * g + j, :], wp[:, k, 1 + 2 * g + j, :], x[k],
                                                start=k == 0, stop=k == 1)
                last.then_inc(s[done], 1)
            pe.wait_ge(s["ang_in"], i * 4 + n + 1)
            pe.wait_ge(s["sq_b"], i * 8 + 2 * n + 2)
            for j in range(2):
                last = nc.tensor.matmul(c.bank[:, 4, :], halves[:], sq[:, j, :], start=j == 0, stop=j == 1)
            last.then_inc(s["ssq_b"], 1)
            pe.wait_ge(s["dt_kept"], i * 4 + n + 1)
            pe.wait_ge(s["sq_c"], i * 8 + 2 * n + 2)
            for j in range(2):
                last = nc.tensor.matmul(c.bank[:, 5, :], halves[:], sq[:, 2 + j, :], start=j == 0, stop=j == 1)
            last.then_inc(s["ssq_c"], 1)

        def attend_pe(pe, i, n):
            pe.wait_ge(s["rot_v"], i * 8 + 2 * n + 2)
            pe.wait_ge(s["rot_p"], i * 8 + 2 * n + 3)
            r = rot[:, n % 2]
            for b in range(2):
                pe.wait_ge(s["dec_done"], i * 16 + 4 * n + 2 * b + 1)
                for h in range(2):
                    last = nc.tensor.matmul(c.bank[:, 6, T * h:T * (h + 1)], sel[:, 1 + h, :],
                                            alpha_t[:, SEG * n + T * b:SEG * n + T * (b + 1)],
                                            start=True, stop=True)
                last.then_inc(s["al_done"], 1)
                for h in range(2):
                    u = 2 * b + h
                    pe.wait_ge(s["mix_done"], i * 16 + 4 * n + u + MIX0)
                    if u == 0:
                        pe.wait_ge(s["y_kept"], i * 4 + n + 1)
                    rows = slice(64 * h, 64 * h + 64)
                    for blk in range(2):
                        t0 = T * b + P * blk
                        width = T - P * blk
                        out = c.bank[:, 7, 0:T] if blk == 0 else c.bank[:, 7, T:T + P]
                        for j in range(2):
                            last = nc.tensor.matmul(out, r[rows, j, t0:t0 + P], r[rows, 2 + j, t0:t0 + width],
                                                    start=j == 0, stop=j == 1)
                    last.then_inc(s["s_done"], 1)
                    pe.wait_ge(s["mix_done"], i * 16 + 4 * n + u + MIX0 + 1)
                    m = mix[:, u % 2]
                    tile = 4 * n + 2 * b
                    x0, x1 = (xh[:, tile + blk, bass.ds(i * 16 + 8 * h, 8)] for blk in range(2))
                    y0 = 384 + 32 * b + 8 * h
                    nc.tensor.matmul(c.bank[:, 7, y0:y0 + 8], m[:, 0:P], x0, start=True, stop=True)
                    nc.tensor.matmul(c.bank[:, 7, y0 + 16:y0 + 24], m[:, P:2 * P], x0, start=True, stop=False)
                    last = nc.tensor.matmul(c.bank[:, 7, y0 + 16:y0 + 24], m[:, 2 * P:], x1, start=False,
                                            stop=True)
            last.then_inc(s["y_done"], 1)

        @block.tensor
        def _(pe):
            pe.sem_inc(s["y_done"], 1)
            pe.wait_ge(s["const"], 48)
            with nc.tensor.Fori(0, PAIRS) as i:
                pe.wait_ge(s["w_loaded"], i * 48 + 48)
                for n in range(NSEG + 1):
                    if n < NSEG:
                        project(pe, i, n)
                    if n:
                        attend_pe(pe, i, n - 1)

        @block.scalar
        def _(act):
            for n in ("ln_b", "ln_c", "trig"):
                act.sem_inc(s[n], 1)
            act.wait_ge(s["set"], 1)
            act.wait_ge(s["const"], 48)

            def scale_part(i, n):
                act.wait_ge(s["th_done"], i * 4 + n + 1)
                nc.scalar.activation(dts[:], c.bank[:, 5, :], ACT.Copy).then_inc(s["dt_kept"], 1)
                for g, (done, sqs) in enumerate((("b_done", "sq_b"), ("c_done", "sq_c"))):
                    act.wait_ge(s[done], i * 4 + n + 1)
                    for j in range(2):
                        nc.scalar.activation(sq[:, 2 * g + j, :], c.bank[:, 2 * g + j, :], ACT.Square
                                             ).then_inc(s[sqs], 1)
                for g, (ssq, ln, r) in enumerate((("ssq_b", "ln_b", "r_b"), ("ssq_c", "ln_c", "r_c"))):
                    act.wait_ge(s[ssq], i * 4 + n + 1)
                    nc.scalar.activation(rms[:, g, :], c.bank[:, 4 + g, :], ACT.Ln, scale=1.0 / SN,
                                         bias=eps[:, 0:1]).then_inc(s[ln], 1)
                    act.wait_ge(s[ln], i * 4 + n + 2)
                    nc.scalar.activation(rms[:, g, :], rms[:, g, :], ACT.Exp, scale=-0.5).then_inc(s[r], 1)
                act.wait_ge(s["red_done"], i * 4 + n + 1)
                act.wait_ge(s["prod_p"], i * 8 + 2 * n + 2)
                act.wait_ge(s["prod_v"], i * 4 + n + 1)
                nc.scalar.activation(sn[:], red[:], ACT.Sin).then_inc(s["trig"], 1)
                nc.scalar.activation(cs[:], red[:], ACT.Abs).then_inc(s["cabs"], 1)
                act.wait_ge(s["cabs"], i * 4 + n + 1)
                nc.scalar.activation(cs[:], cs[:], ACT.Sin, scale=-1.0, bias=half_pi[:, 0:1]
                                     ).then_inc(s["trig"], 1)

                for g, (src, done) in enumerate((("n_b", "aff_b"), ("n_c", "aff_c"))):
                    for j in range(2):
                        k = 2 * g + j
                        act.wait_ge(s[src], i * 8 + 2 * n + j + 3)
                        nc.scalar.activation(nbc[:, k, :], nbc[:, k, :], ACT.Identity, scale=norm_w[:, k:k + 1],
                                             bias=bias[:, k:k + 1]).then_inc(s[done], 1)

            with nc.scalar.Fori(0, PAIRS) as i:
                act.wait_ge(s["w_loaded"], i * 48 + 48)
                for n in range(NSEG):
                    scale_part(i, n)

        def rotate_dve(dve, i, n):
            dve.wait_ge(s["dt_kept"], i * 4 + n + 1)
            nc.vector.tensor_tensor(ang[:], c.bank[:, 4, :], dts[:], ALU.mult).then_inc(s["ang_in"], 1)
            dve.wait_ge(s["ang_in"], i * 4 + n + 1)
            for b in range(2):
                last = nc.vector.tensor_tensor_scan(turns[:, T * b:T * (b + 1)],
                                                    c.ones[:, 0:1].broadcast_to([P, T]),
                                                    ang[:, T * b:T * (b + 1)], 0.0, ALU.mult, ALU.add)
            last.then_inc(s["ang_done"], 1)
            dve.wait_ge(s["ang_done"], i * 4 + n + 1)
            nc.vector.tensor_scalar(ang[:], turns[:], INV_2PI, ROUND, ALU.mult, ALU.add).then_inc(s["red_k"], 1)
            dve.wait_ge(s["red_k"], i * 4 + n + 1)
            nc.vector.tensor_scalar(ang[:], ang[:], ROUND, None, ALU.subtract).then_inc(s["ctr_k"], 1)
            dve.wait_ge(s["ctr_k"], i * 12 + 3 * n + 1)
            nc.vector.scalar_tensor_tensor(turns[:], ang[:], -TWO_PI_HI, turns[:], ALU.mult, ALU.add
                                           ).then_inc(s["ctr_k"], 1)
            dve.wait_ge(s["ctr_k"], i * 12 + 3 * n + 2)
            nc.vector.scalar_tensor_tensor(turns[:], ang[:], -TWO_PI_LO, turns[:], ALU.mult, ALU.add
                                           ).then_inc(s["ctr_k"], 1)
            dve.wait_ge(s["ctr_k"], i * 12 + 3 * n + 3)
            dve.wait_ge(s["trig"], i * 8 + 2 * n + 1)
            nc.vector.tensor_scalar(red[:], turns[:], PI, -PI, ALU.min, ALU.max).then_inc(s["red_done"], 1)
            for g, (r, done) in enumerate((("r_b", "n_b"), ("r_c", "n_c"))):
                dve.wait_ge(s[r], i * 4 + n + 1)
                if g == 0:
                    dve.wait_ge(s["prod_p"], i * 8 + 2 * n + 2)
                for j in range(2):
                    nc.vector.tensor_tensor(nbc[:, 2 * g + j, :], c.bank[:, 2 * g + j, :], rms[:, g, :],
                                            ALU.mult).then_inc(s[done], 1)
            dve.wait_ge(s["aff_b"], i * 8 + 2 * n + 2)
            dve.wait_ge(s["trig"], i * 8 + 2 * n + 3)
            nc.vector.tensor_tensor(pr[:, 0, :], nbc[:, 0, :], cs[:], ALU.mult)
            nc.vector.tensor_tensor(pr[:, 1, :], nbc[:, 1, :], sn[:], ALU.mult)
            dve.wait_ge(s["aff_c"], i * 8 + 2 * n + 2)
            nc.vector.tensor_tensor(pr[:, 2, :], nbc[:, 2, :], cs[:], ALU.mult)
            nc.vector.tensor_tensor(pr[:, 3, :], nbc[:, 3, :], sn[:], ALU.mult).then_inc(s["prod_v"], 1)
            dve.wait_ge(s["prod_v"], i * 4 + n + 2)
            nc.vector.tensor_tensor(rot[:, n % 2, 0, :], pr[:, 0, :], pr[:, 1, :], ALU.subtract
                                    ).then_inc(s["rot_v"], 1)
            nc.vector.tensor_tensor(rot[:, n % 2, 2, :], pr[:, 2, :], pr[:, 3, :], ALU.subtract
                                    ).then_inc(s["rot_v"], 1)

        def attend_dve(dve, i, n):
            dve.wait_ge(s["gdiag_done"], i * 4 + n + 2)
            for b in range(2):
                dve.wait_ge(s["al_done"], i * 8 + 2 * n + b + 1)
                for h in range(2):
                    u = 2 * b + h
                    d = dec[:, u % 2]
                    tile = 4 * n + 2 * b
                    g0, g1 = (gdiag[:, n % 2, 2 * (2 * b + k) + h, :] for k in range(2))
                    nc.vector.scalar_tensor_tensor(start[:, 0:P + 1], above[:], bet[:, tile, h:h + 1], g0,
                                                   ALU.mult, ALU.add)
                    nc.vector.scalar_tensor_tensor(start[:, T:T + P], above[:, 0:P], bet[:, tile + 1, h:h + 1],
                                                   g1[:, 0:P], ALU.mult, ALU.add).then_inc(s["start_done"], 1)
                    dve.wait_ge(s["start_done"], i * 16 + 4 * n + u + 1)
                    nc.vector.tensor_tensor_scan(d[:, 0:T], c.bank[:, 6, T * h:T * h + T], start[:, 0:T], 0.0,
                                                 ALU.mult, ALU.add)
                    nc.vector.tensor_tensor_scan(d[:, T:T + P], c.bank[:, 6, T * h + P:T * h + T],
                                                 start[:, T:T + P], 0.0, ALU.mult, ALU.add
                                                 ).then_inc(s["dec_done"], 1)
                    dve.wait_ge(s["dec_done"], i * 16 + 4 * n + u + 2)
                    dve.wait_ge(s["s_done"], i * 16 + 4 * n + u + 1)
                    nc.vector.tensor_tensor(mix[:, u % 2, :], d, c.bank[:, 7, 0:3 * P], ALU.mult
                                            ).then_inc(s["mix_done"], 1)
            dve.wait_ge(s["y_done"], i * 4 + n + 2)
            nc.vector.tensor_copy(y_tok[:, 4 * n:4 * n + 4, bass.ds(i * 16, 16)],
                                  c.bank[:, 7, 384:448].rearrange("p (t h) -> p t h", h=16)
                                  ).then_inc(s["y_kept"], 1)

        @block.vector
        def _(dve):
            for n, v in (("n_b", 2), ("n_c", 2), ("dec_done", 1), ("mix_done", MIX0), ("prod_v", 1), ("y_kept", 1)):
                dve.sem_inc(s[n], v)
            nc.vector.memset(eps[:], 1e-6)
            nc.vector.memset(half_pi[:], HALF_PI)
            nc.vector.memset(gdiag[:], 0.0)
            nc.vector.memset(start[:], 0.0).then_inc(s["set"], 1)
            dve.wait_ge(s["const"], 48)
            with nc.vector.Fori(0, PAIRS) as i:
                dve.wait_ge(s["gdiag_done"], i * 4 + 1)
                nc.vector.tensor_copy(bet[:], beta_tok[:, :, bass.ds(i * 2, 2)]).then_inc(s["cols_kept"], 1)
                nc.vector.tensor_copy(gam[:], gamma_tok[:, :, bass.ds(i * 2, 2)]).then_inc(s["cols_kept"], 1)
                dve.wait_ge(s["cols_kept"], i * 2 + 2)
                for n in range(NSEG + 1):
                    if n < NSEG:
                        rotate_dve(dve, i, n)
                    if n:
                        attend_dve(dve, i, n - 1)

        @block.gpsimd
        def _(pool):
            pool.sem_inc(s["rot_p"], 1)
            pool.sem_inc(s["gdiag_done"], 1)
            pool.wait_ge(s["set"], 1)
            pool.sem_inc(s["prod_p"], 2)
            with nc.gpsimd.Fori(0, PAIRS) as i:
                pool.wait_ge(s["cols_kept"], i * 2 + 2)
                for n in range(NSEG):
                    pool.wait_ge(s["mix_done"], i * 16 + 4 * n + MIX0 - 4)
                    nc.gpsimd.tensor_tensor(
                        gdiag[:, n % 2, :, 0:P], c.ident[:].unsqueeze(1).broadcast_to([P, 8, P]),
                        gam[:, 4 * n:4 * n + 4, :].rearrange("p t h -> p (t h)").unsqueeze(2).broadcast_to(
                            [P, 8, P]), ALU.mult).then_inc(s["gdiag_done"], 1)
                    pool.wait_ge(s["trig"], i * 8 + 2 * n + 3)
                    pool.wait_ge(s["mix_done"], i * 16 + 4 * n + MIX0 - 4)
                    for g in range(2):
                        done = ("aff_b", "aff_c")[g]
                        pool.wait_ge(s[done], i * 8 + 2 * n + 2)
                        pool.wait_ge(s["rot_p"], i * 8 + 2 * n + 1 + g)
                        nc.gpsimd.tensor_tensor(pq[:, 0, :], nbc[:, 2 * g, :], sn[:], ALU.mult)
                        nc.gpsimd.tensor_tensor(pq[:, 1, :], nbc[:, 2 * g + 1, :], cs[:], ALU.mult
                                                ).then_inc(s["prod_p"], 1)
                        pool.wait_ge(s["prod_p"], i * 8 + 2 * n + 3 + g)
                        nc.gpsimd.tensor_tensor(rot[:, n % 2, 2 * g + 1, :], pq[:, 0, :], pq[:, 1, :],
                                                ALU.add).then_inc(s["rot_p"], 1)


def ssm_output(c, w, y_tok):
    nc = c.nc
    own = ExitStack()
    wz = c.sbuf("wz", [P, KD, DIN], ctx=own)
    wo = c.sbuf("ssm_wo", [P, DIN // P, D], ctx=own)
    z = c.sbuf("z", [P, 2, DIN], ctx=own)
    yz = c.sbuf("yz", [P, 2, DIN], ctx=own)
    yz_t = c.sbuf("yz_t", [P, 2, DIN // P, P], ctx=own)
    loaded, z_done, z_kept, gated, turned, copied, o_done, added = (
        c.sem("ssmout_" + n) for n in "loaded z_done z_kept gated turned copied o_done added".split())
    with own, nc.Block() as block:

        @block.sync
        def _(sp):
            sp.dma_start(wz[:], w["z"]).then_inc(loaded, 16)
            sp.dma_start(wo[:], w["out"]).then_inc(loaded, 16)

        @block.tensor
        def _(pe):
            def gate_input(t):
                if t >= 2:
                    pe.wait_ge(z_kept, t - 1)
                for k in range(KD):
                    last = nc.tensor.matmul(c.bank[:, t % 2, :], c.x_t[:, k, P * t:P * (t + 1)], wz[:, k, :],
                                            start=k == 0, stop=k == KD - 1)
                last.then_inc(z_done, 1)

            pe.wait_ge(loaded, 32)
            gate_input(0)
            for t in range(NT):
                if t + 1 < NT:
                    gate_input(t + 1)
                pe.wait_ge(gated, t + 1)
                if t >= 2:
                    pe.wait_ge(copied, t - 1)
                for j in range(4):
                    last = nc.tensor.transpose(c.bank[:, 2 + t % 2, P * j:P * (j + 1)],
                                               yz[:, t % 2, P * j:P * (j + 1)], c.ident[:])
                last.then_inc(turned, 1)
                pe.wait_ge(copied, t + 1)
                if t >= 2:
                    pe.wait_ge(added, t - 1)
                for j in range(4):
                    last = nc.tensor.matmul(c.bank[:, 4 + t % 2, 0:D], yz_t[:, t % 2, j, :], wo[:, j, :],
                                            start=j == 0, stop=j == 3)
                last.then_inc(o_done, 1)

        @block.scalar
        def _(act):
            for t in range(NT):
                act.wait_ge(z_done, t + 1)
                if t >= 2:
                    act.wait_ge(gated, t - 1)
                nc.scalar.activation(z[:, t % 2, :], c.bank[:, t % 2, :], ACT.Silu).then_inc(z_kept, 1)

        @block.vector
        def _(dve):
            for t in range(NT):
                dve.wait_ge(z_kept, t + 1)
                if t >= 2:
                    dve.wait_ge(turned, t - 1)
                nc.vector.tensor_tensor(yz[:, t % 2, :], y_tok[:, t, :], z[:, t % 2, :], ALU.mult
                                        ).then_inc(gated, 1)
                dve.wait_ge(turned, t + 1)
                if t >= 2:
                    dve.wait_ge(o_done, t - 1)
                nc.vector.tensor_copy(yz_t[:, t % 2, :, :].rearrange("p j t -> p (j t)"),
                                      c.bank[:, 2 + t % 2, :]).then_inc(copied, 1)
                dve.wait_ge(o_done, t + 1)
                nc.vector.tensor_tensor(c.x_tok[:, t, :], c.x_tok[:, t, :], c.bank[:, 4 + t % 2, 0:D],
                                        ALU.add).then_inc(added, 1)



XH, XD = 16, 128
XP = XH // 2
BIG = 1e30


def cross_attention(c, w, normed):
    nc = c.nc
    own = ExitStack()
    tag = "xn_" if normed else "xm_"

    def sb(name, shape, dt=F32, ctx=own):
        return c.sbuf(tag + name, shape, dt, ctx=ctx)

    kvh = XH if normed else XP
    wq = sb("wq", [P, KD, XH * XD])
    wo = sb("wo", [P, XH, D])
    k_t = sb("k_t", [P, kvh, B * S2])
    v = sb("v", [P, B, XP * XD])
    neg = sb("neg", [P, B * S2])
    main_loaded = c.sem(tag + "main_loaded")
    with own:
        cross_keys(c, w, normed, tag, kvh, wq, wo, k_t, v, neg, main_loaded)
        cross_heads(c, normed, tag, kvh, wq, wo, k_t, v, neg, main_loaded)


def cross_keys(c, w, normed, tag, kvh, wq, wo, k_t, v, neg, main_loaded):
    nc = c.nc
    own = ExitStack()

    def sb(name, shape, dt=F32):
        return c.sbuf(tag + name, shape, dt, ctx=own)

    par = 2 if normed else 1
    wk = sb("wk", [P, kvh * XD])
    wv = sb("wv", [P, par, XP * XD])
    ctx_t = sb("ctx_t", [P, B * S2])
    loaded, k_done, k_kept, sq_done, ssq_done, r_done, v_done, v_kept, m_done = (
        c.sem(tag + n) for n in "loaded k_done k_kept sq_done ssq_done r_done v_done v_kept m_done".split())
    if normed:
        g = sb("g", [P, 2])
        eps = sb("eps", [P, 1])
        sq = sb("sq", [P, 2, B * S2])
        rms = sb("rms", [P, 2, B * S2])
    else:
        mask_row = sb("mask_row", [P, B * S2], U8)
        mask_col = sb("mask_col", [P, B], U8)
        keep = sb("keep", [P, B])
    with own, nc.Block() as block:

        @block.sync
        def _(sp):
            sp.dma_start(ctx_t[:], w["ctx"]).then_inc(loaded, 16)
            sp.dma_start(wk[:], w["k"]).then_inc(loaded, 16)
            sp.dma_start(wv[:], w["v"]).then_inc(loaded, 16)
            if normed:
                sp.dma_start(g[:], w["g"]).then_inc(loaded, 16)
            else:
                sp.dma_start(mask_row[:], w["mask_row"].partition_broadcast(P)).then_inc(loaded, 16)
                sp.dma_start(mask_col[:], w["mask_col"]).then_inc(loaded, 16)
            sp.dma_start(wq[:], w["q"]).then_inc(main_loaded, 16)
            sp.dma_start(wo[:], w["o"]).then_inc(main_loaded, 16)

        all_in = 64 if normed else 80

        @block.tensor
        def _(pe):
            pe.wait_ge(loaded, all_in)
            for h in range(kvh + 1):
                if h < kvh:
                    if h >= 2:
                        pe.wait_ge(k_kept, h - 1)
                    nc.tensor.matmul(c.bank[:, h % 2, :], wk[:, XD * h:XD * (h + 1)], ctx_t[:], start=True,
                                     stop=True).then_inc(k_done, 1)
                if h and normed:
                    pe.wait_ge(sq_done, h)
                    if h >= 3:
                        pe.wait_ge(r_done, 2 * (h - 2) - 1)
                    nc.tensor.matmul(c.bank[:, 2 + h % 2, :], c.ones[:], sq[:, (h - 1) % 2, :], start=True,
                                     stop=True).then_inc(ssq_done, 1)
            for j in range(2 * B):
                b, half = divmod(j, 2)
                if j >= 2:
                    pe.wait_ge(v_kept, j - 1)
                for parity in range(2):
                    last = nc.tensor.matmul(c.bank[64 * parity:64 * parity + 64, 4 + j % 2, :],
                                            ctx_t[:, S2 * b:S2 * (b + 1)],
                                            wv[:, parity % par, SEG * half:SEG * (half + 1)],
                                            start=True, stop=True)
                last.then_inc(v_done, 1)

        @block.scalar
        def _(act):
            if normed:
                act.wait_ge(m_done, 1)
                for h in range(kvh):
                    act.wait_ge(k_done, h + 1)
                    if h >= 2:
                        act.wait_ge(ssq_done, h - 1)
                    nc.scalar.activation(sq[:, h % 2, :], c.bank[:, h % 2, :], ACT.Square).then_inc(sq_done, 1)
                    act.wait_ge(ssq_done, h + 1)
                    if h >= 2:
                        act.wait_ge(k_kept, h - 1)
                    nc.scalar.activation(rms[:, h % 2, :], c.bank[:, 2 + (h + 1) % 2, :], ACT.Ln, scale=1.0 / XD,
                                         bias=eps[:, 0:1]).then_inc(r_done, 1)
                    act.wait_ge(r_done, 2 * h + 1)
                    nc.scalar.activation(rms[:, h % 2, :], rms[:, h % 2, :], ACT.Exp, scale=-0.5
                                         ).then_inc(r_done, 1)
            if not normed:
                act.wait_ge(m_done, 1)
            for j in range(2 * B):
                b, half = divmod(j, 2)
                act.wait_ge(v_done, j + 1)
                out = v[:, b, SEG * half:SEG * (half + 1)]
                if normed:
                    nc.scalar.activation(out, c.bank[:, 4 + j % 2, :], ACT.Copy).then_inc(v_kept, 1)
                else:
                    nc.scalar.activation(out, c.bank[:, 4 + j % 2, :], ACT.Copy, scale=keep[:, b:b + 1]
                                         ).then_inc(v_kept, 1)

        @block.vector
        def _(dve):
            if normed:
                nc.vector.memset(eps[:], 1e-5).then_inc(m_done, 1)
            dve.wait_ge(loaded, all_in)
            if not normed:
                nc.vector.tensor_copy(keep[:], mask_col[:]).then_inc(m_done, 1)
                nc.vector.tensor_scalar(neg[:], mask_row[:], -1.0, BIG, ALU.add, ALU.mult)
            for h in range(kvh):
                if normed:
                    dve.wait_ge(r_done, 2 * h + 2)
                    nc.vector.tensor_tensor(k_t[:, h, :], c.bank[:, h % 2, :], rms[:, h % 2, :], ALU.mult
                                            ).then_inc(k_kept, 1)
                    dve.wait_ge(k_kept, h + 1)
                    nc.vector.tensor_scalar(k_t[:, h, :], k_t[:, h, :], g[:, 0:1], g[:, 1:2], ALU.mult, ALU.mult)
                else:
                    dve.wait_ge(k_done, h + 1)
                    nc.vector.tensor_copy(k_t[:, h, :], c.bank[:, h % 2, :]).then_inc(k_kept, 1)


def cross_heads(c, normed, tag, kvh, wq, wo, k_t, v, neg, main_loaded):
    nc = c.nc
    own = ExitStack()

    def sb(name, shape, dt=F32):
        return c.sbuf(tag + name, shape, dt, ctx=own)

    scale = XD ** -0.5
    q = sb("q", [P, 2, 2, T])
    sc = sb("sc", [P, 2, 4, S2])
    probs = sb("probs", [P, 2, 4, S2])
    top = sb("top", [P, 2, 4])
    total = sb("total", [P, 2, 4])
    p_t = sb("p_t", [P, 2, T])
    o_t = sb("o_t", [P, XH, T])
    vb = sb("vb", [P, XP * XD])
    names = ("q_done q_kept s_done s_used shifted top_done exp_done sums p_done t_done t_kept o_done o_kept v_kept "
             "out_done added sq_done rq_in rq_ln rq_done eps_set").split()
    s = {n: c.sem(tag + "h_" + n) for n in names}
    if normed:
        qsq = sb("qsq", [P, 2, 2, T])
        rq = sb("rq", [P, 2, 4])
        eps = sb("eps_q", [P, 1])
    with own, nc.Block() as block:

        @block.tensor
        def _(pe):
            def queries(i, j):
                pe.wait_ge(s["q_kept"], i * XP + j + 1)
                for h in range(2):
                    for k in range(KD):
                        last = nc.tensor.matmul(c.bank[:, j % 2, T * h:T * (h + 1)],
                                                wq[:, k, XD * (2 * j + h):XD * (2 * j + h + 1)],
                                                c.x_t[:, k, bass.ds(i * T, T)], start=k == 0, stop=k == 1)
                last.then_inc(s["q_done"], 1)

            def scores(i, j):
                pe.wait_ge(s["q_kept"], i * XP + j + 3)
                if normed:
                    pe.wait_ge(s["sq_done"], i * XP + j + 1)
                pe.wait_ge(s["s_used"], i * XP + j + 1)
                for t in range(2):
                    for h in range(2):
                        at = (2 * t + h) * S2
                        head = 2 * j + h if normed else j
                        last = nc.tensor.matmul(c.bank[:, 2 + j % 2, at:at + S2], q[:, j % 2, h, P * t:P * (t + 1)],
                                                k_t[:, head, bass.ds(i * S2, S2)], start=True, stop=True)
                if normed:
                    for t in range(2):
                        for h in range(2):
                            at = 4 * S2 + 2 * t + h
                            last = nc.tensor.matmul(c.bank[:, 2 + j % 2, at:at + 1],
                                                    qsq[:, j % 2, h, P * t:P * (t + 1)], c.ones[:, 0:1],
                                                    start=True, stop=True)
                last.then_inc(s["s_done"], 1)

            def turn(i, j):
                pe.wait_ge(s["p_done"], i * XP + j + 1)
                pe.wait_ge(s["t_kept"], i * XP + j + 1)
                for t in range(2):
                    last = nc.tensor.transpose(c.bank[:, 4, P * t:P * (t + 1)],
                                               probs[:, j % 2, 2 * t:2 * t + 2, :].rearrange("p h s -> p (h s)"),
                                               c.ident[:])
                last.then_inc(s["t_done"], 1)

            def values(i, j):
                pe.wait_ge(s["t_kept"], i * XP + j + 2)
                pe.wait_ge(s["o_kept"], i * XP + j + 1)
                if j == 0:
                    pe.wait_ge(s["v_kept"], i + 1)
                for h in range(2):
                    rows = slice(64 * h, 64 * h + 64)
                    last = nc.tensor.matmul(c.bank[:, 5 + h, 0:T], vb[rows, XD * j:XD * (j + 1)],
                                            p_t[rows, j % 2, :], start=True, stop=True)
                last.then_inc(s["o_done"], 1)

            for n, v_ in (("s_done", 2), ("t_done", 2), ("o_done", 2), ("out_done", 1)):
                pe.sem_inc(s[n], v_)
            pe.wait_ge(main_loaded, 32)
            if normed:
                pe.wait_ge(s["eps_set"], 1)
            with nc.tensor.Fori(0, B) as i:
                queries(i, 0)
                for j in range(XP + 2):
                    if j + 1 < XP:
                        queries(i, j + 1)
                    if j < XP:
                        scores(i, j)
                    if 1 <= j <= XP:
                        turn(i, j - 1)
                    if j >= 2:
                        values(i, j - 2)
                pe.wait_ge(s["o_kept"], i * XP + XP + 1)
                pe.wait_ge(s["added"], i + 1)
                for t in range(2):
                    for h in range(XH):
                        last = nc.tensor.matmul(c.bank[:, 7, D * t:D * (t + 1)], o_t[:, h, P * t:P * (t + 1)],
                                                wo[:, h, :], start=h == 0, stop=h == XH - 1)
                last.then_inc(s["out_done"], 1)

        @block.scalar
        def _(act):
            act.sem_inc(s["q_kept"], 2)
            act.sem_inc(s["t_kept"], 1)
            act.sem_inc(s["o_kept"], 1)

            def keep_q(i, j):
                act.wait_ge(s["q_done"], i * XP + j + 1)
                act.wait_ge(s["s_done"], i * XP + j + 1)
                nc.scalar.activation(q[:, j % 2].rearrange("p h t -> p (h t)"), c.bank[:, j % 2, :], ACT.Copy
                                     ).then_inc(s["q_kept"], 1)

            def exps(i, j):
                if normed:
                    act.wait_ge(s["rq_in"], i * XP + j + 1)
                    nc.scalar.activation(rq[:, j % 2, :], rq[:, j % 2, :], ACT.Ln,
                                         scale=1.0 / XD, bias=eps[:, 0:1]).then_inc(s["rq_ln"], 1)
                    act.wait_ge(s["rq_ln"], i * XP + j + 1)
                    nc.scalar.activation(rq[:, j % 2, :], rq[:, j % 2, :], ACT.Exp, scale=-0.5
                                         ).then_inc(s["rq_done"], 1)
                act.wait_ge(s["shifted"], i * XP + j + 1)
                nc.scalar.activation(sc[:, j % 2], sc[:, j % 2], ACT.Exp, scale=scale).then_inc(s["exp_done"], 1)

            def keep_t(i, j):
                act.wait_ge(s["t_done"], i * XP + j + 3)
                act.wait_ge(s["o_done"], i * XP + j + 1)
                nc.scalar.activation(p_t[:, j % 2, :], c.bank[:, 4, 0:T], ACT.Copy).then_inc(s["t_kept"], 1)

            def keep_o(i, j):
                act.wait_ge(s["o_done"], i * XP + j + 3)
                if j == 0:
                    act.wait_ge(s["out_done"], i + 1)
                nc.scalar.activation(o_t[:, 2 * j:2 * j + 2, :],
                                     c.bank[:, 5:7, 0:T], ACT.Copy
                                     ).then_inc(s["o_kept"], 1)

            if normed:
                act.wait_ge(s["eps_set"], 1)
            with nc.scalar.Fori(0, B) as i:
                keep_q(i, 0)
                for j in range(XP + 2):
                    if j + 1 < XP:
                        keep_q(i, j + 1)
                    if j < XP:
                        exps(i, j)
                    if 1 <= j <= XP:
                        keep_t(i, j - 1)
                    if j >= 2:
                        keep_o(i, j - 2)

        @block.vector
        def _(dve):
            dve.sem_inc(s["s_used"], 2)
            dve.sem_inc(s["added"], 1)
            if normed:
                nc.vector.memset(eps[:], 1e-5).then_inc(s["eps_set"], 1)

            def shift(i, j):
                dve.wait_ge(s["s_done"], i * XP + j + 3)
                scores = c.bank[:, 2 + j % 2, 0:4 * S2].rearrange("p (g s) -> p g s", s=S2)
                spread = top[:, j % 2, :].unsqueeze(2).broadcast_to([P, 4, S2])
                if normed:
                    nc.vector.tensor_copy(rq[:, j % 2, :], c.bank[:, 2 + j % 2, 4 * S2:4 * S2 + 4]
                                          ).then_inc(s["rq_in"], 1)
                    nc.vector.tensor_reduce(top[:, j % 2, :], scores, AX.X, ALU.max).then_inc(s["top_done"], 1)
                    dve.wait_ge(s["rq_done"], i * XP + j + 1)
                    dve.wait_ge(s["top_done"], i * XP + j + 1)
                    nc.vector.tensor_tensor(sc[:, j % 2], scores, spread, ALU.subtract).then_inc(s["s_used"], 1)
                    dve.wait_ge(s["s_used"], i * XP + j + 3)
                    nc.vector.tensor_tensor(sc[:, j % 2], sc[:, j % 2],
                                            rq[:, j % 2, :].unsqueeze(2).broadcast_to([P, 4, S2]), ALU.mult
                                            ).then_inc(s["shifted"], 1)
                else:
                    bias = neg[:, bass.ds(i * S2, S2)].unsqueeze(1).broadcast_to([P, 4, S2])
                    nc.vector.tensor_tensor(sc[:, j % 2], scores, bias, ALU.add).then_inc(s["s_used"], 1)
                    dve.wait_ge(s["s_used"], i * XP + j + 3)
                    nc.vector.tensor_reduce(top[:, j % 2, :], sc[:, j % 2], AX.X, ALU.max).then_inc(s["top_done"], 1)
                    dve.wait_ge(s["top_done"], i * XP + j + 1)
                    nc.vector.tensor_tensor(sc[:, j % 2], sc[:, j % 2], spread, ALU.subtract
                                            ).then_inc(s["shifted"], 1)

            def normalise(i, j):
                dve.wait_ge(s["exp_done"], i * XP + j + 1)
                nc.vector.tensor_reduce(total[:, j % 2, :], sc[:, j % 2], AX.X, ALU.add).then_inc(s["sums"], 1)
                dve.wait_ge(s["sums"], i * 2 * XP + 2 * j + 1)
                nc.vector.reciprocal(total[:, j % 2, :], total[:, j % 2, :]).then_inc(s["sums"], 1)
                dve.wait_ge(s["sums"], i * 2 * XP + 2 * j + 2)
                dve.wait_ge(s["t_done"], i * XP + j + 1)
                nc.vector.tensor_tensor(probs[:, j % 2], sc[:, j % 2],
                                        total[:, j % 2, :].unsqueeze(2).broadcast_to([P, 4, S2]), ALU.mult
                                        ).then_inc(s["p_done"], 1)

            with nc.vector.Fori(0, B) as i:
                for j in range(XP + 1):
                    if j < XP:
                        shift(i, j)
                    if j:
                        normalise(i, j - 1)
                dve.wait_ge(s["out_done"], i + 2)
                nc.vector.tensor_tensor(c.x_tok[:, bass.ds(i * 2, 2), :], c.x_tok[:, bass.ds(i * 2, 2), :],
                                        c.bank[:, 7, :].rearrange("p (t d) -> p t d", t=2), ALU.add
                                        ).then_inc(s["added"], 1)

        @block.gpsimd
        def _(pool):
            with nc.gpsimd.Fori(0, B) as i:
                pool.wait_ge(s["o_done"], i * XP + 2)
                nc.gpsimd.tensor_copy(vb[:], v[:, bass.ds(i, 1), :].rearrange("p o n -> p (o n)")
                                      ).then_inc(s["v_kept"], 1)
                if normed:
                    for j in range(XP):
                        pool.wait_ge(s["q_kept"], i * XP + j + 3)
                        pool.wait_ge(s["s_done"], i * XP + j + 1)
                        nc.gpsimd.tensor_tensor(qsq[:, j % 2], q[:, j % 2], q[:, j % 2], ALU.mult
                                                ).then_inc(s["sq_done"], 1)



def gated_ffn(c, tag, rows, w_in, w_out, scale_gate, scale_up, ready):
    nc = c.nc
    own = ExitStack()
    M = len(rows)
    gate = c.sbuf(tag + "gate_out", [P, 2, SEG], ctx=own)
    hid = c.sbuf(tag + "hid", [P, M, SEG], ctx=own)
    s = {n: c.sem(tag + n) for n in "in_done silu_done hid_done out_done added".split()}
    with own, nc.Block() as block:

        @block.tensor
        def _(pe):
            with nc.tensor.Fori(0, NSEG) as i:
                for m in range(M):
                    r = rows[m]
                    pe.wait_ge(s["hid_done"], i * M + m + 1)
                    for g in range(2):
                        for k in range(KD):
                            last = nc.tensor.matmul(c.bank[:, 2 * (m % 2) + g, :], w_in[:, k, g, P * m:P * (m + 1)],
                                                    c.x_t[:, k, bass.ds(i * SEG, SEG)], start=k == 0, stop=k == 1)
                    last.then_inc(s["in_done"], 1)
                pe.wait_ge(s["hid_done"], i * M + M + 2)
                for half in range(2):
                    pe.wait_ge(s["added"], i * 2 + half + 1)
                    for t in range(2):
                        for m in range(M):
                            r = rows[m]
                            at = P * (2 * half + t)
                            last = nc.tensor.matmul(c.bank[:, 4 + half, D * t:D * (t + 1)], hid[0:r, m, at:at + P],
                                                    w_out[0:r, m, :], start=m == 0, stop=m == M - 1)
                    last.then_inc(s["out_done"], 1)

        @block.scalar
        def _(act):
            with nc.scalar.Fori(0, NSEG) as i:
                for m in range(M):
                    r = rows[m]
                    act.wait_ge(s["in_done"], i * M + m + 1)
                    act.wait_ge(s["hid_done"], i * M + m + 1)
                    nc.scalar.activation(gate[0:r, m % 2, :], c.bank[0:r, 2 * (m % 2), :], ACT.Silu,
                                         scale=scale_gate[0:r, m:m + 1]).then_inc(s["silu_done"], 1)

        @block.vector
        def _(dve):
            dve.sem_inc(s["hid_done"], 2)
            dve.sem_inc(s["added"], 2)
            with nc.vector.Fori(0, NSEG) as i:
                for m in range(M):
                    r = rows[m]
                    dve.wait_ge(s["silu_done"], i * M + m + 1)
                    nc.vector.scalar_tensor_tensor(hid[0:r, m, :], c.bank[0:r, 2 * (m % 2) + 1, :],
                                                   scale_up[0:r, m:m + 1], gate[0:r, m % 2, :], ALU.mult, ALU.mult
                                                   ).then_inc(s["hid_done"], 1)
                for half in range(2):
                    dve.wait_ge(s["out_done"], i * 2 + half + 1)
                    x = c.x_tok[:, bass.ds(i * 4 + 2 * half, 2), :]
                    nc.vector.tensor_tensor(x, x, c.bank[:, 4 + half, :].rearrange("p (t d) -> p t d", t=2),
                                            ALU.add).then_inc(s["added"], 1)


HID0, HSCALE = 1024, 64.0


def hadamard_ffn(c, w):
    nc = c.nc
    own = ExitStack()
    M = HID0 // P
    w_in = c.sbuf("had_in", [P, KD, 2, HID0], ctx=own)
    w_out = c.sbuf("had_out", [P, M, D], ctx=own)
    scales = c.sbuf("had_scales", [P, 2, M], ctx=own)
    with own:
        mine = ExitStack()
        up = c.sbuf("had_rows", [P, 2, 2 * M, D], ctx=mine)
        dn = c.sbuf("had_down_rows", [P, 2, KD, HID0], ctx=mine)
        su_in = c.sbuf("had_su_in", [P, KD], ctx=mine)
        su_out = c.sbuf("had_su_out", [P, M], ctx=mine)
        down_scale = c.sbuf("had_down_scale", [P, KD], ctx=mine)
        loaded, plus, minus, turned, kept, scaled = (
            c.sem("had_" + n) for n in "loaded plus minus turned kept scaled".split())
        stages_in = D.bit_length() - 1
        stages_out = HID0.bit_length() - 1
        with mine, nc.Block() as block:

            @block.sync
            def _(sp):
                sp.dma_start(up[:, 0], w["rows"]).then_inc(loaded, 16)
                sp.dma_start(dn[:, 0], w["down"]).then_inc(loaded, 16)
                for t, n in ((su_in, "su_in"), (su_out, "su_out"), (down_scale, "down_scale"), (scales, "scales")):
                    sp.dma_start(t[:], w[n]).then_inc(loaded, 16)

            def butterflies(eng, unit, op, mine_done, other_done):
                eng.wait_ge(loaded, 96)
                n = 0
                for buf, stages in ((up, stages_in), (dn, stages_out)):
                    for st in range(stages):
                        if n:
                            eng.wait_ge(mine_done, n)
                            eng.wait_ge(other_done, n)
                        h = 1 << st
                        src, dst = (buf[:, (st + o) % 2].rearrange("p m d -> p (m d)").rearrange(
                            "p (g two h) -> p g two h", two=2, h=h) for o in range(2))
                        which = 0 if op == ALU.add else 1
                        unit.tensor_tensor(dst[:, :, which, :], src[:, :, 0, :], src[:, :, 1, :], op
                                           ).then_inc(mine_done, 1)
                        n += 1

            all_stages = stages_in + stages_out
            up_at, dn_at = stages_in % 2, stages_out % 2

            @block.vector
            def _(dve):
                butterflies(dve, nc.vector, ALU.add, plus, minus)
                dve.wait_ge(plus, all_stages)
                dve.wait_ge(minus, all_stages)
                nc.vector.tensor_scalar(scales[:], scales[:], HSCALE, None, ALU.mult)
                nc.vector.tensor_scalar(down_scale[:], down_scale[:], HSCALE, None, ALU.mult).then_inc(scaled, 1)
                nc.vector.tensor_scalar(su_in[:], su_in[:], D ** -0.5 / HSCALE, None, ALU.mult).then_inc(scaled, 1)
                nc.vector.tensor_scalar(su_out[:], su_out[:], HID0 ** -0.5 / HSCALE, None, ALU.mult
                                        ).then_inc(scaled, 1)
                dve.wait_ge(scaled, 1)
                for k in range(KD):
                    nc.vector.tensor_scalar(dn[:, dn_at, k, :], dn[:, dn_at, k, :], down_scale[:, k:k + 1], None,
                                            ALU.mult).then_inc(scaled, 1)

            @block.gpsimd
            def _(pool):
                butterflies(pool, nc.gpsimd, ALU.subtract, minus, plus)

            @block.tensor
            def _(pe):
                pe.wait_ge(plus, stages_in)
                pe.wait_ge(minus, stages_in)
                n = 0
                for g in range(2):
                    for k in range(KD):
                        for half in range(2):
                            if n >= 4:
                                pe.wait_ge(kept, n - 3)
                            for j in range(4):
                                m = g * M + 4 * half + j
                                last = nc.tensor.transpose(c.bank[:, n % 4, P * j:P * (j + 1)],
                                                           up[:, up_at, m, P * k:P * (k + 1)], c.ident[:])
                            last.then_inc(turned, 1)
                            n += 1
                pe.wait_ge(scaled, 3 + KD)
                for m in range(M):
                    pe.wait_ge(kept, n - 3)
                    for k in range(KD):
                        last = nc.tensor.transpose(c.bank[:, n % 4, P * k:P * (k + 1)],
                                                   dn[:, dn_at, k, P * m:P * (m + 1)], c.ident[:])
                    last.then_inc(turned, 1)
                    n += 1

            @block.scalar
            def _(act):
                act.wait_ge(scaled, 3)
                n = 0
                for g in range(2):
                    for k in range(KD):
                        for half in range(2):
                            act.wait_ge(turned, n + 1)
                            nc.scalar.activation(w_in[:, k, g, SEG * half:SEG * (half + 1)], c.bank[:, n % 4, :],
                                                 ACT.Copy, scale=su_in[:, k:k + 1]).then_inc(kept, 1)
                            n += 1
                for m in range(M):
                    act.wait_ge(turned, n + 1)
                    nc.scalar.activation(w_out[:, m, :], c.bank[:, n % 4, 0:D], ACT.Copy, scale=su_out[:, m:m + 1]
                                         ).then_inc(kept, 1)
                    n += 1

        gated_ffn(c, "had_", [P] * M, w_in, w_out, scales[:, 0, :], scales[:, 1, :], None)


HID1, ZERO_POINT = 704, 128.0


def dequant_ffn(c, w):
    nc = c.nc
    own = ExitStack()
    M = -(-HID1 // P)
    rows = [min(P, HID1 - P * m) for m in range(M)]
    w_in = c.sbuf("deq_in", [P, KD, 2, P * M], ctx=own)
    w_out = c.sbuf("deq_out", [P, M, D], ctx=own)
    s_gate = c.sbuf("deq_s_gate", [P, M], ctx=own)
    s_up = c.sbuf("deq_s_up", [P, M], ctx=own)
    with own:
        mine = ExitStack()
        q_in = c.sbuf("deq_q_in", [P, KD, 2, HID1], I32, ctx=mine)
        q_out = c.sbuf("deq_q_out", [P, M, D], I32, ctx=mine)
        s_down = c.sbuf("deq_s_down", [P, D], ctx=mine)
        loaded, centred = c.sem("deq_loaded"), c.sem("deq_centred")
        with mine, nc.Block() as block:

            @block.sync
            def _(sp):
                sp.dma_start(q_in[:], w["in"]).then_inc(loaded, 16)
                sp.dma_start(s_down[:], w["s_down"].partition_broadcast(P)).then_inc(loaded, 16)
                for m in range(M):
                    r = rows[m]
                    for t, src in ((q_out[0:r, m, :], w["out"][P * m:P * m + r, :]),
                                   (s_gate[0:r, m:m + 1], w["s_gate"][P * m:P * m + r, :]),
                                   (s_up[0:r, m:m + 1], w["s_up"][P * m:P * m + r, :])):
                        sp.dma_start(t, src).then_inc(loaded, 16)

            @block.vector
            def _(dve):
                dve.wait_ge(loaded, 16 * (2 + 3 * M))
                for k in range(KD):
                    nc.vector.memset(w_in[:, k, :, HID1:], 0.0)
                    nc.vector.tensor_scalar(w_in[:, k, :, 0:HID1], q_in[:, k], ZERO_POINT, None, ALU.subtract)
                for m in range(M):
                    r = rows[m]
                    nc.vector.tensor_scalar(w_out[0:r, m, :], q_out[0:r, m, :], ZERO_POINT, None, ALU.subtract
                                            ).then_inc(centred, 1)
                for m in range(M):
                    r = rows[m]
                    dve.wait_ge(centred, m + 1)
                    nc.vector.tensor_tensor(w_out[0:r, m, :], w_out[0:r, m, :], s_down[0:r, :], ALU.mult)

        gated_ffn(c, "deq_", rows, w_in, w_out, s_gate, s_up, None)



KH, KW = 16, 128
LEVELS = 7
CH = SEG // P


def kda(c, w):
    own = ExitStack()
    xf_t = c.sbuf("xf_t", [P, TOK], ctx=own)
    xg_t = c.sbuf("xg_t", [P, TOK], ctx=own)
    beta = c.sbuf("beta", [KH, TOK], ctx=own)
    neg_a = c.sbuf("kda_neg_a", [P, KH], ctx=own)
    with own:
        kda_gates(c, w, xf_t, xg_t, beta, neg_a)
        kda_heads(c, w, xf_t, xg_t, beta, neg_a)


def kda_gates(c, w, xf_t, xg_t, beta, neg_a):
    nc = c.nc
    own = ExitStack()
    wfg = c.sbuf("wfg", [P, KD, 2, KW], ctx=own)
    wb = c.sbuf("wb", [P, KD, KH], ctx=own)
    loaded, done, kept = (c.sem("kg_" + n) for n in "loaded done kept".split())
    with own, nc.Block() as block:

        @block.sync
        def _(sp):
            sp.dma_start(wfg[:], w["fg"]).then_inc(loaded, 16)
            sp.dma_start(wb[:], w["b"]).then_inc(loaded, 16)
            sp.dma_start(neg_a[:], w["A_log"].partition_broadcast(P)).then_inc(loaded, 16)

        @block.tensor
        def _(pe):
            pe.wait_ge(loaded, 48)
            for q in range(NSEG):
                if q:
                    pe.wait_ge(kept, 3 * q)
                for g in range(3):
                    for k in range(KD):
                        lhs = wb[:, k, :] if g == 2 else wfg[:, k, g, :]
                        out = c.bank[0:KH, 2, :] if g == 2 else c.bank[:, g, :]
                        last = nc.tensor.matmul(out, lhs, c.x_t[:, k, SEG * q:SEG * (q + 1)], start=k == 0,
                                                stop=k == 1)
                    last.then_inc(done, 1)

        @block.scalar
        def _(act):
            for q in range(NSEG):
                cols = slice(SEG * q, SEG * (q + 1))
                for g, out in enumerate((xf_t, xg_t)):
                    act.wait_ge(done, 3 * q + g + 1)
                    nc.scalar.activation(out[:, cols], c.bank[:, g, :], ACT.Copy).then_inc(kept, 1)
                act.wait_ge(done, 3 * q + 3)
                nc.scalar.activation(beta[:, cols], c.bank[0:KH, 2, :], ACT.Sigmoid).then_inc(kept, 1)
            act.wait_ge(loaded, 48)
            nc.scalar.activation(neg_a[:], neg_a[:], ACT.Exp).then_inc(kept, 1)

        @block.vector
        def _(dve):
            dve.wait_ge(kept, 3 * NSEG + 1)
            nc.vector.tensor_scalar(neg_a[:], neg_a[:], -1.0, None, ALU.mult)


def halves_of(ap, m, side):
    if len(ap.shape) == 2:
        return ap.rearrange("p (g two m) -> p g two m", two=2, m=m)[:, :, side, :]
    return ap.rearrange("p c (g two m) -> p c g two m", two=2, m=m)[:, :, :, side, :]


def kda_heads(c, w, xf_t, xg_t, beta, neg_a):
    nc = c.nc
    own = ExitStack()

    def sb(name, shape, dt=F32):
        return c.sbuf("k_" + name, shape, dt, ctx=own)

    wqkv = sb("wqkv", [P, KD, 3, KW])
    wfg2 = sb("wfg2", [P, 2, KW])
    wo = sb("wo", [P, D])
    taps = sb("taps", [P, 3, 5])
    dt_bias = sb("dt_bias", [P, 1])
    sel = sb("sel", [KH, P])
    decay = sb("decay", [P, 1])
    o_norm = sb("o_norm", [P, 1])
    masks = sb("masks", [P, LEVELS, P // 2])
    masks_i = sb("masks_i", [P, LEVELS, P // 2], I32)
    eps6 = sb("eps6", [P, 1])
    eps5 = sb("eps5", [P, 1])
    raw = sb("raw", [P, 3, 2, T + 3])
    conv = sb("conv", [P, 3, SEG])
    act_out = sb("act_out", [P, 3, SEG])
    sq = sb("sq", [P, 2, SEG])
    rn = sb("rn", [P, 2, SEG])
    z = sb("z", [P, SEG])
    tail = sb("tail", [P, SEG])
    low = sb("low", [P, SEG])
    kn = sb("kn", [P, SEG])
    vals = sb("vals", [P, 2, CH, KW])
    sgate = sb("sgate", [P, 2, SEG])
    qn = sb("qn", [P, 2, SEG])
    kq = sb("kq", [P, 2, SEG])
    kqp = sb("kqp", [P, 2, 2, SEG])
    e = sb("e", [P, 2, 2 * SEG])
    ct = sb("ct", [P, LEVELS, CH, P])
    ysb = sb("ysb", [P, LEVELS, CH, P])
    bt = sb("bt", [P, CH, P])
    tm = sb("tm", [P, CH, P])
    xm = sb("xm", [P, CH, P])
    cross = sb("cross", [P, 2, 2, P])
    u = sb("u", [P, CH, KW])
    rest = sb("rest", [P, 2, KW])
    osq = sb("osq", [P, SEG])
    orn = sb("orn", [P, SEG])
    og = sb("og", [P, SEG])
    names = ("const zeroed w_loaded decay_set proj_done raw_kept g_done z_done tail_done low_done ln1_done sp_done a_done gt_done "
             "sg_done tap silu_done vt_done v_kept beta_done sq_done ssq_done ln_done rn_done kn_done kq_done dg_done "
             "ab_done ct_done bt_done upq upp e_done y_done yk d_done tx_done t_init x_done x_kept u_done u_kept "
             "r_done rs_done o_done osq_done oss_done or_ln or_done og_mul og_done out_done xadd").split()
    s = {n: c.sem("kda_" + n) for n in names}
    e_at = [0]
    for lv in range(LEVELS):
        e_at.append(e_at[-1] + (SEG >> lv))

    with own, nc.Block() as block:

        @block.sync
        def _(sp):
            sp.dma_start(o_norm[:], w["o_norm"]).then_inc(s["const"], 16)
            sp.dma_start(masks[:], w["masks"]).then_inc(s["const"], 16)
            with nc.sync.Fori(0, KH) as i:
                sp.wait_ge(s["xadd"], i * 4 + 1)
                for t, n, how in ((wqkv, "qkv", "o p k g m -> p (o k) g m"), (wfg2, "fg2", "o p g m -> p (o g) m"),
                                  (wo, "o", "o p m -> p (o m)"), (taps, "taps", "o p g m -> p (o g) m"),
                                  (dt_bias, "dt_bias", "o p m -> p (o m)"), (sel, "sel", "o p m -> p (o m)")):
                    sp.dma_start(t[:], w[n][bass.ds(i, 1)].rearrange(how)).then_inc(s["w_loaded"], 16)

        def front_pe(pe, i, n, piece):
            cols = slice(SEG * n, SEG * (n + 1))
            if piece == 0:
                pe.wait_ge(s["ln_done"], i * 4 + n + 1)
                pe.wait_ge(s["kq_done"], i * 4 + n + 1)
                for g in range(3):
                    for k in range(KD):
                        last = nc.tensor.matmul(c.bank[:, g, :], wqkv[:, k, g, :], c.x_t[:, k, cols],
                                                start=k == 0, stop=k == 1)
                last.then_inc(s["proj_done"], 1)
                pe.wait_ge(s["sg_done"], i * 4 + n + 1)
                nc.tensor.matmul(c.bank[:, 3, :], wfg2[:, 0, :], xf_t[:, cols], start=True, stop=True
                                 ).then_inc(s["g_done"], 1)
            elif piece == 1:
                pe.wait_ge(s["z_done"], i * 4 + n + 1)
                nc.tensor.matmul(c.bank[:, 3, :], wfg2[:, 1, :], xg_t[:, cols], start=True, stop=True
                                 ).then_inc(s["gt_done"], 1)
            elif piece == 3:
                pe.wait_ge(s["silu_done"], i * 4 + n + 2)
                for j in range(CH):
                    last = nc.tensor.transpose(c.bank[:, 2, P * j:P * (j + 1)], act_out[:, 2, P * j:P * (j + 1)],
                                               c.ident[:])
                last.then_inc(s["vt_done"], 1)
                pe.wait_ge(s["sq_done"], i * 4 + n + 1)
                for g in range(2):
                    last = nc.tensor.matmul(c.bank[:, g, :], c.ones[:], sq[:, g, :], start=True, stop=True)
                last.then_inc(s["ssq_done"], 1)
            elif piece == 4:
                pe.wait_ge(s["v_kept"], i * 4 + n + 1)
                nc.tensor.matmul(c.bank[:, 2, :], sel[:], beta[:, cols], start=True, stop=True
                                 ).then_inc(s["beta_done"], 1)

        def pairs(pe, i, n, lv):
            pr = n % 2
            if lv:
                pe.wait_ge(s["upq"], i * 28 + 7 * n + lv)
                pe.wait_ge(s["upp"], i * 28 + 7 * n + lv)
                pe.wait_ge(s["bt_done"], i * 32 + 8 * n + lv)
            for ch in range(CH):
                right = halves_of(kqp[:, pr, :, P * ch:P * (ch + 1)], 1 << lv, 1)
                last = nc.tensor.matmul(c.bank[:, 4 + (lv + 1) % 2, P * ch:P * (ch + 1)], kq[:, pr, P * ch:P * (ch + 1)],
                                        right, start=True, stop=True)
            last.then_inc(s["ab_done"], 1)

        def core_pe(pe, i, n, front):
            pr = n % 2
            pe.wait_ge(s["kq_done"], i * 4 + n + 2)
            pe.wait_ge(s["og_done"], i * 4 + n + 2)
            for ch in range(CH):
                last = nc.tensor.matmul(c.bank[:, 4, P * ch:P * (ch + 1)], kq[:, pr, P * ch:P * (ch + 1)],
                                        qn[:, pr, P * ch:P * (ch + 1)], start=True, stop=True)
            last.then_inc(s["dg_done"], 1)
            pairs(pe, i, n, 0)
            pe.wait_ge(s["xadd"], i * 4 + n + 1)
            for lv in range(LEVELS):
                if lv + 1 < LEVELS:
                    pairs(pe, i, n, lv + 1)
                pe.wait_ge(s["ct_done"], i * 28 + 7 * n + lv + 1)
                if lv:
                    pe.wait_ge(s["tx_done"], i * 28 + 7 * n + lv)
                for ch in range(CH):
                    left = c.ident[:] if lv == 0 else tm[:, ch, :]
                    last = nc.tensor.matmul(c.bank[:, 6, 64 * ch:64 * ch + 64], ct[:, lv, ch, :],
                                            halves_of(left, 1 << lv, 0), start=True, stop=True)
                last.then_inc(s["y_done"], 1)
                front(lv)
                if lv:
                    pe.wait_ge(s["yk"], i * 24 + 6 * n + lv)
                    for ch in range(CH):
                        if lv + 1 < LEVELS:
                            nc.tensor.matmul(c.bank[:, 7, 64 * ch:64 * ch + 64], xm[:, ch, :],
                                             halves_of(ysb[:, lv, ch, :], 1 << lv, 0), start=True, stop=True)
                        last = nc.tensor.matmul(c.bank[:, 7, 256 + 64 * ch:320 + 64 * ch], ysb[:, lv, ch, :],
                                                halves_of(xm[:, ch, :], 1 << lv, 1), start=True, stop=True)
                    last.then_inc(s["d_done"], 1)
            pe.wait_ge(s["upq"], i * 28 + 7 * n + 7)
            pe.wait_ge(s["upp"], i * 28 + 7 * n + 7)
            pe.wait_ge(s["bt_done"], i * 32 + 8 * n + 7)
            for b in range(2):
                last = nc.tensor.matmul(c.bank[:, 4, 2 * P * b:2 * P * (b + 1)],
                                        kq[:, pr, 2 * P * b:2 * P * b + P],
                                        kqp[:, pr, :, 2 * P * b + P:2 * P * (b + 1)], start=True, stop=True)
            last.then_inc(s["x_done"], 1)
            pe.wait_ge(s["tx_done"], i * 28 + 7 * n + 7)
            pe.wait_ge(s["v_kept"], i * 4 + n + 1)
            pe.wait_ge(s["bt_done"], i * 32 + 8 * n + 8)
            for b in range(2):
                last = nc.tensor.matmul(c.bank[:, 5, P * b:P * (b + 1)], xm[:, 2 * b, :], vals[:, pr, 2 * b, :],
                                        start=True, stop=True)
            last.then_inc(s["u_done"], 1)
            pe.wait_ge(s["x_kept"], i * 4 + n + 1)
            pe.wait_ge(s["u_kept"], i * 8 + 2 * n + 1)
            for b in range(2):
                last = nc.tensor.matmul(c.bank[:, 6, P * b:P * (b + 1)], cross[:, b, 0, :], u[:, 2 * b, :],
                                        start=True, stop=True)
            last.then_inc(s["r_done"], 1)
            pe.wait_ge(s["rs_done"], i * 4 + n + 1)
            for b in range(2):
                last = nc.tensor.matmul(c.bank[:, 7, P * b:P * (b + 1)], xm[:, 2 * b + 1, :], rest[:, b, :],
                                        start=True, stop=True)
            last.then_inc(s["u_done"], 1)
            pe.wait_ge(s["u_kept"], i * 8 + 2 * n + 2)
            for b in range(2):
                nc.tensor.matmul(c.bank[:, 4, 2 * P * b:2 * P * b + P], u[:, 2 * b, :], bt[:, 2 * b, :],
                                 start=True, stop=True)
                o1 = c.bank[:, 4, 2 * P * b + P:2 * P * (b + 1)]
                nc.tensor.matmul(o1, u[:, 2 * b, :], cross[:, b, 1, :], start=True, stop=False)
                last = nc.tensor.matmul(o1, u[:, 2 * b + 1, :], bt[:, 2 * b + 1, :], start=False, stop=True)
            last.then_inc(s["o_done"], 1)
            pe.wait_ge(s["osq_done"], i * 4 + n + 1)
            nc.tensor.matmul(c.bank[:, 5, :], c.ones[:], osq[:], start=True, stop=True).then_inc(s["oss_done"], 1)
            pe.wait_ge(s["og_done"], i * 4 + n + 3)
            for ch in range(CH):
                last = nc.tensor.matmul(c.bank[:, 6 + ch // 2, D * (ch % 2):D * (ch % 2 + 1)],
                                        og[:, P * ch:P * (ch + 1)], wo[:], start=True, stop=True)
            last.then_inc(s["out_done"], 1)

        def segments(i, front, core):
            for piece in range(LEVELS):
                front(i, 0, piece)
            for n in range(NSEG):
                core(i, n, lambda piece: front(i, n + 1, piece) if n + 1 < NSEG else None)

        @block.tensor
        def _(pe):
            pe.wait_ge(s["const"], 32)
            pe.wait_ge(s["zeroed"], 2)
            pe.sem_inc(s["y_done"], 1)
            with nc.tensor.Fori(0, KH) as i:
                pe.wait_ge(s["w_loaded"], i * 96 + 96)
                segments(i, lambda *a: front_pe(pe, *a), lambda *a: core_pe(pe, *a))

        def front_act(act, i, n, piece):
            pr = n % 2
            if piece == 0:
                act.wait_ge(s["proj_done"], i * 4 + n + 1)
                nc.scalar.activation(raw[:, :, :, 3:], c.bank[:, 0:3, :].rearrange("p g (b t) -> p g b t", b=2),
                                     ACT.Copy).then_inc(s["raw_kept"], 1)
                act.wait_ge(s["g_done"], i * 4 + n + 1)
                nc.scalar.activation(z[:], c.bank[:, 3, :], ACT.Identity, bias=dt_bias[:, 0:1]
                                     ).then_inc(s["z_done"], 1)
                act.wait_ge(s["z_done"], i * 4 + n + 1)
                nc.scalar.activation(tail[:], z[:], ACT.Abs).then_inc(s["tail_done"], 1)
                act.wait_ge(s["tail_done"], i * 8 + 2 * n + 1)
                nc.scalar.activation(tail[:], tail[:], ACT.Exp, scale=-1.0).then_inc(s["tail_done"], 1)
            elif piece == 1:
                act.wait_ge(s["low_done"], i * 8 + 2 * n + 2)
                nc.scalar.activation(low[:], low[:], ACT.Ln, bias=1.0).then_inc(s["ln1_done"], 1)
            elif piece == 2:
                act.wait_ge(s["tap"], i * 16 + 4 * n + 4)
                act.wait_ge(s["kq_done"], i * 4 + n + 1)
                nc.scalar.activation(act_out[:], conv[:], ACT.Silu).then_inc(s["silu_done"], 1)
                act.wait_ge(s["silu_done"], i * 4 + n + 2)
                nc.scalar.activation(sq[:], act_out[:, 0:2, :], ACT.Square).then_inc(s["sq_done"], 1)
            elif piece == 3:
                act.wait_ge(s["sp_done"], i * 8 + 2 * n + 2)
                act.wait_ge(s["og_done"], i * 4 + n + 1)
                nc.scalar.activation(e[:, pr, 0:SEG], z[:], ACT.Exp, scale=decay[:, 0:1]).then_inc(s["a_done"], 1)
                act.wait_ge(s["vt_done"], i * 4 + n + 1)
                nc.scalar.activation(vals[:, pr].rearrange("p c v -> p (c v)"), c.bank[:, 2, :], ACT.Copy
                                     ).then_inc(s["v_kept"], 1)
                act.wait_ge(s["gt_done"], i * 4 + n + 1)
                nc.scalar.activation(sgate[:, pr, :], c.bank[:, 3, :], ACT.Sigmoid).then_inc(s["sg_done"], 1)
            elif piece == 4:
                act.wait_ge(s["ssq_done"], i * 4 + n + 1)
                nc.scalar.activation(rn[:], c.bank[:, 0:2, :], ACT.Ln, bias=eps6[:, 0:1]).then_inc(s["ln_done"], 1)
                act.wait_ge(s["ln_done"], i * 4 + n + 2)
                nc.scalar.activation(rn[:], rn[:], ACT.Exp, scale=-0.5).then_inc(s["rn_done"], 1)

        def core_act(act, i, n, front):
            for lv in range(LEVELS):
                if lv:
                    act.wait_ge(s["y_done"], i * 28 + 7 * n + lv + 2)
                    nc.scalar.activation(halves_of(ysb[:, lv], 1 << lv, 0),
                                         c.bank[:, 6, 0:256].rearrange("p (c g m) -> p c g m", c=CH, m=1 << lv),
                                         ACT.Copy).then_inc(s["yk"], 1)
                front(lv)
            act.wait_ge(s["x_done"], i * 4 + n + 1)
            nc.scalar.activation(cross[:].rearrange("p b g t -> p (b g t)"), c.bank[:, 4, :], ACT.Copy
                                 ).then_inc(s["x_kept"], 1)
            for half in range(2):
                act.wait_ge(s["u_done"], i * 8 + 2 * n + half + 1)
                nc.scalar.activation(u[:, half:CH:2, :],
                                     c.bank[:, 5 + 2 * half, 0:256].rearrange("p (b v) -> p b v", b=2), ACT.Copy
                                     ).then_inc(s["u_kept"], 1)
            act.wait_ge(s["o_done"], i * 4 + n + 1)
            nc.scalar.activation(osq[:], c.bank[:, 4, :], ACT.Square).then_inc(s["osq_done"], 1)
            act.wait_ge(s["oss_done"], i * 4 + n + 1)
            nc.scalar.activation(orn[:], c.bank[:, 5, :], ACT.Ln, scale=1.0 / KW, bias=eps5[:, 0:1]
                                 ).then_inc(s["or_ln"], 1)
            act.wait_ge(s["or_ln"], i * 4 + n + 1)
            nc.scalar.activation(orn[:], orn[:], ACT.Exp, scale=-0.5).then_inc(s["or_done"], 1)

        @block.scalar
        def _(act):
            act.sem_inc(s["ln_done"], 1)
            act.sem_inc(s["sg_done"], 1)
            act.sem_inc(s["silu_done"], 1)
            act.wait_ge(s["zeroed"], 2)
            with nc.scalar.Fori(0, KH) as i:
                act.wait_ge(s["w_loaded"], i * 96 + 96)
                act.wait_ge(s["decay_set"], i + 1)
                segments(i, lambda *a: front_act(act, *a), lambda *a: core_act(act, *a))

        def front_dve(dve, i, n, piece):
            pr = n % 2
            if piece == 0:
                dve.wait_ge(s["raw_kept"], i * 4 + n + 1)
                dve.wait_ge(s["silu_done"], i * 4 + n + 1)
            for step in {0: (0, 1), 1: (2, 3)}.get(piece, ()):
                tap = 3 - step
                if step:
                    dve.wait_ge(s["tap"], i * 16 + 4 * n + step)
                for g in range(3):
                    out = conv[:, g, :].rearrange("p (b t) -> p b t", b=2)
                    src = raw[:, g, :, tap:tap + T]
                    if step == 0:
                        last = nc.vector.tensor_scalar(out, src, taps[:, g, 3:4], taps[:, g, 4:5], ALU.mult, ALU.add)
                    else:
                        last = nc.vector.scalar_tensor_tensor(out, src, taps[:, g, tap:tap + 1], out, ALU.mult,
                                                              ALU.add)
                last.then_inc(s["tap"], 1)
            if piece == 1:
                dve.wait_ge(s["tail_done"], i * 8 + 2 * n + 2)
                nc.vector.tensor_scalar(low[:], tail[:], 1.0, 1.0, ALU.add, ALU.subtract).then_inc(s["low_done"], 1)
                dve.wait_ge(s["low_done"], i * 8 + 2 * n + 1)
                nc.vector.tensor_tensor(tail[:], tail[:], low[:], ALU.subtract).then_inc(s["low_done"], 1)
            if piece == 2:
                dve.wait_ge(s["ln1_done"], i * 4 + n + 1)
                nc.vector.scalar_tensor_tensor(z[:], z[:], 0.0, low[:], ALU.max, ALU.add).then_inc(s["sp_done"], 1)
                dve.wait_ge(s["sp_done"], i * 8 + 2 * n + 1)
                nc.vector.tensor_tensor(z[:], z[:], tail[:], ALU.add).then_inc(s["sp_done"], 1)
            if piece == 5:
                dve.wait_ge(s["rn_done"], i * 4 + n + 1)
                nc.vector.tensor_tensor(kn[:], act_out[:, 1, :], rn[:, 1, :], ALU.mult)
                nc.vector.scalar_tensor_tensor(qn[:, pr, :], act_out[:, 0, :], KW ** -0.5, rn[:, 0, :], ALU.mult,
                                               ALU.mult).then_inc(s["kn_done"], 1)
                dve.wait_ge(s["kn_done"], i * 4 + n + 1)
                dve.wait_ge(s["a_done"], i * 4 + n + 1)
                nc.vector.tensor_tensor(kqp[:, pr, 0, :], kn[:], e[:, pr, 0:SEG], ALU.mult)
                nc.vector.tensor_tensor(kqp[:, pr, 1, :], qn[:, pr, :], e[:, pr, 0:SEG], ALU.mult)
                dve.wait_ge(s["beta_done"], i * 4 + n + 1)
                nc.vector.tensor_tensor(kq[:, pr, :], kn[:], c.bank[:, 2, :], ALU.mult).then_inc(s["kq_done"], 1)

        def level_dve(dve, i, n, lv):
            pr, m = n % 2, 1 << lv
            dve.wait_ge(s["bt_done"], i * 32 + 8 * n + lv + 1)
            dve.wait_ge(s["ab_done"], i * 28 + 7 * n + lv + 1)
            ab = c.bank[:, 4 + (lv + 1) % 2, :].rearrange("p (c two g m) -> p c two g m", two=2, c=CH, m=m)
            mask = masks[:, lv, :].unsqueeze(1).broadcast_to([P, CH, 64]).rearrange("p c (g m) -> p c g m", m=m)
            mask_i = masks_i[:, lv, :].unsqueeze(1).broadcast_to([P, CH, 64]).rearrange("p c (g m) -> p c g m", m=m)
            nc.vector.tensor_tensor(halves_of(ct[:, lv], m, 1), ab[:, :, 0], mask, ALU.mult).then_inc(s["ct_done"], 1)
            nc.vector.copy_predicated(halves_of(bt[:], m, 1), mask_i, ab[:, :, 1]).then_inc(s["bt_done"], 1)
            if lv:
                dve.wait_ge(s["e_done"], i * 24 + 6 * n + lv)
                dve.wait_ge(s["upq"], i * 28 + 7 * n + lv)
            g = SEG >> (lv + 1)
            pairs_e = e[:, pr, e_at[lv]:e_at[lv + 1]].rearrange("p (g two) -> p g two", two=2)
            left = halves_of(kq[:, pr, :], m, 0)
            nc.vector.tensor_tensor(left, left, pairs_e[:, :, 1:2].broadcast_to([P, g, m]), ALU.mult
                                    ).then_inc(s["upq"], 1)
            if lv + 1 < LEVELS:
                nc.vector.tensor_tensor(e[:, pr, e_at[lv + 1]:e_at[lv + 1] + g], pairs_e[:, :, 0], pairs_e[:, :, 1],
                                        ALU.mult).then_inc(s["e_done"], 1)

        def inverse_dve(dve, i, n, lv):
            m = 1 << lv
            eye = c.ident[:].unsqueeze(1).broadcast_to([P, CH, P])
            if lv == 0:
                dve.wait_ge(s["ct_done"], i * 28 + 7 * n + 1)
                nc.vector.tensor_tensor(xm[:], eye, ct[:, 0], ALU.subtract)
                dve.wait_ge(s["t_init"], i * 4 + n + 1)
                dve.wait_ge(s["y_done"], i * 28 + 7 * n + 2)
                left = halves_of(tm[:], m, 0)
                y = c.bank[:, 6, 0:256].rearrange("p (c g m) -> p c g m", c=CH, m=m)
                nc.vector.tensor_tensor(left, left, y, ALU.subtract).then_inc(s["tx_done"], 1)
                return
            dve.wait_ge(s["tx_done"], i * 28 + 7 * n + lv)
            dve.wait_ge(s["d_done"], i * 24 + 6 * n + lv)
            dt_, dx = (c.bank[:, 7, 256 * k:256 * (k + 1)].rearrange("p (c g m) -> p c g m", c=CH, m=m)
                       for k in range(2))
            if lv + 1 < LEVELS:
                left = halves_of(tm[:], m, 0)
                nc.vector.tensor_tensor(left, left, dt_, ALU.subtract)
            right = halves_of(xm[:], m, 1)
            nc.vector.tensor_tensor(right, right, dx, ALU.subtract).then_inc(s["tx_done"], 1)

        def core_dve(dve, i, n, front):
            pr = n % 2
            dve.wait_ge(s["dg_done"], i * 4 + n + 1)
            nc.vector.tensor_tensor(bt[:], c.bank[:, 4, :].rearrange("p (c t) -> p c t", c=CH),
                                    c.ident[:].unsqueeze(1).broadcast_to([P, CH, P]), ALU.mult
                                    ).then_inc(s["bt_done"], 1)
            level_dve(dve, i, n, 0)
            for lv in range(LEVELS):
                if lv + 1 < LEVELS:
                    level_dve(dve, i, n, lv + 1)
                inverse_dve(dve, i, n, lv)
                front(lv)
            dve.wait_ge(s["r_done"], i * 4 + n + 1)
            nc.vector.tensor_tensor(rest[:], vals[:, pr, 1:CH:2, :],
                                    c.bank[:, 6, 0:256].rearrange("p (b v) -> p b v", b=2), ALU.subtract
                                    ).then_inc(s["rs_done"], 1)
            dve.wait_ge(s["or_done"], i * 4 + n + 1)
            nc.vector.tensor_tensor(og[:], c.bank[:, 4, :], orn[:], ALU.mult).then_inc(s["og_mul"], 1)
            dve.wait_ge(s["og_mul"], i * 4 + n + 1)
            dve.wait_ge(s["sg_done"], i * 4 + n + 2)
            nc.vector.scalar_tensor_tensor(og[:], og[:], o_norm[:, 0:1], sgate[:, pr, :], ALU.mult, ALU.mult
                                           ).then_inc(s["og_done"], 1)
            dve.wait_ge(s["out_done"], i * 4 + n + 1)
            x = c.x_tok[:, 4 * n:4 * n + 4, :].rearrange("p t d -> p (t d)")
            nc.vector.tensor_tensor(x, x, c.bank[:, 6:8, :].rearrange("p k n -> p (k n)"), ALU.add
                                    ).then_inc(s["xadd"], 1)

        @block.vector
        def _(dve):
            dve.sem_inc(s["kq_done"], 1)
            dve.sem_inc(s["og_done"], 2)
            dve.sem_inc(s["xadd"], 1)
            nc.vector.memset(eps6[:], 1e-6)
            nc.vector.memset(eps5[:], 1e-5)
            nc.vector.memset(raw[:, :, :, 0:3], 0.0)
            nc.vector.memset(ct[:], 0.0)
            nc.vector.memset(ysb[:], 0.0).then_inc(s["zeroed"], 1)
            dve.wait_ge(s["const"], 32)
            nc.vector.tensor_copy(masks_i[:], masks[:]).then_inc(s["zeroed"], 1)
            dve.wait_ge(s["zeroed"], 2)
            with nc.vector.Fori(0, KH) as i:
                dve.wait_ge(s["w_loaded"], i * 96 + 96)
                nc.vector.tensor_copy(decay[:], neg_a[:, bass.ds(i, 1)]).then_inc(s["decay_set"], 1)
                segments(i, lambda *a: front_dve(dve, *a), lambda *a: core_dve(dve, *a))

        @block.gpsimd
        def _(pool):
            def core(i, n, front):
                pr = n % 2
                pool.wait_ge(s["y_done"], i * 28 + 7 * n + 1)
                nc.gpsimd.tensor_tensor(tm[:], c.ident[:].unsqueeze(1).broadcast_to([P, CH, P]),
                                        c.ident[:].unsqueeze(1).broadcast_to([P, CH, P]), ALU.mult
                                        ).then_inc(s["t_init"], 1)
                for lv in range(LEVELS):
                    m = 1 << lv
                    if lv:
                        pool.wait_ge(s["e_done"], i * 24 + 6 * n + lv)
                    pool.wait_ge(s["ab_done"], i * 28 + 7 * n + lv + 1)
                    g = SEG >> (lv + 1)
                    factor = e[:, pr, e_at[lv]:e_at[lv + 1]].rearrange("p (g two) -> p g two", two=2)[:, :, 0:1]
                    for k in range(2):
                        right = halves_of(kqp[:, pr, k, :], m, 1)
                        last = nc.gpsimd.tensor_tensor(right, right, factor.broadcast_to([P, g, m]), ALU.mult)
                    last.then_inc(s["upp"], 1)

            with nc.gpsimd.Fori(0, KH) as i:
                for n in range(NSEG):
                    core(i, n, None)


def host_layout(a):
    f = {}

    def cols(m):
        m = np.asarray(m)
        return np.ascontiguousarray(m.reshape(m.shape[0] // P, P, m.shape[1]).transpose(1, 0, 2))

    x = np.asarray(a["x"])
    f["x_tok"] = x.reshape(NT, P, D).transpose(1, 0, 2)
    f["x_t"] = x.reshape(TOK, KD, P).transpose(2, 1, 0)
    f["ident"] = np.eye(P, dtype=np.float32)
    L = {k[8:]: np.asarray(v) for k, v in a.items() if k.startswith("L0_attn_")}
    f["ssm_dt_lam"] = np.stack([cols(L["Wdt"].T), cols(L["Wlam"].T)], axis=2)
    f["ssm_A_log"] = L["A_log"].reshape(SH, 1)
    f["ssm_x"] = cols(L["Wx"].T)
    f["ssm_z"] = cols(L["Wz"].T)
    f["ssm_out"] = cols(L["Wout"].T)

    def pair_rows(m):
        return m.reshape(PAIRS, 2, 64, 2, D).transpose(0, 3, 1, 2, 4).reshape(PAIRS, 2, P, D)

    rows = np.concatenate([L["Wth"].reshape(PAIRS, 1, P, D), pair_rows(L["WB"]), pair_rows(L["WC"])], axis=1)
    f["ssm_pair"] = rows.reshape(PAIRS, 5, P, KD, P).transpose(0, 4, 3, 1, 2)
    sel = np.zeros((PAIRS, SH, 3, P), np.float32)
    for i in range(PAIRS):
        sel[i, 2 * i, 0, :64] = sel[i, 2 * i + 1, 0, 64:] = 1
        sel[i, 2 * i, 1, :] = sel[i, 2 * i + 1, 2, :] = 1
    f["ssm_sel"] = sel
    b = [L[k].reshape(PAIRS, 2, 64, 2).transpose(0, 3, 1, 2).reshape(PAIRS, 2, P) for k in ("B_bias", "C_bias")]
    f["ssm_bias"] = np.concatenate(b, axis=1).transpose(0, 2, 1)
    f["ssm_norm_w"] = np.stack([np.tile(L[k][j::2], 2) for k in ("Bn_w", "Cn_w") for j in range(2)], axis=1)
    f["ssm_above"] = np.eye(P, P + 1, 1, dtype=np.float32)
    f["ssm_halves"] = np.kron(np.eye(2, dtype=np.float32), np.ones((64, 64), np.float32))
    ctx_t = np.asarray(a["ctx_1024"]).reshape(B * S2, DC).T
    mask = np.asarray(a["mask_BxS2_bf1"]).view(np.uint8)
    for tag, name in (("xm_", "L0_xattn_"), ("xn_", "L1_xattn_")):
        L = {k[len(name):]: np.asarray(v) for k, v in a.items() if k.startswith(name)}
        f[tag + "ctx"] = ctx_t
        f[tag + "q"] = cols(L["Wq"])
        f[tag + "o"] = cols(L["Wo"])
        f[tag + "k"] = L["Wk"]
        f[tag + "v"] = L["Wv"].reshape(DC, 1, -1) if tag == "xm_" else (
            L["Wv"].reshape(DC, XP, 2, XD).transpose(0, 2, 1, 3).reshape(DC, 2, XP * XD))
    f["xn_g"] = np.stack([L["gk"], L["gq"]], axis=1)
    f["xm_mask_row"] = mask.reshape(B * S2)
    f["xm_mask_col"] = np.concatenate([mask.T, mask.T])
    L = {k[7:]: np.asarray(v) for k, v in a.items() if k.startswith("L0_ffn_")}
    f["had_rows"] = np.concatenate([L[k].reshape(HID0 // P, P, D) for k in ("W_gate", "W_up")]).transpose(1, 0, 2)
    f["had_down"] = L["W_down"].reshape(KD, P, HID0).transpose(1, 0, 2)
    f["had_su_in"] = L["SU_ug"].reshape(KD, P).T
    f["had_su_out"] = L["SU_dp"].reshape(HID0 // P, P).T
    f["had_down_scale"] = L["Wscale_dp"].reshape(KD, P).T
    f["had_scales"] = L["Wscale_ug"].reshape(2, HID0 // P, P)[::-1].transpose(2, 0, 1)
    L = {k[7:]: np.asarray(v) for k, v in a.items() if k.startswith("L1_ffn_")}
    f["deq_in"] = np.stack([cols(L["wq_gate"].T), cols(L["wq_up"].T)], axis=2)
    f["deq_out"] = L["wq_down"].T
    f["deq_s_down"] = L["s_down"]
    f["deq_s_gate"] = L["s_gate"].reshape(HID1, 1)
    f["deq_s_up"] = L["s_up"].reshape(HID1, 1)
    L = {k[8:]: np.asarray(v) for k, v in a.items() if k.startswith("L1_attn_")}

    def by_head(m):
        return m.reshape(m.shape[0], KH, KW).transpose(1, 0, 2)

    f["kda_fg"] = np.stack([cols(L["Wfa"]), cols(L["Wga"])], axis=2)
    f["kda_b"] = cols(L["Wb"])
    f["kda_A_log"] = L["A_log"]
    f["kda_o_norm"] = L["o_norm_w"].reshape(KW, 1)
    f["kda_qkv"] = np.stack([by_head(L[k]) for k in ("Wq", "Wk", "Wv")], axis=2).reshape(
        KH, KD, P, 3, KW).transpose(0, 2, 1, 3, 4)
    f["kda_fg2"] = np.stack([by_head(L["Wfb"]), by_head(L["Wgb"])], axis=2)
    f["kda_o"] = L["Wo"].reshape(KH, KW, D)
    f["kda_taps"] = np.stack([np.concatenate([L[f"conv_{g}_w"], L[f"conv_{g}_b"][:, None]], axis=1).reshape(
        KH, KW, 5) for g in "qkv"], axis=2)
    f["kda_dt_bias"] = L["dt_bias"].reshape(KH, KW, 1)
    f["kda_sel"] = np.repeat(np.eye(KH, dtype=np.float32)[:, :, None], P, axis=2)
    masks = np.zeros((P, LEVELS, P // 2), np.float32)
    for lv in range(LEVELS):
        m = 1 << lv
        right = np.arange(P).reshape(-1, 2, m)[:, 1].ravel()
        rows = np.arange(P)
        masks[:, lv] = (rows[:, None] // (2 * m) == right[None, :] // (2 * m)) & ((rows[:, None] // m) % 2 == 0)
    f["kda_masks"] = masks
    return {k: np.ascontiguousarray(v) for k, v in f.items()}


def part(d, prefix):
    return {k[len(prefix):]: v for k, v in d.items() if k.startswith(prefix)}


def program(nc, d, out_d, only=None):
    with ExitStack() as ctx:
        c = Core(nc, ctx)
        load_start(c, d["x_tok"], d["x_t"], d["ident"])
        layers = [
            (ssm, "ssm_"),
            (lambda c, w: cross_attention(c, w, False), "xm_"),
            (hadamard_ffn, "had_"),
            (kda, "kda_"),
            (lambda c, w: cross_attention(c, w, True), "xn_"),
            (dequant_ffn, "deq_"),
        ]
        for n, (layer, prefix) in enumerate(layers):
            if only is None or n == only:
                layer(c, part(d, prefix))
                last = len(layers) - 1 if only is None else only
                layer_norm(c, f"norm{n}", out_d if n == last else None)
                if n != last:
                    c.release_sems()
        c.sems.close()


def kernel(**inputs):
    from concourse import bacc
    from concourse.bass_utils import run_bass_kernel_spmd

    nc = bacc.Bacc("TRN2", target_bir_lowering=False, num_devices=1)
    arrays = host_layout(inputs)
    d = {k: nc.dram_tensor("in_" + k, v.shape, mybir.dt.from_np(v.dtype), kind="ExternalInput").ap()
         for k, v in arrays.items()}
    out = nc.dram_tensor("out_x", (P, NT, D), F32, kind="ExternalOutput").ap()
    program(nc, d, out)
    r = run_bass_kernel_spmd(nc, [{"in_" + k: v for k, v in arrays.items()}], core_ids=[0])
    return np.asarray(r.results[0]["out_x"]).transpose(1, 0, 2).reshape(B, T, D)
```

```python
from contextlib import ExitStack

import numpy as np

import concourse.bass as bass
from concourse import mybir

F32 = mybir.dt.float32
I32 = mybir.dt.int32
U8 = mybir.dt.uint8
ALU = mybir.AluOpType
ACT = mybir.ActivationFunctionType
AX = mybir.AxisListType

P = 128
B, T, D = 8, 256, 256
TOK = B * T
NT = TOK // P
KD = D // P
SEG = 512
NSEG = TOK // SEG
S2, DC = 64, 128
PI = 3.1415925
HALF_PI = 1.5707963267948966


class Core:

    def __init__(self, nc, ctx):
        self.nc, self.ctx = nc, ctx
        self.held, self.sems = [], ExitStack()
        self.x_tok = self.sbuf("x_tok", [P, NT, D])
        self.x_t = self.sbuf("x_t", [P, KD, TOK])
        self.ident = self.sbuf("ident", [P, P])
        self.ones = self.sbuf("ones", [P, P])
        self.bank = ctx.enter_context(nc.psum_tensor("bank", [P, 8, 512], F32))

    def sbuf(self, name, shape, dt=F32, ctx=None):
        return (ctx or self.ctx).enter_context(self.nc.sbuf_tensor(name, shape, dt))

    def sem(self, name):
        self.held.append(self.sems.enter_context(self.nc.semaphore(name)))
        return self.held[-1]

    def release_sems(self):
        with self.nc.Block() as block:

            @block.sync
            def _(sp):
                for held in self.held:
                    sp.sem_clear(held)

        self.sems.close()
        self.held, self.sems = [], ExitStack()


def load_start(c, x_tok_d, x_t_d, ident_d):
    nc = c.nc
    loaded = c.sem("start_loaded")
    with nc.Block() as block:

        @block.sync
        def _(sp):
            sp.dma_start(c.x_tok[:], x_tok_d).then_inc(loaded, 16)
            sp.dma_start(c.x_t[:], x_t_d).then_inc(loaded, 16)
            sp.dma_start(c.ident[:], ident_d).then_inc(loaded, 16)
            sp.wait_ge(loaded, 48)

        @block.vector
        def _(dve):
            nc.vector.memset(c.ones[:], 1.0)


def layer_norm(c, tag, out_d=None):
    nc = c.nc
    own = ExitStack()
    stats = c.sbuf(tag + "_stats", [P, NT, 6], ctx=own)
    mean_var = c.sbuf(tag + "_mean_var", [P, NT, 2], ctx=own)
    std = c.sbuf(tag + "_std", [P, NT], ctx=own)
    rstd = c.sbuf(tag + "_rstd", [P, NT], ctx=own)
    eps = c.sbuf(tag + "_eps", [P, 1], ctx=own)
    measured, rooted, scaled, turned, copied, stored = (
        c.sem(f"{tag}_{n}") for n in ("measured", "rooted", "scaled", "turned", "copied", "stored"))
    groups = NT // 4 * KD
    with own, nc.Block() as block:

        @block.vector
        def _(dve):
            nc.vector.memset(eps[:], 1e-5).then_inc(measured, 1)
            for t in range(NT):
                nc.vector.bn_stats(stats[:, t, :], c.x_tok[:, t, :]).then_inc(measured, 1)
            for t in range(NT):
                dve.wait_ge(measured, 2 + t)
                nc.vector.bn_aggr(mean_var[:, t, :], stats[:, t, :]).then_inc(measured, 1)
            dve.wait_ge(rooted, 1)
            nc.vector.reciprocal(rstd[:], std[:]).then_inc(rooted, 1)
            dve.wait_ge(rooted, 2)
            for t in range(NT):
                nc.vector.tensor_scalar(c.x_tok[:, t, :], c.x_tok[:, t, :], mean_var[:, t, 0:1],
                                        rstd[:, t:t + 1], ALU.subtract, ALU.mult).then_inc(scaled, 1)

        @block.scalar
        def _(act):
            act.wait_ge(measured, 1 + 2 * NT)
            nc.scalar.activation(std[:], mean_var[:, :, 1], ACT.Sqrt, bias=eps[:, 0:1]).then_inc(rooted, 1)
            if out_d is None:
                for g in range(groups):
                    q, k = divmod(g, KD)
                    act.wait_ge(turned, g + 1)
                    nc.scalar.activation(c.x_t[:, k, SEG * q:SEG * (q + 1)], c.bank[:, g % 4, :],
                                         ACT.Copy).then_inc(copied, 1)

        if out_d is None:

            @block.tensor
            def _(pe):
                for g in range(groups):
                    q, k = divmod(g, KD)
                    pe.wait_ge(scaled, 4 * (q + 1))
                    if g >= 4:
                        pe.wait_ge(copied, g - 3)
                    for j in range(4):
                        last = nc.tensor.transpose(c.bank[:, g % 4, P * j:P * (j + 1)],
                                                   c.x_tok[:, 4 * q + j, P * k:P * (k + 1)], c.ident[:])
                    last.then_inc(turned, 1)
        else:

            @block.sync
            def _(sp):
                for q in range(4):
                    sp.wait_ge(scaled, 4 * (q + 1))
                    sp.dma_start(out_d[:, 4 * q:4 * q + 4, :], c.x_tok[:, 4 * q:4 * q + 4, :]).then_inc(stored, 16)
                sp.wait_ge(stored, 64)



SH, SN, SP_ = 64, 128, 8
DIN = SH * SP_
PAIRS = SH // 2
INV_2PI = 0.15915494309189535
ROUND = 12582912.0
DEC = T + P
TWO_PI_HI, TWO_PI_LO = 6.28125, 0.0019353071795864769


def ssm(c, w):
    nc = c.nc
    dt_d = nc.dram_tensor("ssm_dt_rows", (SH, TOK), F32).ap()
    alpha_d = nc.dram_tensor("ssm_alpha_rows", (SH, B, DEC), F32).ap()
    own = ExitStack()
    xh = c.sbuf("xh", [P, NT, DIN], ctx=own)
    y_tok = c.sbuf("y_tok", [P, NT, DIN], ctx=own)
    with own:
        tables = ExitStack()
        beta_tok = c.sbuf("beta_tok", [P, SH, NT], ctx=tables)
        gamma_tok = c.sbuf("gamma_tok", [P, SH, NT], ctx=tables)
        with tables:
            ssm_gates(c, w, xh, dt_d, alpha_d, beta_tok, gamma_tok)
            ssm_heads(c, w, xh, y_tok, dt_d, alpha_d, beta_tok, gamma_tok)
        ssm_output(c, w, y_tok)


def ssm_gates(c, w, xh, dt_d, alpha_d, beta_tok, gamma_tok):
    nc = c.nc
    own = ExitStack()
    dt_t = c.sbuf("dt_t", [SH, TOK], ctx=own)
    alpha_x = c.sbuf("alpha_x", [SH, B, DEC], ctx=own)
    wx = c.sbuf("wx", [P, KD, DIN], ctx=own)
    wdl = c.sbuf("wdl", [P, KD, 2, SH], ctx=own)
    a_log = c.sbuf("a_log", [SH, 1], ctx=own)
    neg_a = c.sbuf("neg_a", [SH, 1], ctx=own)
    tail = c.sbuf("softplus_tail", [SH, SEG], ctx=own)
    low = c.sbuf("softplus_low", [SH, SEG], ctx=own)
    lam = c.sbuf("lam", [SH, SEG], ctx=own)
    rest = c.sbuf("rest", [SH, SEG], ctx=own)
    gamma_t = c.sbuf("gamma_t", [SH, TOK], ctx=own)
    beta_t = c.sbuf("beta_t", [SH, TOK], ctx=own)
    loaded, saved, x_done, x_kept, dl_done, soft, low_done, dt_done, lam_done, gk_done, turned, kept = (
        c.sem("gates_" + n) for n in ("loaded", "saved", "x_done", "x_kept", "dl_done", "soft", "low_done", "dt_done", "lam_done",
                                      "gk_done", "turned", "kept"))
    with own, nc.Block() as block:

        @block.sync
        def _(sp):
            sp.dma_start(wdl[:], w["dt_lam"]).then_inc(loaded, 16)
            sp.dma_start(a_log[:], w["A_log"]).then_inc(loaded, 16)
            sp.dma_start(wx[:], w["x"]).then_inc(loaded, 16)
            sp.wait_ge(gk_done, 4 * NSEG + 1)
            sp.dma_start(dt_d, dt_t[:]).then_inc(saved, 16)
            sp.dma_start(alpha_d, alpha_x[:]).then_inc(saved, 16)
            sp.wait_ge(saved, 32)

        @block.tensor
        def _(pe):
            pe.wait_ge(loaded, 48)
            for q in range(NSEG):
                if q:
                    pe.wait_ge(lam_done, 2 * q)
                    pe.wait_ge(dt_done, 2 * q)
                for g in range(2):
                    for k in range(KD):
                        last = nc.tensor.matmul(c.bank[0:SH, 4 + g, :], wdl[:, k, g, :],
                                                c.x_t[:, k, SEG * q:SEG * (q + 1)],
                                                start=k == 0, stop=k == KD - 1)
                last.then_inc(dl_done, 1)
            for t in range(NT):
                if t >= 4:
                    pe.wait_ge(x_kept, t - 3)
                for k in range(KD):
                    last = nc.tensor.matmul(c.bank[:, t % 4, :], c.x_t[:, k, P * t:P * (t + 1)], wx[:, k, :],
                                            start=k == 0, stop=k == KD - 1)
                last.then_inc(x_done, 1)
            for g, source in enumerate((beta_t, gamma_t)):
                for half in range(2):
                    pe.wait_ge(gk_done, 4 * NSEG + 1)
                    for t in range(8 * half, 8 * half + 8):
                        last = nc.tensor.transpose(c.bank[:, 4 + 2 * g + half, SH * (t % 8):SH * (t % 8 + 1)],
                                                   source[:, P * t:P * (t + 1)], c.ident[0:SH, 0:SH])
                    last.then_inc(turned, 1)

        @block.scalar
        def _(act):
            act.wait_ge(loaded, 48)
            nc.scalar.activation(neg_a[:], a_log[:], ACT.Exp).then_inc(soft, 1)
            for q in range(NSEG):
                cols = slice(SEG * q, SEG * (q + 1))
                act.wait_ge(dl_done, q + 1)
                if q:
                    act.wait_ge(gk_done, 4 * q + 1)
                nc.scalar.activation(tail[:], c.bank[0:SH, 4, :], ACT.Abs).then_inc(soft, 1)
                act.wait_ge(soft, 4 * q + 2)
                nc.scalar.activation(tail[:], tail[:], ACT.Exp, scale=-1.0).then_inc(soft, 1)
                act.wait_ge(low_done, 2 * q + 2)
                nc.scalar.activation(low[:], low[:], ACT.Ln, bias=1.0).then_inc(soft, 1)
                nc.scalar.activation(lam[:], c.bank[0:SH, 5, :], ACT.Sigmoid).then_inc(lam_done, 1)
                nc.scalar.activation(rest[:], c.bank[0:SH, 5, :], ACT.Sigmoid, scale=-1.0).then_inc(lam_done, 1)
                act.wait_ge(dt_done, 2 * q + 2)
                act.wait_ge(gk_done, 1)
                nc.scalar.activation(alpha_x[:, 2 * q:2 * q + 2, 0:T],
                                     dt_t[:, cols].rearrange("h (b t) -> h b t", t=T), ACT.Exp,
                                     scale=neg_a[:, 0:1]).then_inc(soft, 1)
            for t in range(NT):
                act.wait_ge(x_done, t + 1)
                nc.scalar.activation(xh[:, t, :], c.bank[:, t % 4, :], ACT.Copy).then_inc(x_kept, 1)
            for j in range(4):
                act.wait_ge(turned, j + 1)
                target = (beta_tok, gamma_tok)[j // 2]
                nc.scalar.activation(target[:, :, 8 * (j % 2):8 * (j % 2) + 8],
                                     c.bank[:, 4 + j, :].rearrange("p (t h) -> p h t", h=SH),
                                     ACT.Copy).then_inc(kept, 1)

        @block.vector
        def _(dve):
            for q in range(NSEG):
                cols = slice(SEG * q, SEG * (q + 1))
                dve.wait_ge(soft, 4 * q + 3)
                nc.vector.tensor_scalar(low[:], tail[:], 1.0, 1.0, ALU.add, ALU.subtract).then_inc(low_done, 1)
                dve.wait_ge(low_done, 2 * q + 1)
                nc.vector.tensor_tensor(tail[:], tail[:], low[:], ALU.subtract).then_inc(low_done, 1)
                dve.wait_ge(low_done, 2 * q + 2)
                dve.wait_ge(soft, 4 * q + 4)
                nc.vector.scalar_tensor_tensor(dt_t[:, cols], c.bank[0:SH, 4, :], 0.0, low[:], ALU.max,
                                               ALU.add).then_inc(dt_done, 1)
                dve.wait_ge(dt_done, 2 * q + 1)
                nc.vector.tensor_tensor(dt_t[:, cols], dt_t[:, cols], tail[:], ALU.add).then_inc(dt_done, 1)
                if q == 0:
                    nc.vector.tensor_scalar(neg_a[:], neg_a[:], -1.0, None, ALU.mult).then_inc(gk_done, 1)
                dve.wait_ge(dt_done, 2 * q + 2)
                dve.wait_ge(lam_done, 2 * q + 2)
                nc.vector.tensor_tensor(gamma_t[:, cols], lam[:], dt_t[:, cols], ALU.mult).then_inc(gk_done, 1)
                nc.vector.tensor_tensor(rest[:], rest[:], dt_t[:, cols], ALU.mult).then_inc(gk_done, 1)
                dve.wait_ge(gk_done, 4 * q + 3)
                dve.wait_ge(soft, 4 * q + 5)
                r3 = rest[:, :].rearrange("h (b t) -> h b t", t=T)
                alpha = alpha_x[:, 2 * q:2 * q + 2, :]
                nc.vector.tensor_tensor(r3, r3, alpha[:, :, 0:T], ALU.mult).then_inc(gk_done, 1)
                dve.wait_ge(gk_done, 4 * q + 4)
                nc.vector.memset(alpha[:, :, 0:1], 0.0)
                nc.vector.memset(alpha[:, :, T:T + 1], 0.0)
                nc.vector.tensor_copy(alpha[:, :, T + 1:], alpha[:, :, P + 1:T])
                b3 = beta_t[:, cols].rearrange("h (b t) -> h b t", t=T)
                nc.vector.memset(b3[:, :, T - 1:T], 0.0)
                nc.vector.tensor_copy(b3[:, :, 0:T - 1], r3[:, :, 1:T]).then_inc(gk_done, 1)


def ssm_heads(c, w, xh, y_tok, dt_d, alpha_d, beta_tok, gamma_tok):
    nc = c.nc
    own = ExitStack()

    def sb(name, shape, dt=F32):
        return c.sbuf(name, shape, dt, ctx=own)

    w_pair = [sb(f"w_pair{e}", [P, KD, 5, P]) for e in range(2)]
    bias = sb("bc_bias", [P, PAIRS, 4])
    norm_w = sb("bc_norm_w", [P, 4])
    halves = sb("halves", [P, P])
    above = sb("above", [P, P + 1])
    diag = sb("diag", [P, P + 1])
    eps = sb("ssm_eps", [P, 1])
    half_pi = sb("ssm_half_pi", [P, 1])
    bet = sb("bet", [P, 2, 2, NT])
    gam = sb("gam", [P, 2, 2, NT])
    pair_bias = sb("pair_bias", [P, 2, 4])
    dts = sb("dts", [P, SEG])
    alphas = sb("alphas", [P, 2, 2, DEC])
    ang = sb("ang", [P, SEG])
    turns = sb("turns", [P, SEG])
    red = sb("red", [P, SEG])
    sn = sb("sn", [P, 2, SEG])
    cs = sb("cs", [P, 2, SEG])
    sq = sb("sq", [P, 4, SEG])
    rms = sb("rms", [P, 2, SEG])
    nbc = sb("nbc", [P, 4, SEG])
    pr = sb("pr", [P, 4, SEG])
    pq = sb("pool_products", [P, 2, SEG])
    rot = sb("rot", [P, 2, 2, SEG])
    start = sb("start", [P, 2, 2, 2, DEC])
    beside = sb("beside", [P, 2, 2, 2, P + 1])
    dec = sb("dec", [P, 2, 2, DEC])
    mix = sb("mix", [P, 4, DEC])
    names = ("const w_even w_odd dts_loaded al_loaded th_done b_done c_done sq_b sq_c ssq_b ssq_c ln_b ln_c r_b r_c "
             "ang_in ang_done red_k red_done trig cabs n_b n_c aff_b aff_c prod_v rot_v prod_p rot_p diag_done beta_done "
             "dec_done mix_done s_done y_done y_kept cols_kept start_done set ctr_k").split()
    s = {n: c.sem("ssm_" + n) for n in names}
    PASSES = PAIRS // 2 - 1
    alpha_rows = alpha_d.rearrange("(i h) r t -> i h r t", h=2)
    dt_rows = dt_d.rearrange("(i h) t -> i h t", h=2)
    with own, nc.Block() as block:

        def load_pair(sp, p, e):
            sp.dma_start(w_pair[e][:], w["pair"][bass.ds(p, 1)].rearrange("o p k j m -> p (o k) j m")
                         ).then_inc(s[("w_even", "w_odd")[e]], 16)

        def load_dt(sp, pair, n):
            for h in range(2):
                sp.dma_start(dts[64 * h:64 * h + 64, :], dt_rows[bass.ds(pair, 1), h, SEG * n:SEG * (n + 1)
                                                                 ].broadcast_to([64, SEG])
                             ).then_inc(s["dts_loaded"], 16)

        def load_alpha(sp, pair, n):
            for h in range(2):
                sp.dma_start(alphas[:, h], alpha_rows[bass.ds(pair, 1), h, 2 * n:2 * n + 2, :
                                                      ].broadcast_to([P, 2, DEC])
                             ).then_inc(s["al_loaded"], 16)

        @block.sync
        def _(sp):
            sp.dma_start(norm_w[:], w["norm_w"]).then_inc(s["const"], 16)
            sp.dma_start(halves[:], w["halves"]).then_inc(s["const"], 16)
            sp.dma_start(above[:], w["above"]).then_inc(s["const"], 16)
            sp.dma_start(bias[:], w["bias"]).then_inc(s["const"], 16)
            load_pair(sp, 0, 0)
            load_dt(sp, 0, 0)
            load_alpha(sp, 0, 0)
            load_pair(sp, 1, 1)

            def ahead(i, m, final):
                k = i * 8 + m + 1
                pair = i * 2 + (m + 1) // 4
                sp.wait_ge(s["ang_in"], k)
                load_dt(sp, pair, (m + 1) % 4)
                sp.wait_ge(s["dec_done"], k)
                load_alpha(sp, pair, (m + 1) % 4)
                if not final and m == 2:
                    sp.wait_ge(s["c_done"], i * 8 + 4)
                    load_pair(sp, i * 2 + 2, 0)
                if not final and m == 6:
                    sp.wait_ge(s["c_done"], i * 8 + 8)
                    load_pair(sp, i * 2 + 3, 1)

            with nc.sync.Fori(0, PASSES) as i:
                for m in range(8):
                    ahead(i, m, False)
            for m in range(7):
                ahead(PASSES, m, True)

        def project_angles(pe, n, k, e):
            pe.wait_ge(s["ln_b"], k + 1)
            for j in range(KD):
                last = nc.tensor.matmul(c.bank[:, 4, :], w_pair[e][:, j, 0, :],
                                        c.x_t[:, j, SEG * n:SEG * (n + 1)], start=j == 0, stop=j == 1)
            last.then_inc(s["th_done"], 1)

        def project(pe, n, k, e):
            x = [c.x_t[:, j, SEG * n:SEG * (n + 1)] for j in range(KD)]
            wp = w_pair[e]
            for g, (free, done) in enumerate((("n_b", "b_done"), ("n_c", "c_done"))):
                pe.wait_ge(s[free], k * 2 + 2)
                for part in range(2):
                    for j in range(KD):
                        last = nc.tensor.matmul(c.bank[:, 2 * g + part, :], wp[:, j, 1 + 2 * g + part, :], x[j],
                                                start=j == 0, stop=j == 1)
                last.then_inc(s[done], 1)

        def sums_of_squares(pe, k):
            pe.wait_ge(s["ang_in"], k + 1)
            pe.wait_ge(s["sq_b"], k * 2 + 2)
            for j in range(2):
                last = nc.tensor.matmul(c.bank[:, 4, :], halves[:], sq[:, j, :], start=j == 0, stop=j == 1)
            last.then_inc(s["ssq_b"], 1)
            pe.wait_ge(s["ln_c"], k + 1)
            pe.wait_ge(s["sq_c"], k * 2 + 2)
            for j in range(2):
                last = nc.tensor.matmul(c.bank[:, 5, :], halves[:], sq[:, 2 + j, :], start=j == 0, stop=j == 1)
            last.then_inc(s["ssq_c"], 1)

        def attend(pe, pair, n, k, between):
            pe.wait_ge(s["rot_v"], k + 1)
            pe.wait_ge(s["rot_p"], k * 4 + 5)
            pe.wait_ge(s["y_kept"], k + 1)

            def scores(u):
                b, h = u // 2, u % 2
                for blk in range(2):
                    t0 = T * b + P * blk
                    last = nc.tensor.matmul(c.bank[:, 6 + h, T * blk:T * blk + T - P * blk],
                                            rot[:, h, 0, t0:t0 + P], rot[:, h, 1, t0:T * (b + 1)],
                                            start=True, stop=True)
                last.then_inc(s["s_done"], 1)

            def outputs(u):
                b, h = u // 2, u % 2
                pe.wait_ge(s["mix_done"], k * 4 + u + 1)
                m = mix[:, u]
                tile = 4 * n + 2 * b
                x0, x1 = (xh[:, tile + blk, bass.ds(pair * 16 + 8 * h, 8)] for blk in range(2))
                y0 = DEC + 16 * b
                nc.tensor.matmul(c.bank[:, 6 + h, y0:y0 + 8], m[:, 0:P], x0, start=True, stop=True)
                nc.tensor.matmul(c.bank[:, 6 + h, y0 + 8:y0 + 16], m[:, P:T], x0, start=True, stop=False)
                return nc.tensor.matmul(c.bank[:, 6 + h, y0 + 8:y0 + 16], m[:, T:], x1, start=False, stop=True)

            scores(0)
            for u in range(1, 4):
                scores(u)
                outputs(u - 1) if u < 3 else between()
            outputs(2)
            outputs(3).then_inc(s["y_done"], 1)

        @block.tensor
        def _(pe):
            pe.sem_inc(s["s_done"], 1)
            pe.wait_ge(s["const"], 64)
            pe.wait_ge(s["w_even"], 16)
            project_angles(pe, 0, 0, 0)
            project(pe, 0, 0, 0)
            sums_of_squares(pe, 0)
            project_angles(pe, 1, 1, 0)
            project(pe, 1, 1, 0)

            def step(i, m, final):
                k = i * 8 + m
                if m < 7 or not final:
                    sums_of_squares(pe, k + 1)

                def next_angles():
                    if m == 2:
                        pe.wait_ge(s["w_odd"], i * 16 + 16)
                    if m == 6 and not final:
                        pe.wait_ge(s["w_even"], i * 16 + 32)
                    if m < 6 or not final:
                        project_angles(pe, (m + 2) % 4, k + 2, (m + 2) // 4 % 2)

                attend(pe, i * 2 + m // 4, m % 4, k, next_angles)
                if m < 6 or not final:
                    project(pe, (m + 2) % 4, k + 2, (m + 2) // 4 % 2)

            with nc.tensor.Fori(0, PASSES) as i:
                for m in range(8):
                    step(i, m, False)
            for m in range(8):
                step(PASSES, m, True)

        def squares(act, k):
            for g, (done, sqs) in enumerate((("b_done", "sq_b"), ("c_done", "sq_c"))):
                act.wait_ge(s[done], k + 1)
                for j in range(2):
                    nc.scalar.activation(sq[:, 2 * g + j, :], c.bank[:, 2 * g + j, :], ACT.Square
                                         ).then_inc(s[sqs], 1)

        def scale(act, k):
            for g, (ssq, ln) in enumerate((("ssq_b", "ln_b"), ("ssq_c", "ln_c"))):
                act.wait_ge(s[ssq], k + 1)
                nc.scalar.activation(rms[:, g, :], c.bank[:, 4 + g, :], ACT.Ln, scale=1.0 / SN,
                                     bias=eps[:, 0:1]).then_inc(s[ln], 1)
            for g, (ln, r) in enumerate((("ln_b", "r_b"), ("ln_c", "r_c"))):
                act.wait_ge(s[ln], k + 2)
                nc.scalar.activation(rms[:, g, :], rms[:, g, :], ACT.Exp, scale=-0.5).then_inc(s[r], 1)

        def weigh_and_bias(act, e, k):
            for g, (src, done) in enumerate((("n_b", "aff_b"), ("n_c", "aff_c"))):
                act.wait_ge(s[src], k * 2 + 4)
                for j in range(2 * g, 2 * g + 2):
                    last = nc.scalar.activation(nbc[:, j, :], nbc[:, j, :], ACT.Identity,
                                                scale=norm_w[:, j:j + 1], bias=pair_bias[:, e, j:j + 1])
                last.then_inc(s[done], 1)

        def turn(act, m, k):
            act.wait_ge(s["red_done"], k + 1)
            nc.scalar.activation(sn[:, m % 2, :], red[:], ACT.Sin).then_inc(s["trig"], 1)
            nc.scalar.activation(cs[:, m % 2, :], red[:], ACT.Abs).then_inc(s["cabs"], 1)
            act.wait_ge(s["cabs"], k + 1)
            nc.scalar.activation(cs[:, m % 2, :], cs[:, m % 2, :], ACT.Sin, scale=-1.0, bias=half_pi[:, 0:1]
                                 ).then_inc(s["trig"], 1)

        @block.scalar
        def _(act):
            for n in ("ln_b", "ln_c", "trig", "y_kept"):
                act.sem_inc(s[n], 1)
            act.wait_ge(s["set"], 1)
            act.wait_ge(s["const"], 64)
            squares(act, 0)
            act.wait_ge(s["cols_kept"], 1)
            scale(act, 0)
            turn(act, 0, 0)
            weigh_and_bias(act, 0, 0)
            squares(act, 1)

            def step(i, m, final):
                k = i * 8 + m
                if m < 7 or not final:
                    if m % 4 == 3:
                        act.wait_ge(s["cols_kept"], i * 2 + (m + 1) // 4 + 1)
                    scale(act, k + 1)
                    act.wait_ge(s["prod_p"], k * 2 + 2)
                    act.wait_ge(s["prod_v"], k + 1)
                    turn(act, m + 1, k + 1)
                    weigh_and_bias(act, (m + 1) // 4 % 2, k + 1)
                act.wait_ge(s["y_done"], k + 1)
                for h in range(2):
                    last = nc.scalar.activation(
                        y_tok[:, 4 * (m % 4):4 * (m % 4) + 4, bass.ds(i * 32 + 16 * (m // 4) + 8 * h, 8)],
                        c.bank[:, 6 + h, DEC:DEC + 32].rearrange("p (t h) -> p t h", h=8), ACT.Copy)
                last.then_inc(s["y_kept"], 1)
                if m < 6 or not final:
                    squares(act, k + 2)

            with nc.scalar.Fori(0, PASSES) as i:
                for m in range(8):
                    step(i, m, False)
            for m in range(8):
                step(PASSES, m, True)

        def pair_columns(pair, e):
            nc.vector.tensor_copy(bet[:, e], beta_tok[:, bass.ds(pair * 2, 2), :])
            nc.vector.tensor_copy(gam[:, e], gamma_tok[:, bass.ds(pair * 2, 2), :])
            nc.vector.tensor_copy(pair_bias[:, e:e + 1, :], bias[:, bass.ds(pair, 1), :]
                                  ).then_inc(s["cols_kept"], 1)

        def angles(dve, k):
            dve.wait_ge(s["dts_loaded"], k * 32 + 32)
            dve.wait_ge(s["th_done"], k + 1)
            nc.vector.tensor_tensor(ang[:], c.bank[:, 4, :], dts[:], ALU.mult).then_inc(s["ang_in"], 1)
            dve.wait_ge(s["ang_in"], k + 1)
            for b in range(2):
                last = nc.vector.tensor_tensor_scan(turns[:, T * b:T * (b + 1)],
                                                    c.ones[:, 0:1].broadcast_to([P, T]),
                                                    ang[:, T * b:T * (b + 1)], 0.0, ALU.mult, ALU.add)
            last.then_inc(s["ang_done"], 1)
            dve.wait_ge(s["ang_done"], k + 1)
            nc.vector.tensor_scalar(ang[:], turns[:], INV_2PI, ROUND, ALU.mult, ALU.add).then_inc(s["red_k"], 1)
            dve.wait_ge(s["red_k"], k + 1)
            nc.vector.tensor_scalar(ang[:], ang[:], ROUND, None, ALU.subtract).then_inc(s["ctr_k"], 1)
            dve.wait_ge(s["ctr_k"], k * 3 + 1)
            nc.vector.scalar_tensor_tensor(turns[:], ang[:], -TWO_PI_HI, turns[:], ALU.mult, ALU.add
                                           ).then_inc(s["ctr_k"], 1)
            dve.wait_ge(s["ctr_k"], k * 3 + 2)
            nc.vector.scalar_tensor_tensor(turns[:], ang[:], -TWO_PI_LO, turns[:], ALU.mult, ALU.add
                                           ).then_inc(s["ctr_k"], 1)
            dve.wait_ge(s["ctr_k"], k * 3 + 3)
            dve.wait_ge(s["trig"], k * 2 + 1)
            nc.vector.tensor_scalar(red[:], turns[:], PI, -PI, ALU.min, ALU.max).then_inc(s["red_done"], 1)

        def norm(dve, g, k):
            r, done = (("r_b", "n_b"), ("r_c", "n_c"))[g]
            dve.wait_ge(s[r], k + 1)
            dve.wait_ge(s["prod_p"], k * 2 + 1 + g)
            for j in range(2 * g, 2 * g + 2):
                nc.vector.tensor_tensor(nbc[:, j, :], c.bank[:, j, :], rms[:, g, :], ALU.mult
                                        ).then_inc(s[done], 1)

        def rotate(dve, m, k):
            dve.wait_ge(s["trig"], k * 2 + 3)
            for g, done in enumerate(("aff_b", "aff_c")):
                dve.wait_ge(s[done], k + 1)
                for part, angle in enumerate((cs, sn)):
                    j = 2 * g + part
                    last = nc.vector.tensor_tensor(pr[:, j, :], nbc[:, j, :], angle[:, m % 2, :], ALU.mult)
            last.then_inc(s["prod_v"], 1)
            dve.wait_ge(s["prod_v"], k + 2)
            dve.wait_ge(s["s_done"], k * 4 + 1)
            for h in range(2):
                half = pr[64 * h:64 * h + 64].rearrange("p (g q) t -> p g q t", q=2)
                last = nc.vector.tensor_tensor(rot[0:64, h], half[:, :, 0, :], half[:, :, 1, :], ALU.subtract)
            last.then_inc(s["rot_v"], 1)

        def decays(dve, m, k):
            dve.wait_ge(s["al_loaded"], k * 32 + 32)
            dve.wait_ge(s["start_done"], k + 1)
            nc.vector.tensor_tensor_scan(dec[:].rearrange("p h b t -> p (h b t)"),
                                         alphas[:].rearrange("p h b t -> p (h b t)"),
                                         start[:, m % 2].rearrange("p h b t -> p (h b t)"), 0.0,
                                         ALU.mult, ALU.add).then_inc(s["dec_done"], 1)

        def weigh(dve, u, k):
            dve.wait_ge(s["s_done"], k * 4 + u + 2)
            nc.vector.tensor_tensor(mix[:, u, :], dec[:, u % 2, u // 2], c.bank[:, 6 + u % 2, 0:DEC], ALU.mult
                                    ).then_inc(s["mix_done"], 1)

        @block.vector
        def _(dve):
            for n, v in (("n_b", 2), ("n_c", 2), ("prod_v", 1)):
                dve.sem_inc(s[n], v)
            nc.vector.memset(eps[:], 1e-6)
            nc.vector.memset(half_pi[:], HALF_PI)
            nc.vector.memset(diag[:, P:], 0.0)
            nc.vector.tensor_copy(diag[:, 0:P], c.ident[:])
            nc.vector.memset(start[:], 0.0).then_inc(s["set"], 1)
            dve.wait_ge(s["const"], 64)
            pair_columns(0, 0)
            dve.wait_ge(s["cols_kept"], 1)
            angles(dve, 0)
            norm(dve, 0, 0)
            norm(dve, 1, 0)
            rotate(dve, 0, 0)
            angles(dve, 1)
            decays(dve, 0, 0)

            def step(i, m, final):
                k = i * 8 + m
                if m % 4 == 2 and not (final and m == 6):
                    pair_columns(i * 2 + (m + 2) // 4, (m + 2) // 4 % 2)
                dve.wait_ge(s["dec_done"], k + 1)
                weigh(dve, 0, k)
                weigh(dve, 1, k)
                weigh(dve, 2, k)
                if m < 7 or not final:
                    norm(dve, 0, k + 1)
                weigh(dve, 3, k)
                if m < 7 or not final:
                    norm(dve, 1, k + 1)
                    rotate(dve, m + 1, k + 1)
                if m < 6 or not final:
                    angles(dve, k + 2)
                if m < 7 or not final:
                    decays(dve, m + 1, k + 1)

            with nc.vector.Fori(0, PASSES) as i:
                for m in range(8):
                    step(i, m, False)
            for m in range(8):
                step(PASSES, m, True)

        def starts(pool, m, n, e, k):
            across = diag, above
            for blk in range(2):
                width = P + 1 - blk
                for j, (out, table) in enumerate(((start[:, m % 2, :, :, T * blk:T * blk + width], gam),
                                                  (beside[:, blk, :, :, 0:width], bet))):
                    last = nc.gpsimd.tensor_tensor(
                        out, across[j][:, 0:width].unsqueeze(1).unsqueeze(1).broadcast_to([P, 2, 2, width]),
                        table[:, e, :, 4 * n + blk:4 * n + blk + 3:2].unsqueeze(3).broadcast_to([P, 2, 2, width]),
                        ALU.mult)
            last.then_inc(s["diag_done"], 1)
            pool.wait_ge(s["diag_done"], k + 1)
            for blk in range(2):
                width = P + 1 - blk
                out = start[:, m % 2, :, :, T * blk:T * blk + width]
                last = nc.gpsimd.tensor_tensor(out, out, beside[:, blk, :, :, 0:width], ALU.add)
            last.then_inc(s["start_done"], 1)

        def rotate_pool(pool, m, k):
            pool.wait_ge(s["trig"], k * 2 + 3)
            pool.wait_ge(s["s_done"], k * 4 + 1)
            for g in range(2):
                pool.wait_ge(s[("aff_b", "aff_c")[g]], k + 1)
                pool.wait_ge(s["rot_p"], k * 4 + 1 + 2 * g)
                for part, angle in enumerate((sn, cs)):
                    j = 2 * g + part
                    last = nc.gpsimd.tensor_tensor(pq[:, part, :], nbc[:, j, :], angle[:, m % 2, :], ALU.mult)
                last.then_inc(s["prod_p"], 1)
                pool.wait_ge(s["prod_p"], k * 2 + 3 + g)
                for h in range(2):
                    half = pq[64 * h:64 * h + 64]
                    nc.gpsimd.tensor_tensor(rot[64:128, h, g, :], half[:, 0, :], half[:, 1, :], ALU.add
                                            ).then_inc(s["rot_p"], 1)
                    pool.wait_ge(s["rot_p"], k * 4 + 2 * g + h + 2)

        @block.gpsimd
        def _(pool):
            pool.sem_inc(s["rot_p"], 1)
            pool.wait_ge(s["set"], 1)
            pool.sem_inc(s["prod_p"], 2)
            pool.wait_ge(s["cols_kept"], 1)
            starts(pool, 0, 0, 0, 0)
            rotate_pool(pool, 0, 0)
            pool.wait_ge(s["start_done"], 1)
            starts(pool, 1, 1, 0, 1)

            def step(i, m, final):
                k = i * 8 + m
                if m < 7 or not final:
                    rotate_pool(pool, m + 1, k + 1)
                if m < 6 or not final:
                    if m % 4 == 2:
                        pool.wait_ge(s["cols_kept"], i * 2 + (m + 2) // 4 + 1)
                    pool.wait_ge(s["dec_done"], k + 1)
                    pool.wait_ge(s["start_done"], k + 2)
                    starts(pool, m, (m + 2) % 4, (m + 2) // 4 % 2, k + 2)

            with nc.gpsimd.Fori(0, PASSES) as i:
                for m in range(8):
                    step(i, m, False)
            for m in range(8):
                step(PASSES, m, True)


def ssm_output(c, w, y_tok):
    nc = c.nc
    own = ExitStack()
    wz = c.sbuf("wz", [P, KD, DIN], ctx=own)
    wo = c.sbuf("ssm_wo", [P, DIN // P, D], ctx=own)
    z = c.sbuf("z", [P, 2, DIN], ctx=own)
    yz = c.sbuf("yz", [P, 2, DIN], ctx=own)
    yz_t = c.sbuf("yz_t", [P, 2, DIN // P, P], ctx=own)
    loaded, z_done, z_kept, gated, turned, copied, o_done, added = (
        c.sem("ssmout_" + n) for n in "loaded z_done z_kept gated turned copied o_done added".split())
    with own, nc.Block() as block:

        @block.sync
        def _(sp):
            sp.dma_start(wz[:], w["z"]).then_inc(loaded, 16)
            sp.dma_start(wo[:], w["out"]).then_inc(loaded, 16)

        @block.tensor
        def _(pe):
            def gate_input(t):
                if t >= 2:
                    pe.wait_ge(z_kept, t - 1)
                for k in range(KD):
                    last = nc.tensor.matmul(c.bank[:, t % 2, :], c.x_t[:, k, P * t:P * (t + 1)], wz[:, k, :],
                                            start=k == 0, stop=k == KD - 1)
                last.then_inc(z_done, 1)

            pe.wait_ge(loaded, 32)
            gate_input(0)
            for t in range(NT):
                if t + 1 < NT:
                    gate_input(t + 1)
                pe.wait_ge(gated, t + 1)
                if t >= 2:
                    pe.wait_ge(copied, t - 1)
                for j in range(4):
                    last = nc.tensor.transpose(c.bank[:, 2 + t % 2, P * j:P * (j + 1)],
                                               yz[:, t % 2, P * j:P * (j + 1)], c.ident[:])
                last.then_inc(turned, 1)
                pe.wait_ge(copied, t + 1)
                if t >= 2:
                    pe.wait_ge(added, t - 1)
                for j in range(4):
                    last = nc.tensor.matmul(c.bank[:, 4 + t % 2, 0:D], yz_t[:, t % 2, j, :], wo[:, j, :],
                                            start=j == 0, stop=j == 3)
                last.then_inc(o_done, 1)

        @block.scalar
        def _(act):
            for t in range(NT):
                act.wait_ge(z_done, t + 1)
                if t >= 2:
                    act.wait_ge(gated, t - 1)
                nc.scalar.activation(z[:, t % 2, :], c.bank[:, t % 2, :], ACT.Silu).then_inc(z_kept, 1)

        @block.vector
        def _(dve):
            for t in range(NT):
                dve.wait_ge(z_kept, t + 1)
                if t >= 2:
                    dve.wait_ge(turned, t - 1)
                nc.vector.tensor_tensor(yz[:, t % 2, :], y_tok[:, t, :], z[:, t % 2, :], ALU.mult
                                        ).then_inc(gated, 1)
                dve.wait_ge(turned, t + 1)
                if t >= 2:
                    dve.wait_ge(o_done, t - 1)
                nc.vector.tensor_copy(yz_t[:, t % 2, :, :].rearrange("p j t -> p (j t)"),
                                      c.bank[:, 2 + t % 2, :]).then_inc(copied, 1)
                dve.wait_ge(o_done, t + 1)
                nc.vector.tensor_tensor(c.x_tok[:, t, :], c.x_tok[:, t, :], c.bank[:, 4 + t % 2, 0:D],
                                        ALU.add).then_inc(added, 1)



XH, XD = 16, 128
XP = XH // 2
BIG = 1e30


def cross_attention(c, w, normed):
    nc = c.nc
    own = ExitStack()
    tag = "xn_" if normed else "xm_"

    def sb(name, shape, dt=F32, ctx=own):
        return c.sbuf(tag + name, shape, dt, ctx=ctx)

    kvh = XH if normed else XP
    wq = sb("wq", [P, KD, XH * XD])
    wo = sb("wo", [P, XH, D])
    k_t = sb("k_t", [P, kvh, B * S2])
    v = sb("v", [P, B, XP * XD])
    neg = sb("neg", [P, B * S2])
    main_loaded = c.sem(tag + "main_loaded")
    with own:
        cross_keys(c, w, normed, tag, kvh, wq, wo, k_t, v, neg, main_loaded)
        cross_heads(c, normed, tag, kvh, wq, wo, k_t, v, neg, main_loaded)


def cross_keys(c, w, normed, tag, kvh, wq, wo, k_t, v, neg, main_loaded):
    nc = c.nc
    own = ExitStack()

    def sb(name, shape, dt=F32):
        return c.sbuf(tag + name, shape, dt, ctx=own)

    par = 2 if normed else 1
    wk = sb("wk", [P, kvh * XD])
    wv = sb("wv", [P, par, XP * XD])
    ctx_t = sb("ctx_t", [P, B * S2])
    loaded, k_done, k_kept, sq_done, ssq_done, r_done, v_done, v_kept, m_done = (
        c.sem(tag + n) for n in "loaded k_done k_kept sq_done ssq_done r_done v_done v_kept m_done".split())
    if normed:
        g = sb("g", [P, 2])
        eps = sb("eps", [P, 1])
        sq = sb("sq", [P, 2, B * S2])
        rms = sb("rms", [P, 2, B * S2])
    else:
        mask_row = sb("mask_row", [P, B * S2], U8)
        mask_col = sb("mask_col", [P, B], U8)
        keep = sb("keep", [P, B])
    with own, nc.Block() as block:

        @block.sync
        def _(sp):
            sp.dma_start(ctx_t[:], w["ctx"]).then_inc(loaded, 16)
            sp.dma_start(wk[:], w["k"]).then_inc(loaded, 16)
            sp.dma_start(wv[:], w["v"]).then_inc(loaded, 16)
            if normed:
                sp.dma_start(g[:], w["g"]).then_inc(loaded, 16)
            else:
                sp.dma_start(mask_row[:], w["mask_row"].partition_broadcast(P)).then_inc(loaded, 16)
                sp.dma_start(mask_col[:], w["mask_col"]).then_inc(loaded, 16)
            sp.dma_start(wq[:], w["q"]).then_inc(main_loaded, 16)
            sp.dma_start(wo[:], w["o"]).then_inc(main_loaded, 16)

        all_in = 64 if normed else 80

        @block.tensor
        def _(pe):
            pe.wait_ge(loaded, all_in)
            for h in range(kvh + 1):
                if h < kvh:
                    if h >= 2:
                        pe.wait_ge(k_kept, h - 1)
                    nc.tensor.matmul(c.bank[:, h % 2, :], wk[:, XD * h:XD * (h + 1)], ctx_t[:], start=True,
                                     stop=True).then_inc(k_done, 1)
                if h and normed:
                    pe.wait_ge(sq_done, h)
                    if h >= 3:
                        pe.wait_ge(r_done, 2 * (h - 2) - 1)
                    nc.tensor.matmul(c.bank[:, 2 + h % 2, :], c.ones[:], sq[:, (h - 1) % 2, :], start=True,
                                     stop=True).then_inc(ssq_done, 1)
            for j in range(2 * B):
                b, half = divmod(j, 2)
                if j >= 2:
                    pe.wait_ge(v_kept, j - 1)
                for parity in range(2):
                    last = nc.tensor.matmul(c.bank[64 * parity:64 * parity + 64, 4 + j % 2, :],
                                            ctx_t[:, S2 * b:S2 * (b + 1)],
                                            wv[:, parity % par, SEG * half:SEG * (half + 1)],
                                            start=True, stop=True)
                last.then_inc(v_done, 1)

        @block.scalar
        def _(act):
            if normed:
                act.wait_ge(m_done, 1)
                for h in range(kvh):
                    act.wait_ge(k_done, h + 1)
                    if h >= 2:
                        act.wait_ge(ssq_done, h - 1)
                    nc.scalar.activation(sq[:, h % 2, :], c.bank[:, h % 2, :], ACT.Square).then_inc(sq_done, 1)
                    act.wait_ge(ssq_done, h + 1)
                    if h >= 2:
                        act.wait_ge(k_kept, h - 1)
                    nc.scalar.activation(rms[:, h % 2, :], c.bank[:, 2 + (h + 1) % 2, :], ACT.Ln, scale=1.0 / XD,
                                         bias=eps[:, 0:1]).then_inc(r_done, 1)
                    act.wait_ge(r_done, 2 * h + 1)
                    nc.scalar.activation(rms[:, h % 2, :], rms[:, h % 2, :], ACT.Exp, scale=-0.5
                                         ).then_inc(r_done, 1)
            if not normed:
                act.wait_ge(m_done, 1)
            for j in range(2 * B):
                b, half = divmod(j, 2)
                act.wait_ge(v_done, j + 1)
                out = v[:, b, SEG * half:SEG * (half + 1)]
                if normed:
                    nc.scalar.activation(out, c.bank[:, 4 + j % 2, :], ACT.Copy).then_inc(v_kept, 1)
                else:
                    nc.scalar.activation(out, c.bank[:, 4 + j % 2, :], ACT.Copy, scale=keep[:, b:b + 1]
                                         ).then_inc(v_kept, 1)

        @block.vector
        def _(dve):
            if normed:
                nc.vector.memset(eps[:], 1e-5).then_inc(m_done, 1)
            dve.wait_ge(loaded, all_in)
            if not normed:
                nc.vector.tensor_copy(keep[:], mask_col[:]).then_inc(m_done, 1)
                nc.vector.tensor_scalar(neg[:], mask_row[:], -1.0, BIG, ALU.add, ALU.mult)
            for h in range(kvh):
                if normed:
                    dve.wait_ge(r_done, 2 * h + 2)
                    nc.vector.tensor_tensor(k_t[:, h, :], c.bank[:, h % 2, :], rms[:, h % 2, :], ALU.mult
                                            ).then_inc(k_kept, 1)
                    dve.wait_ge(k_kept, h + 1)
                    nc.vector.tensor_scalar(k_t[:, h, :], k_t[:, h, :], g[:, 0:1], g[:, 1:2], ALU.mult, ALU.mult)
                else:
                    dve.wait_ge(k_done, h + 1)
                    nc.vector.tensor_copy(k_t[:, h, :], c.bank[:, h % 2, :]).then_inc(k_kept, 1)


def cross_heads(c, normed, tag, kvh, wq, wo, k_t, v, neg, main_loaded):
    nc = c.nc
    own = ExitStack()

    def sb(name, shape, dt=F32):
        return c.sbuf(tag + name, shape, dt, ctx=own)

    scale = XD ** -0.5
    q = sb("q", [P, 2, 2, T])
    sc = sb("sc", [P, 2, 4, S2])
    probs = sb("probs", [P, 2, 4, S2])
    top = sb("top", [P, 2, 4])
    total = sb("total", [P, 2, 4])
    p_t = sb("p_t", [P, 2, T])
    o_t = sb("o_t", [P, XH, T])
    vb = sb("vb", [P, XP * XD])
    names = ("q_done q_kept s_done s_used shifted top_done exp_done sums p_done t_done t_kept o_done o_kept v_kept "
             "out_done added sq_done rq_in rq_ln rq_done eps_set").split()
    s = {n: c.sem(tag + "h_" + n) for n in names}
    if normed:
        qsq = sb("qsq", [P, 2, 2, T])
        rq = sb("rq", [P, 2, 4])
        eps = sb("eps_q", [P, 1])
    with own, nc.Block() as block:

        @block.tensor
        def _(pe):
            def queries(i, j):
                pe.wait_ge(s["q_kept"], i * XP + j + 1)
                for h in range(2):
                    for k in range(KD):
                        last = nc.tensor.matmul(c.bank[:, j % 2, T * h:T * (h + 1)],
                                                wq[:, k, XD * (2 * j + h):XD * (2 * j + h + 1)],
                                                c.x_t[:, k, bass.ds(i * T, T)], start=k == 0, stop=k == 1)
                last.then_inc(s["q_done"], 1)

            def scores(i, j):
                pe.wait_ge(s["q_kept"], i * XP + j + 3)
                if normed:
                    pe.wait_ge(s["sq_done"], i * XP + j + 1)
                pe.wait_ge(s["s_used"], i * XP + j + 1)
                for t in range(2):
                    for h in range(2):
                        at = (2 * t + h) * S2
                        head = 2 * j + h if normed else j
                        last = nc.tensor.matmul(c.bank[:, 2 + j % 2, at:at + S2], q[:, j % 2, h, P * t:P * (t + 1)],
                                                k_t[:, head, bass.ds(i * S2, S2)], start=True, stop=True)
                if normed:
                    for t in range(2):
                        for h in range(2):
                            at = 4 * S2 + 2 * t + h
                            last = nc.tensor.matmul(c.bank[:, 2 + j % 2, at:at + 1],
                                                    qsq[:, j % 2, h, P * t:P * (t + 1)], c.ones[:, 0:1],
                                                    start=True, stop=True)
                last.then_inc(s["s_done"], 1)

            def turn(i, j):
                pe.wait_ge(s["p_done"], i * XP + j + 1)
                pe.wait_ge(s["t_kept"], i * XP + j + 1)
                for t in range(2):
                    last = nc.tensor.transpose(c.bank[:, 4, P * t:P * (t + 1)],
                                               probs[:, j % 2, 2 * t:2 * t + 2, :].rearrange("p h s -> p (h s)"),
                                               c.ident[:])
                last.then_inc(s["t_done"], 1)

            def values(i, j):
                pe.wait_ge(s["t_kept"], i * XP + j + 2)
                pe.wait_ge(s["o_kept"], i * XP + j + 1)
                if j == 0:
                    pe.wait_ge(s["v_kept"], i + 1)
                for h in range(2):
                    rows = slice(64 * h, 64 * h + 64)
                    last = nc.tensor.matmul(c.bank[:, 5 + h, 0:T], vb[rows, XD * j:XD * (j + 1)],
                                            p_t[rows, j % 2, :], start=True, stop=True)
                last.then_inc(s["o_done"], 1)

            for n, v_ in (("s_done", 2), ("t_done", 2), ("o_done", 2), ("out_done", 1)):
                pe.sem_inc(s[n], v_)
            pe.wait_ge(main_loaded, 32)
            if normed:
                pe.wait_ge(s["eps_set"], 1)
            with nc.tensor.Fori(0, B) as i:
                queries(i, 0)
                for j in range(XP + 2):
                    if j + 1 < XP:
                        queries(i, j + 1)
                    if j < XP:
                        scores(i, j)
                    if 1 <= j <= XP:
                        turn(i, j - 1)
                    if j >= 2:
                        values(i, j - 2)
                pe.wait_ge(s["o_kept"], i * XP + XP + 1)
                pe.wait_ge(s["added"], i + 1)
                for t in range(2):
                    for h in range(XH):
                        last = nc.tensor.matmul(c.bank[:, 7, D * t:D * (t + 1)], o_t[:, h, P * t:P * (t + 1)],
                                                wo[:, h, :], start=h == 0, stop=h == XH - 1)
                last.then_inc(s["out_done"], 1)

        @block.scalar
        def _(act):
            act.sem_inc(s["q_kept"], 2)
            act.sem_inc(s["t_kept"], 1)
            act.sem_inc(s["o_kept"], 1)

            def keep_q(i, j):
                act.wait_ge(s["q_done"], i * XP + j + 1)
                act.wait_ge(s["s_done"], i * XP + j + 1)
                nc.scalar.activation(q[:, j % 2].rearrange("p h t -> p (h t)"), c.bank[:, j % 2, :], ACT.Copy
                                     ).then_inc(s["q_kept"], 1)

            def exps(i, j):
                if normed:
                    act.wait_ge(s["rq_in"], i * XP + j + 1)
                    nc.scalar.activation(rq[:, j % 2, :], rq[:, j % 2, :], ACT.Ln,
                                         scale=1.0 / XD, bias=eps[:, 0:1]).then_inc(s["rq_ln"], 1)
                    act.wait_ge(s["rq_ln"], i * XP + j + 1)
                    nc.scalar.activation(rq[:, j % 2, :], rq[:, j % 2, :], ACT.Exp, scale=-0.5
                                         ).then_inc(s["rq_done"], 1)
                act.wait_ge(s["shifted"], i * XP + j + 1)
                nc.scalar.activation(sc[:, j % 2], sc[:, j % 2], ACT.Exp, scale=scale).then_inc(s["exp_done"], 1)

            def keep_t(i, j):
                act.wait_ge(s["t_done"], i * XP + j + 3)
                act.wait_ge(s["o_done"], i * XP + j + 1)
                nc.scalar.activation(p_t[:, j % 2, :], c.bank[:, 4, 0:T], ACT.Copy).then_inc(s["t_kept"], 1)

            def keep_o(i, j):
                act.wait_ge(s["o_done"], i * XP + j + 3)
                if j == 0:
                    act.wait_ge(s["out_done"], i + 1)
                nc.scalar.activation(o_t[:, 2 * j:2 * j + 2, :],
                                     c.bank[:, 5:7, 0:T], ACT.Copy
                                     ).then_inc(s["o_kept"], 1)

            if normed:
                act.wait_ge(s["eps_set"], 1)
            with nc.scalar.Fori(0, B) as i:
                keep_q(i, 0)
                for j in range(XP + 2):
                    if j + 1 < XP:
                        keep_q(i, j + 1)
                    if j < XP:
                        exps(i, j)
                    if 1 <= j <= XP:
                        keep_t(i, j - 1)
                    if j >= 2:
                        keep_o(i, j - 2)

        @block.vector
        def _(dve):
            dve.sem_inc(s["s_used"], 2)
            dve.sem_inc(s["added"], 1)
            if normed:
                nc.vector.memset(eps[:], 1e-5).then_inc(s["eps_set"], 1)

            def shift(i, j):
                dve.wait_ge(s["s_done"], i * XP + j + 3)
                scores = c.bank[:, 2 + j % 2, 0:4 * S2].rearrange("p (g s) -> p g s", s=S2)
                spread = top[:, j % 2, :].unsqueeze(2).broadcast_to([P, 4, S2])
                if normed:
                    nc.vector.tensor_copy(rq[:, j % 2, :], c.bank[:, 2 + j % 2, 4 * S2:4 * S2 + 4]
                                          ).then_inc(s["rq_in"], 1)
                    nc.vector.tensor_reduce(top[:, j % 2, :], scores, AX.X, ALU.max).then_inc(s["top_done"], 1)
                    dve.wait_ge(s["rq_done"], i * XP + j + 1)
                    dve.wait_ge(s["top_done"], i * XP + j + 1)
                    nc.vector.tensor_tensor(sc[:, j % 2], scores, spread, ALU.subtract).then_inc(s["s_used"], 1)
                    dve.wait_ge(s["s_used"], i * XP + j + 3)
                    nc.vector.tensor_tensor(sc[:, j % 2], sc[:, j % 2],
                                            rq[:, j % 2, :].unsqueeze(2).broadcast_to([P, 4, S2]), ALU.mult
                                            ).then_inc(s["shifted"], 1)
                else:
                    bias = neg[:, bass.ds(i * S2, S2)].unsqueeze(1).broadcast_to([P, 4, S2])
                    nc.vector.tensor_tensor(sc[:, j % 2], scores, bias, ALU.add).then_inc(s["s_used"], 1)
                    dve.wait_ge(s["s_used"], i * XP + j + 3)
                    nc.vector.tensor_reduce(top[:, j % 2, :], sc[:, j % 2], AX.X, ALU.max).then_inc(s["top_done"], 1)
                    dve.wait_ge(s["top_done"], i * XP + j + 1)
                    nc.vector.tensor_tensor(sc[:, j % 2], sc[:, j % 2], spread, ALU.subtract
                                            ).then_inc(s["shifted"], 1)

            def normalise(i, j):
                dve.wait_ge(s["exp_done"], i * XP + j + 1)
                nc.vector.tensor_reduce(total[:, j % 2, :], sc[:, j % 2], AX.X, ALU.add).then_inc(s["sums"], 1)
                dve.wait_ge(s["sums"], i * 2 * XP + 2 * j + 1)
                nc.vector.reciprocal(total[:, j % 2, :], total[:, j % 2, :]).then_inc(s["sums"], 1)
                dve.wait_ge(s["sums"], i * 2 * XP + 2 * j + 2)
                dve.wait_ge(s["t_done"], i * XP + j + 1)
                nc.vector.tensor_tensor(probs[:, j % 2], sc[:, j % 2],
                                        total[:, j % 2, :].unsqueeze(2).broadcast_to([P, 4, S2]), ALU.mult
                                        ).then_inc(s["p_done"], 1)

            with nc.vector.Fori(0, B) as i:
                for j in range(XP + 1):
                    if j < XP:
                        shift(i, j)
                    if j:
                        normalise(i, j - 1)
                dve.wait_ge(s["out_done"], i + 2)
                nc.vector.tensor_tensor(c.x_tok[:, bass.ds(i * 2, 2), :], c.x_tok[:, bass.ds(i * 2, 2), :],
                                        c.bank[:, 7, :].rearrange("p (t d) -> p t d", t=2), ALU.add
                                        ).then_inc(s["added"], 1)

        @block.gpsimd
        def _(pool):
            with nc.gpsimd.Fori(0, B) as i:
                pool.wait_ge(s["o_done"], i * XP + 2)
                nc.gpsimd.tensor_copy(vb[:], v[:, bass.ds(i, 1), :].rearrange("p o n -> p (o n)")
                                      ).then_inc(s["v_kept"], 1)
                if normed:
                    for j in range(XP):
                        pool.wait_ge(s["q_kept"], i * XP + j + 3)
                        pool.wait_ge(s["s_done"], i * XP + j + 1)
                        nc.gpsimd.tensor_tensor(qsq[:, j % 2], q[:, j % 2], q[:, j % 2], ALU.mult
                                                ).then_inc(s["sq_done"], 1)



def gated_ffn(c, tag, rows, w_in, w_out, scale_gate, scale_up, ready):
    nc = c.nc
    own = ExitStack()
    M = len(rows)
    gate = c.sbuf(tag + "gate_out", [P, 2, SEG], ctx=own)
    hid = c.sbuf(tag + "hid", [P, M, SEG], ctx=own)
    s = {n: c.sem(tag + n) for n in "in_done silu_done hid_done out_done added".split()}
    with own, nc.Block() as block:

        @block.tensor
        def _(pe):
            with nc.tensor.Fori(0, NSEG) as i:
                for m in range(M):
                    r = rows[m]
                    pe.wait_ge(s["hid_done"], i * M + m + 1)
                    for g in range(2):
                        for k in range(KD):
                            last = nc.tensor.matmul(c.bank[:, 2 * (m % 2) + g, :], w_in[:, k, g, P * m:P * (m + 1)],
                                                    c.x_t[:, k, bass.ds(i * SEG, SEG)], start=k == 0, stop=k == 1)
                    last.then_inc(s["in_done"], 1)
                pe.wait_ge(s["hid_done"], i * M + M + 2)
                for half in range(2):
                    pe.wait_ge(s["added"], i * 2 + half + 1)
                    for t in range(2):
                        for m in range(M):
                            r = rows[m]
                            at = P * (2 * half + t)
                            last = nc.tensor.matmul(c.bank[:, 4 + half, D * t:D * (t + 1)], hid[0:r, m, at:at + P],
                                                    w_out[0:r, m, :], start=m == 0, stop=m == M - 1)
                    last.then_inc(s["out_done"], 1)

        @block.scalar
        def _(act):
            with nc.scalar.Fori(0, NSEG) as i:
                for m in range(M):
                    r = rows[m]
                    act.wait_ge(s["in_done"], i * M + m + 1)
                    act.wait_ge(s["hid_done"], i * M + m + 1)
                    nc.scalar.activation(gate[0:r, m % 2, :], c.bank[0:r, 2 * (m % 2), :], ACT.Silu,
                                         scale=scale_gate[0:r, m:m + 1]).then_inc(s["silu_done"], 1)

        @block.vector
        def _(dve):
            dve.sem_inc(s["hid_done"], 2)
            dve.sem_inc(s["added"], 2)
            with nc.vector.Fori(0, NSEG) as i:
                for m in range(M):
                    r = rows[m]
                    dve.wait_ge(s["silu_done"], i * M + m + 1)
                    nc.vector.scalar_tensor_tensor(hid[0:r, m, :], c.bank[0:r, 2 * (m % 2) + 1, :],
                                                   scale_up[0:r, m:m + 1], gate[0:r, m % 2, :], ALU.mult, ALU.mult
                                                   ).then_inc(s["hid_done"], 1)
                for half in range(2):
                    dve.wait_ge(s["out_done"], i * 2 + half + 1)
                    x = c.x_tok[:, bass.ds(i * 4 + 2 * half, 2), :]
                    nc.vector.tensor_tensor(x, x, c.bank[:, 4 + half, :].rearrange("p (t d) -> p t d", t=2),
                                            ALU.add).then_inc(s["added"], 1)


HID0, HSCALE = 1024, 64.0


def hadamard_ffn(c, w):
    nc = c.nc
    own = ExitStack()
    M = HID0 // P
    w_in = c.sbuf("had_in", [P, KD, 2, HID0], ctx=own)
    w_out = c.sbuf("had_out", [P, M, D], ctx=own)
    scales = c.sbuf("had_scales", [P, 2, M], ctx=own)
    with own:
        mine = ExitStack()
        up = c.sbuf("had_rows", [P, 2, 2 * M, D], ctx=mine)
        dn = c.sbuf("had_down_rows", [P, 2, KD, HID0], ctx=mine)
        su_in = c.sbuf("had_su_in", [P, KD], ctx=mine)
        su_out = c.sbuf("had_su_out", [P, M], ctx=mine)
        down_scale = c.sbuf("had_down_scale", [P, KD], ctx=mine)
        loaded, plus, minus, turned, kept, scaled = (
            c.sem("had_" + n) for n in "loaded plus minus turned kept scaled".split())
        stages_in = D.bit_length() - 1
        stages_out = HID0.bit_length() - 1
        with mine, nc.Block() as block:

            @block.sync
            def _(sp):
                sp.dma_start(up[:, 0], w["rows"]).then_inc(loaded, 16)
                sp.dma_start(dn[:, 0], w["down"]).then_inc(loaded, 16)
                for t, n in ((su_in, "su_in"), (su_out, "su_out"), (down_scale, "down_scale"), (scales, "scales")):
                    sp.dma_start(t[:], w[n]).then_inc(loaded, 16)

            def butterflies(eng, unit, op, mine_done, other_done):
                eng.wait_ge(loaded, 96)
                n = 0
                for buf, stages in ((up, stages_in), (dn, stages_out)):
                    for st in range(stages):
                        if n:
                            eng.wait_ge(mine_done, n)
                            eng.wait_ge(other_done, n)
                        h = 1 << st
                        src, dst = (buf[:, (st + o) % 2].rearrange("p m d -> p (m d)").rearrange(
                            "p (g two h) -> p g two h", two=2, h=h) for o in range(2))
                        which = 0 if op == ALU.add else 1
                        unit.tensor_tensor(dst[:, :, which, :], src[:, :, 0, :], src[:, :, 1, :], op
                                           ).then_inc(mine_done, 1)
                        n += 1

            all_stages = stages_in + stages_out
            up_at, dn_at = stages_in % 2, stages_out % 2

            @block.vector
            def _(dve):
                butterflies(dve, nc.vector, ALU.add, plus, minus)
                dve.wait_ge(plus, all_stages)
                dve.wait_ge(minus, all_stages)
                nc.vector.tensor_scalar(scales[:], scales[:], HSCALE, None, ALU.mult)
                nc.vector.tensor_scalar(down_scale[:], down_scale[:], HSCALE, None, ALU.mult).then_inc(scaled, 1)
                nc.vector.tensor_scalar(su_in[:], su_in[:], D ** -0.5 / HSCALE, None, ALU.mult).then_inc(scaled, 1)
                nc.vector.tensor_scalar(su_out[:], su_out[:], HID0 ** -0.5 / HSCALE, None, ALU.mult
                                        ).then_inc(scaled, 1)
                dve.wait_ge(scaled, 1)
                for k in range(KD):
                    nc.vector.tensor_scalar(dn[:, dn_at, k, :], dn[:, dn_at, k, :], down_scale[:, k:k + 1], None,
                                            ALU.mult).then_inc(scaled, 1)

            @block.gpsimd
            def _(pool):
                butterflies(pool, nc.gpsimd, ALU.subtract, minus, plus)

            @block.tensor
            def _(pe):
                pe.wait_ge(plus, stages_in)
                pe.wait_ge(minus, stages_in)
                n = 0
                for g in range(2):
                    for k in range(KD):
                        for half in range(2):
                            if n >= 4:
                                pe.wait_ge(kept, n - 3)
                            for j in range(4):
                                m = g * M + 4 * half + j
                                last = nc.tensor.transpose(c.bank[:, n % 4, P * j:P * (j + 1)],
                                                           up[:, up_at, m, P * k:P * (k + 1)], c.ident[:])
                            last.then_inc(turned, 1)
                            n += 1
                pe.wait_ge(scaled, 3 + KD)
                for m in range(M):
                    pe.wait_ge(kept, n - 3)
                    for k in range(KD):
                        last = nc.tensor.transpose(c.bank[:, n % 4, P * k:P * (k + 1)],
                                                   dn[:, dn_at, k, P * m:P * (m + 1)], c.ident[:])
                    last.then_inc(turned, 1)
                    n += 1

            @block.scalar
            def _(act):
                act.wait_ge(scaled, 3)
                n = 0
                for g in range(2):
                    for k in range(KD):
                        for half in range(2):
                            act.wait_ge(turned, n + 1)
                            nc.scalar.activation(w_in[:, k, g, SEG * half:SEG * (half + 1)], c.bank[:, n % 4, :],
                                                 ACT.Copy, scale=su_in[:, k:k + 1]).then_inc(kept, 1)
                            n += 1
                for m in range(M):
                    act.wait_ge(turned, n + 1)
                    nc.scalar.activation(w_out[:, m, :], c.bank[:, n % 4, 0:D], ACT.Copy, scale=su_out[:, m:m + 1]
                                         ).then_inc(kept, 1)
                    n += 1

        gated_ffn(c, "had_", [P] * M, w_in, w_out, scales[:, 0, :], scales[:, 1, :], None)


HID1, ZERO_POINT = 704, 128.0


def dequant_ffn(c, w):
    nc = c.nc
    own = ExitStack()
    M = -(-HID1 // P)
    rows = [min(P, HID1 - P * m) for m in range(M)]
    w_in = c.sbuf("deq_in", [P, KD, 2, P * M], ctx=own)
    w_out = c.sbuf("deq_out", [P, M, D], ctx=own)
    s_gate = c.sbuf("deq_s_gate", [P, M], ctx=own)
    s_up = c.sbuf("deq_s_up", [P, M], ctx=own)
    with own:
        mine = ExitStack()
        q_in = c.sbuf("deq_q_in", [P, KD, 2, HID1], I32, ctx=mine)
        q_out = c.sbuf("deq_q_out", [P, M, D], I32, ctx=mine)
        s_down = c.sbuf("deq_s_down", [P, D], ctx=mine)
        loaded, centred = c.sem("deq_loaded"), c.sem("deq_centred")
        with mine, nc.Block() as block:

            @block.sync
            def _(sp):
                sp.dma_start(q_in[:], w["in"]).then_inc(loaded, 16)
                sp.dma_start(s_down[:], w["s_down"].partition_broadcast(P)).then_inc(loaded, 16)
                for m in range(M):
                    r = rows[m]
                    for t, src in ((q_out[0:r, m, :], w["out"][P * m:P * m + r, :]),
                                   (s_gate[0:r, m:m + 1], w["s_gate"][P * m:P * m + r, :]),
                                   (s_up[0:r, m:m + 1], w["s_up"][P * m:P * m + r, :])):
                        sp.dma_start(t, src).then_inc(loaded, 16)

            @block.vector
            def _(dve):
                dve.wait_ge(loaded, 16 * (2 + 3 * M))
                for k in range(KD):
                    nc.vector.memset(w_in[:, k, :, HID1:], 0.0)
                    nc.vector.tensor_scalar(w_in[:, k, :, 0:HID1], q_in[:, k], ZERO_POINT, None, ALU.subtract)
                for m in range(M):
                    r = rows[m]
                    nc.vector.tensor_scalar(w_out[0:r, m, :], q_out[0:r, m, :], ZERO_POINT, None, ALU.subtract
                                            ).then_inc(centred, 1)
                for m in range(M):
                    r = rows[m]
                    dve.wait_ge(centred, m + 1)
                    nc.vector.tensor_tensor(w_out[0:r, m, :], w_out[0:r, m, :], s_down[0:r, :], ALU.mult)

        gated_ffn(c, "deq_", rows, w_in, w_out, s_gate, s_up, None)



KH, KW = 16, 128
LEVELS = 7
CH = SEG // P


def kda(c, w):
    own = ExitStack()
    xf_t = c.sbuf("xf_t", [P, TOK], ctx=own)
    xg_t = c.sbuf("xg_t", [P, TOK], ctx=own)
    beta = c.sbuf("beta", [KH, TOK], ctx=own)
    neg_a = c.sbuf("kda_neg_a", [P, KH], ctx=own)
    with own:
        kda_gates(c, w, xf_t, xg_t, beta, neg_a)
        kda_heads(c, w, xf_t, xg_t, beta, neg_a)


def kda_gates(c, w, xf_t, xg_t, beta, neg_a):
    nc = c.nc
    own = ExitStack()
    wfg = c.sbuf("wfg", [P, KD, 2, KW], ctx=own)
    wb = c.sbuf("wb", [P, KD, KH], ctx=own)
    loaded, done, kept = (c.sem("kg_" + n) for n in "loaded done kept".split())
    with own, nc.Block() as block:

        @block.sync
        def _(sp):
            sp.dma_start(wfg[:], w["fg"]).then_inc(loaded, 16)
            sp.dma_start(wb[:], w["b"]).then_inc(loaded, 16)
            sp.dma_start(neg_a[:], w["A_log"].partition_broadcast(P)).then_inc(loaded, 16)

        @block.tensor
        def _(pe):
            pe.wait_ge(loaded, 48)
            for q in range(NSEG):
                if q:
                    pe.wait_ge(kept, 3 * q)
                for g in range(3):
                    for k in range(KD):
                        lhs = wb[:, k, :] if g == 2 else wfg[:, k, g, :]
                        out = c.bank[0:KH, 2, :] if g == 2 else c.bank[:, g, :]
                        last = nc.tensor.matmul(out, lhs, c.x_t[:, k, SEG * q:SEG * (q + 1)], start=k == 0,
                                                stop=k == 1)
                    last.then_inc(done, 1)

        @block.scalar
        def _(act):
            for q in range(NSEG):
                cols = slice(SEG * q, SEG * (q + 1))
                for g, out in enumerate((xf_t, xg_t)):
                    act.wait_ge(done, 3 * q + g + 1)
                    nc.scalar.activation(out[:, cols], c.bank[:, g, :], ACT.Copy).then_inc(kept, 1)
                act.wait_ge(done, 3 * q + 3)
                nc.scalar.activation(beta[:, cols], c.bank[0:KH, 2, :], ACT.Sigmoid).then_inc(kept, 1)
            act.wait_ge(loaded, 48)
            nc.scalar.activation(neg_a[:], neg_a[:], ACT.Exp).then_inc(kept, 1)

        @block.vector
        def _(dve):
            dve.wait_ge(kept, 3 * NSEG + 1)
            nc.vector.tensor_scalar(neg_a[:], neg_a[:], -1.0, None, ALU.mult)


def halves_of(ap, m, side):
    if len(ap.shape) == 2:
        return ap.rearrange("p (g two m) -> p g two m", two=2, m=m)[:, :, side, :]
    return ap.rearrange("p c (g two m) -> p c g two m", two=2, m=m)[:, :, :, side, :]


def kda_heads(c, w, xf_t, xg_t, beta, neg_a):
    nc = c.nc
    own = ExitStack()

    def sb(name, shape, dt=F32):
        return c.sbuf("k_" + name, shape, dt, ctx=own)

    wqkv = sb("wqkv", [P, KD, 3, KW])
    wfg2 = sb("wfg2", [P, 2, KW])
    wo = sb("wo", [P, D])
    taps = sb("taps", [P, 3, 5])
    dt_bias = sb("dt_bias", [P, 1])
    sel = sb("sel", [KH, P])
    decay = sb("decay", [P, 1])
    o_norm = sb("o_norm", [P, 1])
    masks = sb("masks", [P, LEVELS, P // 2])
    masks_i = sb("masks_i", [P, LEVELS, P // 2], I32)
    eps6 = sb("eps6", [P, 1])
    eps5 = sb("eps5", [P, 1])
    raw = sb("raw", [P, 3, 2, T + 3])
    conv = sb("conv", [P, 3, SEG])
    act_out = sb("act_out", [P, 3, SEG])
    sq = sb("sq", [P, 2, SEG])
    rn = sb("rn", [P, 2, SEG])
    z = sb("z", [P, SEG])
    tail = sb("tail", [P, SEG])
    low = sb("low", [P, SEG])
    kn = sb("kn", [P, SEG])
    vals = sb("vals", [P, 2, CH, KW])
    sgate = sb("sgate", [P, 2, SEG])
    qn = sb("qn", [P, 2, SEG])
    kq = sb("kq", [P, 2, SEG])
    kqp = sb("kqp", [P, 2, 2, SEG])
    e = sb("e", [P, 2, 2 * SEG])
    ct = sb("ct", [P, LEVELS, CH, P])
    ysb = sb("ysb", [P, LEVELS, CH, P])
    bt = sb("bt", [P, CH, P])
    tm = sb("tm", [P, CH, P])
    xm = sb("xm", [P, CH, P])
    cross = sb("cross", [P, 2, 2, P])
    u = sb("u", [P, CH, KW])
    rest = sb("rest", [P, 2, KW])
    osq = sb("osq", [P, SEG])
    orn = sb("orn", [P, SEG])
    og = sb("og", [P, SEG])
    names = ("const zeroed w_loaded decay_set proj_done raw_kept g_done z_done tail_done low_done ln1_done sp_done a_done gt_done "
             "sg_done tap silu_done vt_done v_kept beta_done sq_done ssq_done ln_done rn_done kn_done kq_done dg_done "
             "ab_done ct_done bt_done upq upp e_done y_done yk d_done tx_done t_init x_done x_kept u_done u_kept "
             "r_done rs_done o_done osq_done oss_done or_ln or_done og_mul og_done out_done xadd").split()
    s = {n: c.sem("kda_" + n) for n in names}
    e_at = [0]
    for lv in range(LEVELS):
        e_at.append(e_at[-1] + (SEG >> lv))

    with own, nc.Block() as block:

        @block.sync
        def _(sp):
            sp.dma_start(o_norm[:], w["o_norm"]).then_inc(s["const"], 16)
            sp.dma_start(masks[:], w["masks"]).then_inc(s["const"], 16)
            with nc.sync.Fori(0, KH) as i:
                sp.wait_ge(s["xadd"], i * 4 + 1)
                for t, n, how in ((wqkv, "qkv", "o p k g m -> p (o k) g m"), (wfg2, "fg2", "o p g m -> p (o g) m"),
                                  (wo, "o", "o p m -> p (o m)"), (taps, "taps", "o p g m -> p (o g) m"),
                                  (dt_bias, "dt_bias", "o p m -> p (o m)"), (sel, "sel", "o p m -> p (o m)")):
                    sp.dma_start(t[:], w[n][bass.ds(i, 1)].rearrange(how)).then_inc(s["w_loaded"], 16)

        def front_pe(pe, i, n, piece):
            cols = slice(SEG * n, SEG * (n + 1))
            if piece == 0:
                pe.wait_ge(s["ln_done"], i * 4 + n + 1)
                pe.wait_ge(s["kq_done"], i * 4 + n + 1)
                for g in range(3):
                    for k in range(KD):
                        last = nc.tensor.matmul(c.bank[:, g, :], wqkv[:, k, g, :], c.x_t[:, k, cols],
                                                start=k == 0, stop=k == 1)
                last.then_inc(s["proj_done"], 1)
                pe.wait_ge(s["sg_done"], i * 4 + n + 1)
                nc.tensor.matmul(c.bank[:, 3, :], wfg2[:, 0, :], xf_t[:, cols], start=True, stop=True
                                 ).then_inc(s["g_done"], 1)
            elif piece == 1:
                pe.wait_ge(s["z_done"], i * 4 + n + 1)
                nc.tensor.matmul(c.bank[:, 3, :], wfg2[:, 1, :], xg_t[:, cols], start=True, stop=True
                                 ).then_inc(s["gt_done"], 1)
            elif piece == 3:
                pe.wait_ge(s["silu_done"], i * 4 + n + 2)
                for j in range(CH):
                    last = nc.tensor.transpose(c.bank[:, 2, P * j:P * (j + 1)], act_out[:, 2, P * j:P * (j + 1)],
                                               c.ident[:])
                last.then_inc(s["vt_done"], 1)
                pe.wait_ge(s["sq_done"], i * 4 + n + 1)
                for g in range(2):
                    last = nc.tensor.matmul(c.bank[:, g, :], c.ones[:], sq[:, g, :], start=True, stop=True)
                last.then_inc(s["ssq_done"], 1)
            elif piece == 4:
                pe.wait_ge(s["v_kept"], i * 4 + n + 1)
                nc.tensor.matmul(c.bank[:, 2, :], sel[:], beta[:, cols], start=True, stop=True
                                 ).then_inc(s["beta_done"], 1)

        def pairs(pe, i, n, lv):
            pr = n % 2
            if lv:
                pe.wait_ge(s["upq"], i * 28 + 7 * n + lv)
                pe.wait_ge(s["upp"], i * 28 + 7 * n + lv)
                pe.wait_ge(s["bt_done"], i * 32 + 8 * n + lv)
            for ch in range(CH):
                right = halves_of(kqp[:, pr, :, P * ch:P * (ch + 1)], 1 << lv, 1)
                last = nc.tensor.matmul(c.bank[:, 4 + (lv + 1) % 2, P * ch:P * (ch + 1)], kq[:, pr, P * ch:P * (ch + 1)],
                                        right, start=True, stop=True)
            last.then_inc(s["ab_done"], 1)

        def core_pe(pe, i, n, front):
            pr = n % 2
            pe.wait_ge(s["kq_done"], i * 4 + n + 2)
            pe.wait_ge(s["og_done"], i * 4 + n + 2)
            for ch in range(CH):
                last = nc.tensor.matmul(c.bank[:, 4, P * ch:P * (ch + 1)], kq[:, pr, P * ch:P * (ch + 1)],
                                        qn[:, pr, P * ch:P * (ch + 1)], start=True, stop=True)
            last.then_inc(s["dg_done"], 1)
            pairs(pe, i, n, 0)
            pe.wait_ge(s["xadd"], i * 4 + n + 1)
            for lv in range(LEVELS):
                if lv + 1 < LEVELS:
                    pairs(pe, i, n, lv + 1)
                pe.wait_ge(s["ct_done"], i * 28 + 7 * n + lv + 1)
                if lv:
                    pe.wait_ge(s["tx_done"], i * 28 + 7 * n + lv)
                for ch in range(CH):
                    left = c.ident[:] if lv == 0 else tm[:, ch, :]
                    last = nc.tensor.matmul(c.bank[:, 6, 64 * ch:64 * ch + 64], ct[:, lv, ch, :],
                                            halves_of(left, 1 << lv, 0), start=True, stop=True)
                last.then_inc(s["y_done"], 1)
                front(lv)
                if lv:
                    pe.wait_ge(s["yk"], i * 24 + 6 * n + lv)
                    for ch in range(CH):
                        if lv + 1 < LEVELS:
                            nc.tensor.matmul(c.bank[:, 7, 64 * ch:64 * ch + 64], xm[:, ch, :],
                                             halves_of(ysb[:, lv, ch, :], 1 << lv, 0), start=True, stop=True)
                        last = nc.tensor.matmul(c.bank[:, 7, 256 + 64 * ch:320 + 64 * ch], ysb[:, lv, ch, :],
                                                halves_of(xm[:, ch, :], 1 << lv, 1), start=True, stop=True)
                    last.then_inc(s["d_done"], 1)
            pe.wait_ge(s["upq"], i * 28 + 7 * n + 7)
            pe.wait_ge(s["upp"], i * 28 + 7 * n + 7)
            pe.wait_ge(s["bt_done"], i * 32 + 8 * n + 7)
            for b in range(2):
                last = nc.tensor.matmul(c.bank[:, 4, 2 * P * b:2 * P * (b + 1)],
                                        kq[:, pr, 2 * P * b:2 * P * b + P],
                                        kqp[:, pr, :, 2 * P * b + P:2 * P * (b + 1)], start=True, stop=True)
            last.then_inc(s["x_done"], 1)
            pe.wait_ge(s["tx_done"], i * 28 + 7 * n + 7)
            pe.wait_ge(s["v_kept"], i * 4 + n + 1)
            pe.wait_ge(s["bt_done"], i * 32 + 8 * n + 8)
            for b in range(2):
                last = nc.tensor.matmul(c.bank[:, 5, P * b:P * (b + 1)], xm[:, 2 * b, :], vals[:, pr, 2 * b, :],
                                        start=True, stop=True)
            last.then_inc(s["u_done"], 1)
            pe.wait_ge(s["x_kept"], i * 4 + n + 1)
            pe.wait_ge(s["u_kept"], i * 8 + 2 * n + 1)
            for b in range(2):
                last = nc.tensor.matmul(c.bank[:, 6, P * b:P * (b + 1)], cross[:, b, 0, :], u[:, 2 * b, :],
                                        start=True, stop=True)
            last.then_inc(s["r_done"], 1)
            pe.wait_ge(s["rs_done"], i * 4 + n + 1)
            for b in range(2):
                last = nc.tensor.matmul(c.bank[:, 7, P * b:P * (b + 1)], xm[:, 2 * b + 1, :], rest[:, b, :],
                                        start=True, stop=True)
            last.then_inc(s["u_done"], 1)
            pe.wait_ge(s["u_kept"], i * 8 + 2 * n + 2)
            for b in range(2):
                nc.tensor.matmul(c.bank[:, 4, 2 * P * b:2 * P * b + P], u[:, 2 * b, :], bt[:, 2 * b, :],
                                 start=True, stop=True)
                o1 = c.bank[:, 4, 2 * P * b + P:2 * P * (b + 1)]
                nc.tensor.matmul(o1, u[:, 2 * b, :], cross[:, b, 1, :], start=True, stop=False)
                last = nc.tensor.matmul(o1, u[:, 2 * b + 1, :], bt[:, 2 * b + 1, :], start=False, stop=True)
            last.then_inc(s["o_done"], 1)
            pe.wait_ge(s["osq_done"], i * 4 + n + 1)
            nc.tensor.matmul(c.bank[:, 5, :], c.ones[:], osq[:], start=True, stop=True).then_inc(s["oss_done"], 1)
            pe.wait_ge(s["og_done"], i * 4 + n + 3)
            for ch in range(CH):
                last = nc.tensor.matmul(c.bank[:, 6 + ch // 2, D * (ch % 2):D * (ch % 2 + 1)],
                                        og[:, P * ch:P * (ch + 1)], wo[:], start=True, stop=True)
            last.then_inc(s["out_done"], 1)

        def segments(i, front, core):
            for piece in range(LEVELS):
                front(i, 0, piece)
            for n in range(NSEG):
                core(i, n, lambda piece: front(i, n + 1, piece) if n + 1 < NSEG else None)

        @block.tensor
        def _(pe):
            pe.wait_ge(s["const"], 32)
            pe.wait_ge(s["zeroed"], 2)
            pe.sem_inc(s["y_done"], 1)
            with nc.tensor.Fori(0, KH) as i:
                pe.wait_ge(s["w_loaded"], i * 96 + 96)
                segments(i, lambda *a: front_pe(pe, *a), lambda *a: core_pe(pe, *a))

        def front_act(act, i, n, piece):
            pr = n % 2
            if piece == 0:
                act.wait_ge(s["proj_done"], i * 4 + n + 1)
                nc.scalar.activation(raw[:, :, :, 3:], c.bank[:, 0:3, :].rearrange("p g (b t) -> p g b t", b=2),
                                     ACT.Copy).then_inc(s["raw_kept"], 1)
                act.wait_ge(s["g_done"], i * 4 + n + 1)
                nc.scalar.activation(z[:], c.bank[:, 3, :], ACT.Identity, bias=dt_bias[:, 0:1]
                                     ).then_inc(s["z_done"], 1)
                act.wait_ge(s["z_done"], i * 4 + n + 1)
                nc.scalar.activation(tail[:], z[:], ACT.Abs).then_inc(s["tail_done"], 1)
                act.wait_ge(s["tail_done"], i * 8 + 2 * n + 1)
                nc.scalar.activation(tail[:], tail[:], ACT.Exp, scale=-1.0).then_inc(s["tail_done"], 1)
            elif piece == 1:
                act.wait_ge(s["low_done"], i * 8 + 2 * n + 2)
                nc.scalar.activation(low[:], low[:], ACT.Ln, bias=1.0).then_inc(s["ln1_done"], 1)
            elif piece == 2:
                act.wait_ge(s["tap"], i * 16 + 4 * n + 4)
                act.wait_ge(s["kq_done"], i * 4 + n + 1)
                nc.scalar.activation(act_out[:], conv[:], ACT.Silu).then_inc(s["silu_done"], 1)
                act.wait_ge(s["silu_done"], i * 4 + n + 2)
                nc.scalar.activation(sq[:], act_out[:, 0:2, :], ACT.Square).then_inc(s["sq_done"], 1)
            elif piece == 3:
                act.wait_ge(s["sp_done"], i * 8 + 2 * n + 2)
                act.wait_ge(s["og_done"], i * 4 + n + 1)
                nc.scalar.activation(e[:, pr, 0:SEG], z[:], ACT.Exp, scale=decay[:, 0:1]).then_inc(s["a_done"], 1)
                act.wait_ge(s["vt_done"], i * 4 + n + 1)
                nc.scalar.activation(vals[:, pr].rearrange("p c v -> p (c v)"), c.bank[:, 2, :], ACT.Copy
                                     ).then_inc(s["v_kept"], 1)
                act.wait_ge(s["gt_done"], i * 4 + n + 1)
                nc.scalar.activation(sgate[:, pr, :], c.bank[:, 3, :], ACT.Sigmoid).then_inc(s["sg_done"], 1)
            elif piece == 4:
                act.wait_ge(s["ssq_done"], i * 4 + n + 1)
                nc.scalar.activation(rn[:], c.bank[:, 0:2, :], ACT.Ln, bias=eps6[:, 0:1]).then_inc(s["ln_done"], 1)
                act.wait_ge(s["ln_done"], i * 4 + n + 2)
                nc.scalar.activation(rn[:], rn[:], ACT.Exp, scale=-0.5).then_inc(s["rn_done"], 1)

        def core_act(act, i, n, front):
            for lv in range(LEVELS):
                if lv:
                    act.wait_ge(s["y_done"], i * 28 + 7 * n + lv + 2)
                    nc.scalar.activation(halves_of(ysb[:, lv], 1 << lv, 0),
                                         c.bank[:, 6, 0:256].rearrange("p (c g m) -> p c g m", c=CH, m=1 << lv),
                                         ACT.Copy).then_inc(s["yk"], 1)
                front(lv)
            act.wait_ge(s["x_done"], i * 4 + n + 1)
            nc.scalar.activation(cross[:].rearrange("p b g t -> p (b g t)"), c.bank[:, 4, :], ACT.Copy
                                 ).then_inc(s["x_kept"], 1)
            for half in range(2):
                act.wait_ge(s["u_done"], i * 8 + 2 * n + half + 1)
                nc.scalar.activation(u[:, half:CH:2, :],
                                     c.bank[:, 5 + 2 * half, 0:256].rearrange("p (b v) -> p b v", b=2), ACT.Copy
                                     ).then_inc(s["u_kept"], 1)
            act.wait_ge(s["o_done"], i * 4 + n + 1)
            nc.scalar.activation(osq[:], c.bank[:, 4, :], ACT.Square).then_inc(s["osq_done"], 1)
            act.wait_ge(s["oss_done"], i * 4 + n + 1)
            nc.scalar.activation(orn[:], c.bank[:, 5, :], ACT.Ln, scale=1.0 / KW, bias=eps5[:, 0:1]
                                 ).then_inc(s["or_ln"], 1)
            act.wait_ge(s["or_ln"], i * 4 + n + 1)
            nc.scalar.activation(orn[:], orn[:], ACT.Exp, scale=-0.5).then_inc(s["or_done"], 1)

        @block.scalar
        def _(act):
            act.sem_inc(s["ln_done"], 1)
            act.sem_inc(s["sg_done"], 1)
            act.sem_inc(s["silu_done"], 1)
            act.wait_ge(s["zeroed"], 2)
            with nc.scalar.Fori(0, KH) as i:
                act.wait_ge(s["w_loaded"], i * 96 + 96)
                act.wait_ge(s["decay_set"], i + 1)
                segments(i, lambda *a: front_act(act, *a), lambda *a: core_act(act, *a))

        def front_dve(dve, i, n, piece):
            pr = n % 2
            if piece == 0:
                dve.wait_ge(s["raw_kept"], i * 4 + n + 1)
                dve.wait_ge(s["silu_done"], i * 4 + n + 1)
            for step in {0: (0, 1), 1: (2, 3)}.get(piece, ()):
                tap = 3 - step
                if step:
                    dve.wait_ge(s["tap"], i * 16 + 4 * n + step)
                for g in range(3):
                    out = conv[:, g, :].rearrange("p (b t) -> p b t", b=2)
                    src = raw[:, g, :, tap:tap + T]
                    if step == 0:
                        last = nc.vector.tensor_scalar(out, src, taps[:, g, 3:4], taps[:, g, 4:5], ALU.mult, ALU.add)
                    else:
                        last = nc.vector.scalar_tensor_tensor(out, src, taps[:, g, tap:tap + 1], out, ALU.mult,
                                                              ALU.add)
                last.then_inc(s["tap"], 1)
            if piece == 1:
                dve.wait_ge(s["tail_done"], i * 8 + 2 * n + 2)
                nc.vector.tensor_scalar(low[:], tail[:], 1.0, 1.0, ALU.add, ALU.subtract).then_inc(s["low_done"], 1)
                dve.wait_ge(s["low_done"], i * 8 + 2 * n + 1)
                nc.vector.tensor_tensor(tail[:], tail[:], low[:], ALU.subtract).then_inc(s["low_done"], 1)
            if piece == 2:
                dve.wait_ge(s["ln1_done"], i * 4 + n + 1)
                nc.vector.scalar_tensor_tensor(z[:], z[:], 0.0, low[:], ALU.max, ALU.add).then_inc(s["sp_done"], 1)
                dve.wait_ge(s["sp_done"], i * 8 + 2 * n + 1)
                nc.vector.tensor_tensor(z[:], z[:], tail[:], ALU.add).then_inc(s["sp_done"], 1)
            if piece == 5:
                dve.wait_ge(s["rn_done"], i * 4 + n + 1)
                nc.vector.tensor_tensor(kn[:], act_out[:, 1, :], rn[:, 1, :], ALU.mult)
                nc.vector.scalar_tensor_tensor(qn[:, pr, :], act_out[:, 0, :], KW ** -0.5, rn[:, 0, :], ALU.mult,
                                               ALU.mult).then_inc(s["kn_done"], 1)
                dve.wait_ge(s["kn_done"], i * 4 + n + 1)
                dve.wait_ge(s["a_done"], i * 4 + n + 1)
                nc.vector.tensor_tensor(kqp[:, pr, 0, :], kn[:], e[:, pr, 0:SEG], ALU.mult)
                nc.vector.tensor_tensor(kqp[:, pr, 1, :], qn[:, pr, :], e[:, pr, 0:SEG], ALU.mult)
                dve.wait_ge(s["beta_done"], i * 4 + n + 1)
                nc.vector.tensor_tensor(kq[:, pr, :], kn[:], c.bank[:, 2, :], ALU.mult).then_inc(s["kq_done"], 1)

        def level_dve(dve, i, n, lv):
            pr, m = n % 2, 1 << lv
            dve.wait_ge(s["bt_done"], i * 32 + 8 * n + lv + 1)
            dve.wait_ge(s["ab_done"], i * 28 + 7 * n + lv + 1)
            ab = c.bank[:, 4 + (lv + 1) % 2, :].rearrange("p (c two g m) -> p c two g m", two=2, c=CH, m=m)
            mask = masks[:, lv, :].unsqueeze(1).broadcast_to([P, CH, 64]).rearrange("p c (g m) -> p c g m", m=m)
            mask_i = masks_i[:, lv, :].unsqueeze(1).broadcast_to([P, CH, 64]).rearrange("p c (g m) -> p c g m", m=m)
            nc.vector.tensor_tensor(halves_of(ct[:, lv], m, 1), ab[:, :, 0], mask, ALU.mult).then_inc(s["ct_done"], 1)
            nc.vector.copy_predicated(halves_of(bt[:], m, 1), mask_i, ab[:, :, 1]).then_inc(s["bt_done"], 1)
            if lv:
                dve.wait_ge(s["e_done"], i * 24 + 6 * n + lv)
                dve.wait_ge(s["upq"], i * 28 + 7 * n + lv)
            g = SEG >> (lv + 1)
            pairs_e = e[:, pr, e_at[lv]:e_at[lv + 1]].rearrange("p (g two) -> p g two", two=2)
            left = halves_of(kq[:, pr, :], m, 0)
            nc.vector.tensor_tensor(left, left, pairs_e[:, :, 1:2].broadcast_to([P, g, m]), ALU.mult
                                    ).then_inc(s["upq"], 1)
            if lv + 1 < LEVELS:
                nc.vector.tensor_tensor(e[:, pr, e_at[lv + 1]:e_at[lv + 1] + g], pairs_e[:, :, 0], pairs_e[:, :, 1],
                                        ALU.mult).then_inc(s["e_done"], 1)

        def inverse_dve(dve, i, n, lv):
            m = 1 << lv
            eye = c.ident[:].unsqueeze(1).broadcast_to([P, CH, P])
            if lv == 0:
                dve.wait_ge(s["ct_done"], i * 28 + 7 * n + 1)
                nc.vector.tensor_tensor(xm[:], eye, ct[:, 0], ALU.subtract)
                dve.wait_ge(s["t_init"], i * 4 + n + 1)
                dve.wait_ge(s["y_done"], i * 28 + 7 * n + 2)
                left = halves_of(tm[:], m, 0)
                y = c.bank[:, 6, 0:256].rearrange("p (c g m) -> p c g m", c=CH, m=m)
                nc.vector.tensor_tensor(left, left, y, ALU.subtract).then_inc(s["tx_done"], 1)
                return
            dve.wait_ge(s["tx_done"], i * 28 + 7 * n + lv)
            dve.wait_ge(s["d_done"], i * 24 + 6 * n + lv)
            dt_, dx = (c.bank[:, 7, 256 * k:256 * (k + 1)].rearrange("p (c g m) -> p c g m", c=CH, m=m)
                       for k in range(2))
            if lv + 1 < LEVELS:
                left = halves_of(tm[:], m, 0)
                nc.vector.tensor_tensor(left, left, dt_, ALU.subtract)
            right = halves_of(xm[:], m, 1)
            nc.vector.tensor_tensor(right, right, dx, ALU.subtract).then_inc(s["tx_done"], 1)

        def core_dve(dve, i, n, front):
            pr = n % 2
            dve.wait_ge(s["dg_done"], i * 4 + n + 1)
            nc.vector.tensor_tensor(bt[:], c.bank[:, 4, :].rearrange("p (c t) -> p c t", c=CH),
                                    c.ident[:].unsqueeze(1).broadcast_to([P, CH, P]), ALU.mult
                                    ).then_inc(s["bt_done"], 1)
            level_dve(dve, i, n, 0)
            for lv in range(LEVELS):
                if lv + 1 < LEVELS:
                    level_dve(dve, i, n, lv + 1)
                inverse_dve(dve, i, n, lv)
                front(lv)
            dve.wait_ge(s["r_done"], i * 4 + n + 1)
            nc.vector.tensor_tensor(rest[:], vals[:, pr, 1:CH:2, :],
                                    c.bank[:, 6, 0:256].rearrange("p (b v) -> p b v", b=2), ALU.subtract
                                    ).then_inc(s["rs_done"], 1)
            dve.wait_ge(s["or_done"], i * 4 + n + 1)
            nc.vector.tensor_tensor(og[:], c.bank[:, 4, :], orn[:], ALU.mult).then_inc(s["og_mul"], 1)
            dve.wait_ge(s["og_mul"], i * 4 + n + 1)
            dve.wait_ge(s["sg_done"], i * 4 + n + 2)
            nc.vector.scalar_tensor_tensor(og[:], og[:], o_norm[:, 0:1], sgate[:, pr, :], ALU.mult, ALU.mult
                                           ).then_inc(s["og_done"], 1)
            dve.wait_ge(s["out_done"], i * 4 + n + 1)
            x = c.x_tok[:, 4 * n:4 * n + 4, :].rearrange("p t d -> p (t d)")
            nc.vector.tensor_tensor(x, x, c.bank[:, 6:8, :].rearrange("p k n -> p (k n)"), ALU.add
                                    ).then_inc(s["xadd"], 1)

        @block.vector
        def _(dve):
            dve.sem_inc(s["kq_done"], 1)
            dve.sem_inc(s["og_done"], 2)
            dve.sem_inc(s["xadd"], 1)
            nc.vector.memset(eps6[:], 1e-6)
            nc.vector.memset(eps5[:], 1e-5)
            nc.vector.memset(raw[:, :, :, 0:3], 0.0)
            nc.vector.memset(ct[:], 0.0)
            nc.vector.memset(ysb[:], 0.0).then_inc(s["zeroed"], 1)
            dve.wait_ge(s["const"], 32)
            nc.vector.tensor_copy(masks_i[:], masks[:]).then_inc(s["zeroed"], 1)
            dve.wait_ge(s["zeroed"], 2)
            with nc.vector.Fori(0, KH) as i:
                dve.wait_ge(s["w_loaded"], i * 96 + 96)
                nc.vector.tensor_copy(decay[:], neg_a[:, bass.ds(i, 1)]).then_inc(s["decay_set"], 1)
                segments(i, lambda *a: front_dve(dve, *a), lambda *a: core_dve(dve, *a))

        @block.gpsimd
        def _(pool):
            def core(i, n, front):
                pr = n % 2
                pool.wait_ge(s["y_done"], i * 28 + 7 * n + 1)
                nc.gpsimd.tensor_tensor(tm[:], c.ident[:].unsqueeze(1).broadcast_to([P, CH, P]),
                                        c.ident[:].unsqueeze(1).broadcast_to([P, CH, P]), ALU.mult
                                        ).then_inc(s["t_init"], 1)
                for lv in range(LEVELS):
                    m = 1 << lv
                    if lv:
                        pool.wait_ge(s["e_done"], i * 24 + 6 * n + lv)
                    pool.wait_ge(s["ab_done"], i * 28 + 7 * n + lv + 1)
                    g = SEG >> (lv + 1)
                    factor = e[:, pr, e_at[lv]:e_at[lv + 1]].rearrange("p (g two) -> p g two", two=2)[:, :, 0:1]
                    for k in range(2):
                        right = halves_of(kqp[:, pr, k, :], m, 1)
                        last = nc.gpsimd.tensor_tensor(right, right, factor.broadcast_to([P, g, m]), ALU.mult)
                    last.then_inc(s["upp"], 1)

            with nc.gpsimd.Fori(0, KH) as i:
                for n in range(NSEG):
                    core(i, n, None)


def host_layout(a):
    f = {}

    def cols(m):
        m = np.asarray(m)
        return np.ascontiguousarray(m.reshape(m.shape[0] // P, P, m.shape[1]).transpose(1, 0, 2))

    x = np.asarray(a["x"])
    f["x_tok"] = x.reshape(NT, P, D).transpose(1, 0, 2)
    f["x_t"] = x.reshape(TOK, KD, P).transpose(2, 1, 0)
    f["ident"] = np.eye(P, dtype=np.float32)
    L = {k[8:]: np.asarray(v) for k, v in a.items() if k.startswith("L0_attn_")}
    f["ssm_dt_lam"] = np.stack([cols(L["Wdt"].T), cols(L["Wlam"].T)], axis=2)
    f["ssm_A_log"] = L["A_log"].reshape(SH, 1)
    f["ssm_x"] = cols(L["Wx"].T)
    f["ssm_z"] = cols(L["Wz"].T)
    f["ssm_out"] = cols(L["Wout"].T)

    def pair_rows(m):
        return m.reshape(PAIRS, 2, 64, 2, D).transpose(0, 3, 1, 2, 4).reshape(PAIRS, 2, P, D)

    rows = np.concatenate([L["Wth"].reshape(PAIRS, 1, P, D), pair_rows(L["WB"]), pair_rows(L["WC"])], axis=1)
    f["ssm_pair"] = rows.reshape(PAIRS, 5, P, KD, P).transpose(0, 4, 3, 1, 2)
    b = [L[k].reshape(PAIRS, 2, 64, 2).transpose(0, 3, 1, 2).reshape(PAIRS, 2, P) for k in ("B_bias", "C_bias")]
    f["ssm_bias"] = np.concatenate(b, axis=1).transpose(2, 0, 1)
    f["ssm_norm_w"] = np.stack([np.tile(L[k][j::2], 2) for k in ("Bn_w", "Cn_w") for j in range(2)], axis=1)
    f["ssm_above"] = np.eye(P, P + 1, 1, dtype=np.float32)
    f["ssm_halves"] = np.kron(np.eye(2, dtype=np.float32), np.ones((64, 64), np.float32))
    ctx_t = np.asarray(a["ctx_1024"]).reshape(B * S2, DC).T
    mask = np.asarray(a["mask_BxS2_bf1"]).view(np.uint8)
    for tag, name in (("xm_", "L0_xattn_"), ("xn_", "L1_xattn_")):
        L = {k[len(name):]: np.asarray(v) for k, v in a.items() if k.startswith(name)}
        f[tag + "ctx"] = ctx_t
        f[tag + "q"] = cols(L["Wq"])
        f[tag + "o"] = cols(L["Wo"])
        f[tag + "k"] = L["Wk"]
        f[tag + "v"] = L["Wv"].reshape(DC, 1, -1) if tag == "xm_" else (
            L["Wv"].reshape(DC, XP, 2, XD).transpose(0, 2, 1, 3).reshape(DC, 2, XP * XD))
    f["xn_g"] = np.stack([L["gk"], L["gq"]], axis=1)
    f["xm_mask_row"] = mask.reshape(B * S2)
    f["xm_mask_col"] = np.concatenate([mask.T, mask.T])
    L = {k[7:]: np.asarray(v) for k, v in a.items() if k.startswith("L0_ffn_")}
    f["had_rows"] = np.concatenate([L[k].reshape(HID0 // P, P, D) for k in ("W_gate", "W_up")]).transpose(1, 0, 2)
    f["had_down"] = L["W_down"].reshape(KD, P, HID0).transpose(1, 0, 2)
    f["had_su_in"] = L["SU_ug"].reshape(KD, P).T
    f["had_su_out"] = L["SU_dp"].reshape(HID0 // P, P).T
    f["had_down_scale"] = L["Wscale_dp"].reshape(KD, P).T
    f["had_scales"] = L["Wscale_ug"].reshape(2, HID0 // P, P)[::-1].transpose(2, 0, 1)
    L = {k[7:]: np.asarray(v) for k, v in a.items() if k.startswith("L1_ffn_")}
    f["deq_in"] = np.stack([cols(L["wq_gate"].T), cols(L["wq_up"].T)], axis=2)
    f["deq_out"] = L["wq_down"].T
    f["deq_s_down"] = L["s_down"]
    f["deq_s_gate"] = L["s_gate"].reshape(HID1, 1)
    f["deq_s_up"] = L["s_up"].reshape(HID1, 1)
    L = {k[8:]: np.asarray(v) for k, v in a.items() if k.startswith("L1_attn_")}

    def by_head(m):
        return m.reshape(m.shape[0], KH, KW).transpose(1, 0, 2)

    f["kda_fg"] = np.stack([cols(L["Wfa"]), cols(L["Wga"])], axis=2)
    f["kda_b"] = cols(L["Wb"])
    f["kda_A_log"] = L["A_log"]
    f["kda_o_norm"] = L["o_norm_w"].reshape(KW, 1)
    f["kda_qkv"] = np.stack([by_head(L[k]) for k in ("Wq", "Wk", "Wv")], axis=2).reshape(
        KH, KD, P, 3, KW).transpose(0, 2, 1, 3, 4)
    f["kda_fg2"] = np.stack([by_head(L["Wfb"]), by_head(L["Wgb"])], axis=2)
    f["kda_o"] = L["Wo"].reshape(KH, KW, D)
    f["kda_taps"] = np.stack([np.concatenate([L[f"conv_{g}_w"], L[f"conv_{g}_b"][:, None]], axis=1).reshape(
        KH, KW, 5) for g in "qkv"], axis=2)
    f["kda_dt_bias"] = L["dt_bias"].reshape(KH, KW, 1)
    f["kda_sel"] = np.repeat(np.eye(KH, dtype=np.float32)[:, :, None], P, axis=2)
    masks = np.zeros((P, LEVELS, P // 2), np.float32)
    for lv in range(LEVELS):
        m = 1 << lv
        right = np.arange(P).reshape(-1, 2, m)[:, 1].ravel()
        rows = np.arange(P)
        masks[:, lv] = (rows[:, None] // (2 * m) == right[None, :] // (2 * m)) & ((rows[:, None] // m) % 2 == 0)
    f["kda_masks"] = masks
    return {k: np.ascontiguousarray(v) for k, v in f.items()}


def part(d, prefix):
    return {k[len(prefix):]: v for k, v in d.items() if k.startswith(prefix)}


def program(nc, d, out_d, only=None):
    with ExitStack() as ctx:
        c = Core(nc, ctx)
        load_start(c, d["x_tok"], d["x_t"], d["ident"])
        layers = [
            (ssm, "ssm_"),
            (lambda c, w: cross_attention(c, w, False), "xm_"),
            (hadamard_ffn, "had_"),
            (kda, "kda_"),
            (lambda c, w: cross_attention(c, w, True), "xn_"),
            (dequant_ffn, "deq_"),
        ]
        for n, (layer, prefix) in enumerate(layers):
            if only is None or n == only:
                layer(c, part(d, prefix))
                last = len(layers) - 1 if only is None else only
                layer_norm(c, f"norm{n}", out_d if n == last else None)
                if n != last:
                    c.release_sems()
        c.sems.close()


def kernel(**inputs):
    from concourse import bacc
    from concourse.bass_utils import run_bass_kernel_spmd

    nc = bacc.Bacc("TRN2", target_bir_lowering=False, num_devices=1)
    arrays = host_layout(inputs)
    d = {k: nc.dram_tensor("in_" + k, v.shape, mybir.dt.from_np(v.dtype), kind="ExternalInput").ap()
         for k, v in arrays.items()}
    out = nc.dram_tensor("out_x", (P, NT, D), F32, kind="ExternalOutput").ap()
    program(nc, d, out)
    r = run_bass_kernel_spmd(nc, [{"in_" + k: v for k, v in arrays.items()}], core_ids=[0])
    return np.asarray(r.results[0]["out_x"]).transpose(1, 0, 2).reshape(B, T, D)
```

```python
from contextlib import ExitStack

import numpy as np

import concourse.bass as bass
from concourse import mybir

F32 = mybir.dt.float32
I32 = mybir.dt.int32
U8 = mybir.dt.uint8
ALU = mybir.AluOpType
ACT = mybir.ActivationFunctionType
AX = mybir.AxisListType

P = 128
B, T, D = 8, 256, 256
TOK = B * T
NT = TOK // P
KD = D // P
SEG = 512
NSEG = TOK // SEG
S2, DC = 64, 128
PI = 3.1415925
HALF_PI = 1.5707963267948966


class Core:

    def __init__(self, nc, ctx):
        self.nc, self.ctx = nc, ctx
        self.held, self.sems = [], ExitStack()
        self.x_tok = self.sbuf("x_tok", [P, NT, D])
        self.x_t = self.sbuf("x_t", [P, KD, TOK])
        self.ident = self.sbuf("ident", [P, P])
        self.ones = self.sbuf("ones", [P, P])
        self.bank = ctx.enter_context(nc.psum_tensor("bank", [P, 8, 512], F32))

    def sbuf(self, name, shape, dt=F32, ctx=None):
        return (ctx or self.ctx).enter_context(self.nc.sbuf_tensor(name, shape, dt))

    def sem(self, name):
        self.held.append(self.sems.enter_context(self.nc.semaphore(name)))
        return self.held[-1]

    def release_sems(self):
        with self.nc.Block() as block:

            @block.sync
            def _(sp):
                for held in self.held:
                    sp.sem_clear(held)

        self.sems.close()
        self.held, self.sems = [], ExitStack()


def load_start(c, x_tok_d, x_t_d, ident_d, loads):
    nc = c.nc
    loaded = c.sem("start_loaded")
    with nc.Block() as block:

        @block.sync
        def _(sp):
            load_all(sp, [(c.x_tok[:], x_tok_d), (c.x_t[:], x_t_d), (c.ident[:], ident_d), *loads], loaded)

        @block.vector
        def _(dve):
            nc.vector.memset(c.ones[:], 1.0)


def load_all(sp, loads, loaded):
    for place, source in loads:
        sp.dma_start(place, source).then_inc(loaded, 16)
    sp.wait_ge(loaded, 16 * len(loads))


def layer_norm(c, tag, out_d=None, loads=()):
    nc = c.nc
    own = ExitStack()
    stats = c.sbuf(tag + "_stats", [P, NT, 6], ctx=own)
    mean_var = c.sbuf(tag + "_mean_var", [P, NT, 2], ctx=own)
    std = c.sbuf(tag + "_std", [P, NT], ctx=own)
    rstd = c.sbuf(tag + "_rstd", [P, NT], ctx=own)
    eps = c.sbuf(tag + "_eps", [P, 1], ctx=own)
    measured, rooted, scaled, turned, copied, stored, loaded = (
        c.sem(f"{tag}_{n}") for n in ("measured", "rooted", "scaled", "turned", "copied", "stored", "loaded"))
    groups = NT // 4 * KD
    with own, nc.Block() as block:

        @block.vector
        def _(dve):
            nc.vector.memset(eps[:], 1e-5).then_inc(measured, 1)
            for t in range(NT):
                nc.vector.bn_stats(stats[:, t, :], c.x_tok[:, t, :]).then_inc(measured, 1)
            for t in range(NT):
                dve.wait_ge(measured, 2 + t)
                nc.vector.bn_aggr(mean_var[:, t, :], stats[:, t, :]).then_inc(measured, 1)
            dve.wait_ge(rooted, 1)
            nc.vector.reciprocal(rstd[:], std[:]).then_inc(rooted, 1)
            dve.wait_ge(rooted, 2)
            for t in range(NT):
                nc.vector.tensor_scalar(c.x_tok[:, t, :], c.x_tok[:, t, :], mean_var[:, t, 0:1],
                                        rstd[:, t:t + 1], ALU.subtract, ALU.mult).then_inc(scaled, 1)

        @block.scalar
        def _(act):
            act.wait_ge(measured, 1 + 2 * NT)
            nc.scalar.activation(std[:], mean_var[:, :, 1], ACT.Sqrt, bias=eps[:, 0:1]).then_inc(rooted, 1)
            if out_d is None:
                for g in range(groups):
                    q, k = divmod(g, KD)
                    act.wait_ge(turned, g + 1)
                    nc.scalar.activation(c.x_t[:, k, SEG * q:SEG * (q + 1)], c.bank[:, g % 4, :],
                                         ACT.Copy).then_inc(copied, 1)

        if loads:

            @block.sync
            def _(sp):
                load_all(sp, loads, loaded)

        if out_d is None:

            @block.tensor
            def _(pe):
                for g in range(groups):
                    q, k = divmod(g, KD)
                    pe.wait_ge(scaled, 4 * (q + 1))
                    if g >= 4:
                        pe.wait_ge(copied, g - 3)
                    for j in range(4):
                        last = nc.tensor.transpose(c.bank[:, g % 4, P * j:P * (j + 1)],
                                                   c.x_tok[:, 4 * q + j, P * k:P * (k + 1)], c.ident[:])
                    last.then_inc(turned, 1)
        else:

            @block.sync
            def _(sp):
                for q in range(4):
                    sp.wait_ge(scaled, 4 * (q + 1))
                    sp.dma_start(out_d[:, 4 * q:4 * q + 4, :], c.x_tok[:, 4 * q:4 * q + 4, :]).then_inc(stored, 16)
                sp.wait_ge(stored, 64)



SH, SN, SP_ = 64, 128, 8
DIN = SH * SP_
PAIRS = SH // 2
INV_2PI = 0.15915494309189535
ROUND = 12582912.0
DEC = T + P
TWO_PI_HI, TWO_PI_LO = 6.28125, 0.0019353071795864769


def ssm(c, w):
    nc = c.nc
    dt_d = nc.dram_tensor("ssm_dt_rows", (SH, TOK), F32).ap()
    alpha_d = nc.dram_tensor("ssm_alpha_rows", (SH, B, DEC), F32).ap()
    own = ExitStack()
    xh = c.sbuf("xh", [P, NT, DIN], ctx=own)
    y_tok = c.sbuf("y_tok", [P, NT, DIN], ctx=own)
    with own:
        tables = ExitStack()
        yield ()
        beta_tok = c.sbuf("beta_tok", [P, SH, NT], ctx=tables)
        gamma_tok = c.sbuf("gamma_tok", [P, SH, NT], ctx=tables)
        with tables:
            ssm_gates(c, w, xh, dt_d, alpha_d, beta_tok, gamma_tok)
            ssm_heads(c, w, xh, y_tok, dt_d, alpha_d, beta_tok, gamma_tok)
        ssm_output(c, w, y_tok)


def ssm_gates(c, w, xh, dt_d, alpha_d, beta_tok, gamma_tok):
    nc = c.nc
    own = ExitStack()
    dt_t = c.sbuf("dt_t", [SH, TOK], ctx=own)
    alpha_x = c.sbuf("alpha_x", [SH, B, DEC], ctx=own)
    wx = c.sbuf("wx", [P, KD, DIN], ctx=own)
    wdl = c.sbuf("wdl", [P, KD, 2, SH], ctx=own)
    a_log = c.sbuf("a_log", [SH, 1], ctx=own)
    neg_a = c.sbuf("neg_a", [SH, 1], ctx=own)
    tail = c.sbuf("softplus_tail", [SH, SEG], ctx=own)
    low = c.sbuf("softplus_low", [SH, SEG], ctx=own)
    lam = c.sbuf("lam", [SH, SEG], ctx=own)
    rest = c.sbuf("rest", [SH, SEG], ctx=own)
    gamma_t = c.sbuf("gamma_t", [SH, TOK], ctx=own)
    beta_t = c.sbuf("beta_t", [SH, TOK], ctx=own)
    loaded, saved, x_done, x_kept, dl_done, soft, low_done, dt_done, lam_done, gk_done, turned, kept = (
        c.sem("gates_" + n) for n in ("loaded saved x_done x_kept dl_done soft low_done dt_done lam_done gk_done turned "
                                      "kept").split())
    with own, nc.Block() as block:

        @block.sync
        def _(sp):
            sp.dma_start(wdl[:], w["dt_lam"]).then_inc(loaded, 16)
            sp.dma_start(a_log[:], w["A_log"]).then_inc(loaded, 16)
            sp.dma_start(wx[:], w["x"]).then_inc(loaded, 16)
            sp.wait_ge(gk_done, 4 * NSEG + 1)
            sp.dma_start(dt_d, dt_t[:]).then_inc(saved, 16)
            sp.dma_start(alpha_d, alpha_x[:]).then_inc(saved, 16)
            sp.wait_ge(saved, 32)

        @block.tensor
        def _(pe):
            pe.wait_ge(loaded, 48)
            for q in range(NSEG):
                if q:
                    pe.wait_ge(lam_done, 2 * q)
                    pe.wait_ge(dt_done, 2 * q)
                for g in range(2):
                    for k in range(KD):
                        last = nc.tensor.matmul(c.bank[0:SH, 4 + g, :], wdl[:, k, g, :],
                                                c.x_t[:, k, SEG * q:SEG * (q + 1)],
                                                start=k == 0, stop=k == KD - 1)
                last.then_inc(dl_done, 1)
            for t in range(NT):
                if t >= 4:
                    pe.wait_ge(x_kept, t - 3)
                for k in range(KD):
                    last = nc.tensor.matmul(c.bank[:, t % 4, :], c.x_t[:, k, P * t:P * (t + 1)], wx[:, k, :],
                                            start=k == 0, stop=k == KD - 1)
                last.then_inc(x_done, 1)
            for g, source in enumerate((beta_t, gamma_t)):
                for half in range(2):
                    pe.wait_ge(gk_done, 4 * NSEG + 1)
                    for t in range(8 * half, 8 * half + 8):
                        last = nc.tensor.transpose(c.bank[:, 4 + 2 * g + half, SH * (t % 8):SH * (t % 8 + 1)],
                                                   source[:, P * t:P * (t + 1)], c.ident[0:SH, 0:SH])
                    last.then_inc(turned, 1)

        @block.scalar
        def _(act):
            act.wait_ge(loaded, 48)
            nc.scalar.activation(neg_a[:], a_log[:], ACT.Exp).then_inc(soft, 1)
            for q in range(NSEG):
                cols = slice(SEG * q, SEG * (q + 1))
                act.wait_ge(dl_done, q + 1)
                if q:
                    act.wait_ge(gk_done, 4 * q + 1)
                nc.scalar.activation(tail[:], c.bank[0:SH, 4, :], ACT.Abs).then_inc(soft, 1)
                act.wait_ge(soft, 4 * q + 2)
                nc.scalar.activation(tail[:], tail[:], ACT.Exp, scale=-1.0).then_inc(soft, 1)
                act.wait_ge(low_done, 2 * q + 2)
                nc.scalar.activation(low[:], low[:], ACT.Ln, bias=1.0).then_inc(soft, 1)
                nc.scalar.activation(lam[:], c.bank[0:SH, 5, :], ACT.Sigmoid).then_inc(lam_done, 1)
                nc.scalar.activation(rest[:], c.bank[0:SH, 5, :], ACT.Sigmoid, scale=-1.0).then_inc(lam_done, 1)
                act.wait_ge(dt_done, 2 * q + 2)
                act.wait_ge(gk_done, 1)
                nc.scalar.activation(alpha_x[:, 2 * q:2 * q + 2, 0:T],
                                     dt_t[:, cols].rearrange("h (b t) -> h b t", t=T), ACT.Exp,
                                     scale=neg_a[:, 0:1]).then_inc(soft, 1)
            for t in range(NT):
                act.wait_ge(x_done, t + 1)
                nc.scalar.activation(xh[:, t, :], c.bank[:, t % 4, :], ACT.Copy).then_inc(x_kept, 1)
            for j in range(4):
                act.wait_ge(turned, j + 1)
                target = (beta_tok, gamma_tok)[j // 2]
                nc.scalar.activation(target[:, :, 8 * (j % 2):8 * (j % 2) + 8],
                                     c.bank[:, 4 + j, :].rearrange("p (t h) -> p h t", h=SH),
                                     ACT.Copy).then_inc(kept, 1)

        @block.vector
        def _(dve):
            for q in range(NSEG):
                cols = slice(SEG * q, SEG * (q + 1))
                dve.wait_ge(soft, 4 * q + 3)
                nc.vector.tensor_scalar(low[:], tail[:], 1.0, 1.0, ALU.add, ALU.subtract).then_inc(low_done, 1)
                dve.wait_ge(low_done, 2 * q + 1)
                nc.vector.tensor_tensor(tail[:], tail[:], low[:], ALU.subtract).then_inc(low_done, 1)
                dve.wait_ge(low_done, 2 * q + 2)
                dve.wait_ge(soft, 4 * q + 4)
                nc.vector.scalar_tensor_tensor(dt_t[:, cols], c.bank[0:SH, 4, :], 0.0, low[:], ALU.max,
                                               ALU.add).then_inc(dt_done, 1)
                dve.wait_ge(dt_done, 2 * q + 1)
                nc.vector.tensor_tensor(dt_t[:, cols], dt_t[:, cols], tail[:], ALU.add).then_inc(dt_done, 1)
                if q == 0:
                    nc.vector.tensor_scalar(neg_a[:], neg_a[:], -1.0, None, ALU.mult).then_inc(gk_done, 1)
                dve.wait_ge(dt_done, 2 * q + 2)
                dve.wait_ge(lam_done, 2 * q + 2)
                nc.vector.tensor_tensor(gamma_t[:, cols], lam[:], dt_t[:, cols], ALU.mult).then_inc(gk_done, 1)
                nc.vector.tensor_tensor(rest[:], rest[:], dt_t[:, cols], ALU.mult).then_inc(gk_done, 1)
                dve.wait_ge(gk_done, 4 * q + 3)
                dve.wait_ge(soft, 4 * q + 5)
                r3 = rest[:, :].rearrange("h (b t) -> h b t", t=T)
                alpha = alpha_x[:, 2 * q:2 * q + 2, :]
                nc.vector.tensor_tensor(r3, r3, alpha[:, :, 0:T], ALU.mult).then_inc(gk_done, 1)
                dve.wait_ge(gk_done, 4 * q + 4)
                nc.vector.memset(alpha[:, :, 0:1], 0.0)
                nc.vector.memset(alpha[:, :, T:T + 1], 0.0)
                nc.vector.tensor_copy(alpha[:, :, T + 1:], alpha[:, :, P + 1:T])
                b3 = beta_t[:, cols].rearrange("h (b t) -> h b t", t=T)
                nc.vector.memset(b3[:, :, T - 1:T], 0.0)
                nc.vector.tensor_copy(b3[:, :, 0:T - 1], r3[:, :, 1:T]).then_inc(gk_done, 1)


def ssm_heads(c, w, xh, y_tok, dt_d, alpha_d, beta_tok, gamma_tok):
    nc = c.nc
    own = ExitStack()

    def sb(name, shape, dt=F32):
        return c.sbuf(name, shape, dt, ctx=own)

    w_pair = [sb(f"w_pair{e}", [P, KD, 5, P]) for e in range(2)]
    bias = sb("bc_bias", [P, PAIRS, 4])
    norm_w = sb("bc_norm_w", [P, 4])
    halves = sb("halves", [P, P])
    above = sb("above", [P, P + 1])
    diag = sb("diag", [P, P + 1])
    eps = sb("ssm_eps", [P, 1])
    half_pi = sb("ssm_half_pi", [P, 1])
    bet = sb("bet", [P, 2, 2, NT])
    gam = sb("gam", [P, 2, 2, NT])
    pair_bias = sb("pair_bias", [P, 2, 4])
    dts = sb("dts", [P, SEG])
    alphas = sb("alphas", [P, 2, 2, DEC])
    ang = sb("ang", [P, SEG])
    turns = sb("turns", [P, SEG])
    red = sb("red", [P, SEG])
    sn = sb("sn", [P, 2, SEG])
    cs = sb("cs", [P, 2, SEG])
    sq = sb("sq", [P, 4, SEG])
    rms = sb("rms", [P, 2, SEG])
    nbc = sb("nbc", [P, 4, SEG])
    pr = sb("pr", [P, 4, SEG])
    pq = sb("pool_products", [P, 2, SEG])
    rot = sb("rot", [P, 2, 2, SEG])
    start = sb("start", [P, 2, 2, 2, DEC])
    beside = sb("beside", [P, 2, 2, 2, P + 1])
    dec = sb("dec", [P, 2, 2, DEC])
    mix = sb("mix", [P, 4, DEC])
    names = ("const w_even w_odd dts_loaded al_loaded th_done b_done c_done sq_b sq_c ssq_b ssq_c ln_b ln_c r_b r_c "
             "ang_in ang_done red_k red_done trig cabs n_b n_c aff_b aff_c prod_v rot_v prod_p rot_p diag_done "
             "dec_done mix_done s_done y_done y_kept cols_kept start_done set ctr_k").split()
    s = {n: c.sem("ssm_" + n) for n in names}
    PASSES = PAIRS // 2 - 1
    alpha_rows = alpha_d.rearrange("(i h) r t -> i h r t", h=2)
    dt_rows = dt_d.rearrange("(i h) t -> i h t", h=2)
    with own, nc.Block() as block:

        def load_pair(sp, p, e):
            sp.dma_start(w_pair[e][:], w["pair"][bass.ds(p, 1)].rearrange("o p k j m -> p (o k) j m")
                         ).then_inc(s[("w_even", "w_odd")[e]], 16)

        def load_dt(sp, pair, n):
            for h in range(2):
                sp.dma_start(dts[64 * h:64 * h + 64, :], dt_rows[bass.ds(pair, 1), h, SEG * n:SEG * (n + 1)
                                                                 ].broadcast_to([64, SEG])
                             ).then_inc(s["dts_loaded"], 16)

        def load_alpha(sp, pair, n):
            for h in range(2):
                sp.dma_start(alphas[:, h], alpha_rows[bass.ds(pair, 1), h, 2 * n:2 * n + 2, :
                                                      ].broadcast_to([P, 2, DEC])
                             ).then_inc(s["al_loaded"], 16)

        @block.sync
        def _(sp):
            sp.dma_start(norm_w[:], w["norm_w"]).then_inc(s["const"], 16)
            sp.dma_start(halves[:], w["halves"]).then_inc(s["const"], 16)
            sp.dma_start(above[:], w["above"]).then_inc(s["const"], 16)
            sp.dma_start(bias[:], w["bias"]).then_inc(s["const"], 16)
            load_pair(sp, 0, 0)
            load_dt(sp, 0, 0)
            load_alpha(sp, 0, 0)
            load_pair(sp, 1, 1)

            def ahead(i, m, final):
                k = i * 8 + m + 1
                pair = i * 2 + (m + 1) // 4
                sp.wait_ge(s["ang_in"], k)
                load_dt(sp, pair, (m + 1) % 4)
                sp.wait_ge(s["dec_done"], k)
                load_alpha(sp, pair, (m + 1) % 4)
                if not final and m == 2:
                    sp.wait_ge(s["c_done"], i * 8 + 4)
                    load_pair(sp, i * 2 + 2, 0)
                if not final and m == 6:
                    sp.wait_ge(s["c_done"], i * 8 + 8)
                    load_pair(sp, i * 2 + 3, 1)

            with nc.sync.Fori(0, PASSES) as i:
                for m in range(8):
                    ahead(i, m, False)
            for m in range(7):
                ahead(PASSES, m, True)

        def project_angles(pe, n, k, e):
            pe.wait_ge(s["ln_b"], k + 1)
            for j in range(KD):
                last = nc.tensor.matmul(c.bank[:, 4, :], w_pair[e][:, j, 0, :],
                                        c.x_t[:, j, SEG * n:SEG * (n + 1)], start=j == 0, stop=j == 1)
            last.then_inc(s["th_done"], 1)

        def project(pe, n, k, e):
            x = [c.x_t[:, j, SEG * n:SEG * (n + 1)] for j in range(KD)]
            wp = w_pair[e]
            for g, (free, done) in enumerate((("n_b", "b_done"), ("n_c", "c_done"))):
                pe.wait_ge(s[free], k * 2 + 2)
                for part in range(2):
                    for j in range(KD):
                        last = nc.tensor.matmul(c.bank[:, 2 * g + part, :], wp[:, j, 1 + 2 * g + part, :], x[j],
                                                start=j == 0, stop=j == 1)
                last.then_inc(s[done], 1)

        def sums_of_squares(pe, k):
            pe.wait_ge(s["ang_in"], k + 1)
            pe.wait_ge(s["sq_b"], k * 2 + 2)
            for j in range(2):
                last = nc.tensor.matmul(c.bank[:, 4, :], halves[:], sq[:, j, :], start=j == 0, stop=j == 1)
            last.then_inc(s["ssq_b"], 1)
            pe.wait_ge(s["ln_c"], k + 1)
            pe.wait_ge(s["sq_c"], k * 2 + 2)
            for j in range(2):
                last = nc.tensor.matmul(c.bank[:, 5, :], halves[:], sq[:, 2 + j, :], start=j == 0, stop=j == 1)
            last.then_inc(s["ssq_c"], 1)

        def attend(pe, pair, n, k, between):
            pe.wait_ge(s["rot_v"], k + 1)
            pe.wait_ge(s["rot_p"], k * 4 + 5)
            pe.wait_ge(s["y_kept"], k + 1)

            def scores(u):
                b, h = u // 2, u % 2
                for blk in range(2):
                    t0 = T * b + P * blk
                    last = nc.tensor.matmul(c.bank[:, 6 + h, T * blk:T * blk + T - P * blk],
                                            rot[:, h, 0, t0:t0 + P], rot[:, h, 1, t0:T * (b + 1)],
                                            start=True, stop=True)
                last.then_inc(s["s_done"], 1)

            def outputs(u):
                b, h = u // 2, u % 2
                pe.wait_ge(s["mix_done"], k * 4 + u + 1)
                m = mix[:, u]
                tile = 4 * n + 2 * b
                x0, x1 = (xh[:, tile + blk, bass.ds(pair * 16 + 8 * h, 8)] for blk in range(2))
                y0 = DEC + 16 * b
                nc.tensor.matmul(c.bank[:, 6 + h, y0:y0 + 8], m[:, 0:P], x0, start=True, stop=True)
                nc.tensor.matmul(c.bank[:, 6 + h, y0 + 8:y0 + 16], m[:, P:T], x0, start=True, stop=False)
                return nc.tensor.matmul(c.bank[:, 6 + h, y0 + 8:y0 + 16], m[:, T:], x1, start=False, stop=True)

            scores(0)
            for u in range(1, 4):
                scores(u)
                outputs(u - 1) if u < 3 else between()
            outputs(2)
            outputs(3).then_inc(s["y_done"], 1)

        @block.tensor
        def _(pe):
            pe.sem_inc(s["s_done"], 1)
            pe.wait_ge(s["const"], 64)
            pe.wait_ge(s["w_even"], 16)
            project_angles(pe, 0, 0, 0)
            project(pe, 0, 0, 0)
            sums_of_squares(pe, 0)
            project_angles(pe, 1, 1, 0)
            project(pe, 1, 1, 0)

            def step(i, m, final):
                k = i * 8 + m
                if m < 7 or not final:
                    sums_of_squares(pe, k + 1)

                def next_angles():
                    if m == 2:
                        pe.wait_ge(s["w_odd"], i * 16 + 16)
                    if m == 6 and not final:
                        pe.wait_ge(s["w_even"], i * 16 + 32)
                    if m < 6 or not final:
                        project_angles(pe, (m + 2) % 4, k + 2, (m + 2) // 4 % 2)

                attend(pe, i * 2 + m // 4, m % 4, k, next_angles)
                if m < 6 or not final:
                    project(pe, (m + 2) % 4, k + 2, (m + 2) // 4 % 2)

            with nc.tensor.Fori(0, PASSES) as i:
                for m in range(8):
                    step(i, m, False)
            for m in range(8):
                step(PASSES, m, True)

        def squares(act, k):
            for g, (done, sqs) in enumerate((("b_done", "sq_b"), ("c_done", "sq_c"))):
                act.wait_ge(s[done], k + 1)
                for j in range(2):
                    nc.scalar.activation(sq[:, 2 * g + j, :], c.bank[:, 2 * g + j, :], ACT.Square
                                         ).then_inc(s[sqs], 1)

        def scale(act, k):
            for g, (ssq, ln) in enumerate((("ssq_b", "ln_b"), ("ssq_c", "ln_c"))):
                act.wait_ge(s[ssq], k + 1)
                nc.scalar.activation(rms[:, g, :], c.bank[:, 4 + g, :], ACT.Ln, scale=1.0 / SN,
                                     bias=eps[:, 0:1]).then_inc(s[ln], 1)
            for g, (ln, r) in enumerate((("ln_b", "r_b"), ("ln_c", "r_c"))):
                act.wait_ge(s[ln], k + 2)
                nc.scalar.activation(rms[:, g, :], rms[:, g, :], ACT.Exp, scale=-0.5).then_inc(s[r], 1)

        def weigh_and_bias(act, e, k):
            for g, (src, done) in enumerate((("n_b", "aff_b"), ("n_c", "aff_c"))):
                act.wait_ge(s[src], k * 2 + 4)
                for j in range(2 * g, 2 * g + 2):
                    last = nc.scalar.activation(nbc[:, j, :], nbc[:, j, :], ACT.Identity,
                                                scale=norm_w[:, j:j + 1], bias=pair_bias[:, e, j:j + 1])
                last.then_inc(s[done], 1)

        def turn(act, m, k):
            act.wait_ge(s["red_done"], k + 1)
            nc.scalar.activation(sn[:, m % 2, :], red[:], ACT.Sin).then_inc(s["trig"], 1)
            nc.scalar.activation(cs[:, m % 2, :], red[:], ACT.Abs).then_inc(s["cabs"], 1)
            act.wait_ge(s["cabs"], k + 1)
            nc.scalar.activation(cs[:, m % 2, :], cs[:, m % 2, :], ACT.Sin, scale=-1.0, bias=half_pi[:, 0:1]
                                 ).then_inc(s["trig"], 1)

        @block.scalar
        def _(act):
            for n in ("ln_b", "ln_c", "trig", "y_kept"):
                act.sem_inc(s[n], 1)
            act.wait_ge(s["set"], 1)
            act.wait_ge(s["const"], 64)
            squares(act, 0)
            act.wait_ge(s["cols_kept"], 1)
            scale(act, 0)
            turn(act, 0, 0)
            weigh_and_bias(act, 0, 0)
            squares(act, 1)

            def step(i, m, final):
                k = i * 8 + m
                if m < 7 or not final:
                    if m % 4 == 3:
                        act.wait_ge(s["cols_kept"], i * 2 + (m + 1) // 4 + 1)
                    scale(act, k + 1)
                    act.wait_ge(s["prod_p"], k * 2 + 2)
                    act.wait_ge(s["prod_v"], k + 1)
                    turn(act, m + 1, k + 1)
                    weigh_and_bias(act, (m + 1) // 4 % 2, k + 1)
                act.wait_ge(s["y_done"], k + 1)
                for h in range(2):
                    last = nc.scalar.activation(
                        y_tok[:, 4 * (m % 4):4 * (m % 4) + 4, bass.ds(i * 32 + 16 * (m // 4) + 8 * h, 8)],
                        c.bank[:, 6 + h, DEC:DEC + 32].rearrange("p (t h) -> p t h", h=8), ACT.Copy)
                last.then_inc(s["y_kept"], 1)
                if m < 6 or not final:
                    squares(act, k + 2)

            with nc.scalar.Fori(0, PASSES) as i:
                for m in range(8):
                    step(i, m, False)
            for m in range(8):
                step(PASSES, m, True)

        def pair_columns(pair, e):
            nc.vector.tensor_copy(bet[:, e], beta_tok[:, bass.ds(pair * 2, 2), :])
            nc.vector.tensor_copy(gam[:, e], gamma_tok[:, bass.ds(pair * 2, 2), :])
            nc.vector.tensor_copy(pair_bias[:, e:e + 1, :], bias[:, bass.ds(pair, 1), :]
                                  ).then_inc(s["cols_kept"], 1)

        def angles(dve, k):
            dve.wait_ge(s["dts_loaded"], k * 32 + 32)
            dve.wait_ge(s["th_done"], k + 1)
            nc.vector.tensor_tensor(ang[:], c.bank[:, 4, :], dts[:], ALU.mult).then_inc(s["ang_in"], 1)
            dve.wait_ge(s["ang_in"], k + 1)
            for b in range(2):
                last = nc.vector.tensor_tensor_scan(turns[:, T * b:T * (b + 1)],
                                                    c.ones[:, 0:1].broadcast_to([P, T]),
                                                    ang[:, T * b:T * (b + 1)], 0.0, ALU.mult, ALU.add)
            last.then_inc(s["ang_done"], 1)
            dve.wait_ge(s["ang_done"], k + 1)
            nc.vector.tensor_scalar(ang[:], turns[:], INV_2PI, ROUND, ALU.mult, ALU.add).then_inc(s["red_k"], 1)
            dve.wait_ge(s["red_k"], k + 1)
            nc.vector.tensor_scalar(ang[:], ang[:], ROUND, None, ALU.subtract).then_inc(s["ctr_k"], 1)
            dve.wait_ge(s["ctr_k"], k * 3 + 1)
            nc.vector.scalar_tensor_tensor(turns[:], ang[:], -TWO_PI_HI, turns[:], ALU.mult, ALU.add
                                           ).then_inc(s["ctr_k"], 1)
            dve.wait_ge(s["ctr_k"], k * 3 + 2)
            nc.vector.scalar_tensor_tensor(turns[:], ang[:], -TWO_PI_LO, turns[:], ALU.mult, ALU.add
                                           ).then_inc(s["ctr_k"], 1)
            dve.wait_ge(s["ctr_k"], k * 3 + 3)
            dve.wait_ge(s["trig"], k * 2 + 1)
            nc.vector.tensor_scalar(red[:], turns[:], PI, -PI, ALU.min, ALU.max).then_inc(s["red_done"], 1)

        def norm(dve, g, k):
            r, done = (("r_b", "n_b"), ("r_c", "n_c"))[g]
            dve.wait_ge(s[r], k + 1)
            dve.wait_ge(s["prod_p"], k * 2 + 1 + g)
            for j in range(2 * g, 2 * g + 2):
                nc.vector.tensor_tensor(nbc[:, j, :], c.bank[:, j, :], rms[:, g, :], ALU.mult
                                        ).then_inc(s[done], 1)

        def rotate(dve, m, k):
            dve.wait_ge(s["trig"], k * 2 + 3)
            for g, done in enumerate(("aff_b", "aff_c")):
                dve.wait_ge(s[done], k + 1)
                for part, angle in enumerate((cs, sn)):
                    j = 2 * g + part
                    last = nc.vector.tensor_tensor(pr[:, j, :], nbc[:, j, :], angle[:, m % 2, :], ALU.mult)
            last.then_inc(s["prod_v"], 1)
            dve.wait_ge(s["prod_v"], k + 2)
            dve.wait_ge(s["s_done"], k * 4 + 1)
            for h in range(2):
                half = pr[64 * h:64 * h + 64].rearrange("p (g q) t -> p g q t", q=2)
                last = nc.vector.tensor_tensor(rot[0:64, h], half[:, :, 0, :], half[:, :, 1, :], ALU.subtract)
            last.then_inc(s["rot_v"], 1)

        def decays(dve, m, k):
            dve.wait_ge(s["al_loaded"], k * 32 + 32)
            dve.wait_ge(s["start_done"], k + 1)
            nc.vector.tensor_tensor_scan(dec[:].rearrange("p h b t -> p (h b t)"),
                                         alphas[:].rearrange("p h b t -> p (h b t)"),
                                         start[:, m % 2].rearrange("p h b t -> p (h b t)"), 0.0,
                                         ALU.mult, ALU.add).then_inc(s["dec_done"], 1)

        def weigh(dve, u, k):
            dve.wait_ge(s["s_done"], k * 4 + u + 2)
            nc.vector.tensor_tensor(mix[:, u, :], dec[:, u % 2, u // 2], c.bank[:, 6 + u % 2, 0:DEC], ALU.mult
                                    ).then_inc(s["mix_done"], 1)

        @block.vector
        def _(dve):
            for n, v in (("n_b", 2), ("n_c", 2), ("prod_v", 1)):
                dve.sem_inc(s[n], v)
            nc.vector.memset(eps[:], 1e-6)
            nc.vector.memset(half_pi[:], HALF_PI)
            nc.vector.memset(diag[:, P:], 0.0)
            nc.vector.tensor_copy(diag[:, 0:P], c.ident[:])
            nc.vector.memset(start[:], 0.0).then_inc(s["set"], 1)
            dve.wait_ge(s["const"], 64)
            pair_columns(0, 0)
            dve.wait_ge(s["cols_kept"], 1)
            angles(dve, 0)
            norm(dve, 0, 0)
            norm(dve, 1, 0)
            rotate(dve, 0, 0)
            angles(dve, 1)
            decays(dve, 0, 0)

            def step(i, m, final):
                k = i * 8 + m
                if m % 4 == 2 and not (final and m == 6):
                    pair_columns(i * 2 + (m + 2) // 4, (m + 2) // 4 % 2)
                dve.wait_ge(s["dec_done"], k + 1)
                weigh(dve, 0, k)
                weigh(dve, 1, k)
                weigh(dve, 2, k)
                if m < 7 or not final:
                    norm(dve, 0, k + 1)
                weigh(dve, 3, k)
                if m < 7 or not final:
                    norm(dve, 1, k + 1)
                    rotate(dve, m + 1, k + 1)
                if m < 6 or not final:
                    angles(dve, k + 2)
                if m < 7 or not final:
                    decays(dve, m + 1, k + 1)

            with nc.vector.Fori(0, PASSES) as i:
                for m in range(8):
                    step(i, m, False)
            for m in range(8):
                step(PASSES, m, True)

        def starts(pool, m, n, e, k):
            across = diag, above
            for blk in range(2):
                width = P + 1 - blk
                for j, (out, table) in enumerate(((start[:, m % 2, :, :, T * blk:T * blk + width], gam),
                                                  (beside[:, blk, :, :, 0:width], bet))):
                    last = nc.gpsimd.tensor_tensor(
                        out, across[j][:, 0:width].unsqueeze(1).unsqueeze(1).broadcast_to([P, 2, 2, width]),
                        table[:, e, :, 4 * n + blk:4 * n + blk + 3:2].unsqueeze(3).broadcast_to([P, 2, 2, width]),
                        ALU.mult)
            last.then_inc(s["diag_done"], 1)
            pool.wait_ge(s["diag_done"], k + 1)
            for blk in range(2):
                width = P + 1 - blk
                out = start[:, m % 2, :, :, T * blk:T * blk + width]
                last = nc.gpsimd.tensor_tensor(out, out, beside[:, blk, :, :, 0:width], ALU.add)
            last.then_inc(s["start_done"], 1)

        def rotate_pool(pool, m, k):
            pool.wait_ge(s["trig"], k * 2 + 3)
            pool.wait_ge(s["s_done"], k * 4 + 1)
            for g in range(2):
                pool.wait_ge(s[("aff_b", "aff_c")[g]], k + 1)
                pool.wait_ge(s["rot_p"], k * 4 + 1 + 2 * g)
                for part, angle in enumerate((sn, cs)):
                    j = 2 * g + part
                    last = nc.gpsimd.tensor_tensor(pq[:, part, :], nbc[:, j, :], angle[:, m % 2, :], ALU.mult)
                last.then_inc(s["prod_p"], 1)
                pool.wait_ge(s["prod_p"], k * 2 + 3 + g)
                for h in range(2):
                    half = pq[64 * h:64 * h + 64]
                    nc.gpsimd.tensor_tensor(rot[64:128, h, g, :], half[:, 0, :], half[:, 1, :], ALU.add
                                            ).then_inc(s["rot_p"], 1)
                    pool.wait_ge(s["rot_p"], k * 4 + 2 * g + h + 2)

        @block.gpsimd
        def _(pool):
            pool.sem_inc(s["rot_p"], 1)
            pool.wait_ge(s["set"], 1)
            pool.sem_inc(s["prod_p"], 2)
            pool.wait_ge(s["cols_kept"], 1)
            starts(pool, 0, 0, 0, 0)
            rotate_pool(pool, 0, 0)
            pool.wait_ge(s["start_done"], 1)
            starts(pool, 1, 1, 0, 1)

            def step(i, m, final):
                k = i * 8 + m
                if m < 7 or not final:
                    rotate_pool(pool, m + 1, k + 1)
                if m < 6 or not final:
                    if m % 4 == 2:
                        pool.wait_ge(s["cols_kept"], i * 2 + (m + 2) // 4 + 1)
                    pool.wait_ge(s["dec_done"], k + 1)
                    pool.wait_ge(s["start_done"], k + 2)
                    starts(pool, m, (m + 2) % 4, (m + 2) // 4 % 2, k + 2)

            with nc.gpsimd.Fori(0, PASSES) as i:
                for m in range(8):
                    step(i, m, False)
            for m in range(8):
                step(PASSES, m, True)


def ssm_output(c, w, y_tok):
    nc = c.nc
    own = ExitStack()
    wz = c.sbuf("wz", [P, KD, DIN], ctx=own)
    wo = c.sbuf("ssm_wo", [P, DIN // P, D], ctx=own)
    z = c.sbuf("z", [P, 2, DIN], ctx=own)
    yz = c.sbuf("yz", [P, 2, DIN], ctx=own)
    yz_t = c.sbuf("yz_t", [P, 2, DIN // P, P], ctx=own)
    loaded, z_done, z_kept, gated, turned, copied, o_done, added = (
        c.sem("ssmout_" + n) for n in "loaded z_done z_kept gated turned copied o_done added".split())
    with own, nc.Block() as block:

        @block.sync
        def _(sp):
            sp.dma_start(wz[:], w["z"]).then_inc(loaded, 16)
            sp.dma_start(wo[:], w["out"]).then_inc(loaded, 16)

        @block.tensor
        def _(pe):
            def gate_input(t):
                if t >= 2:
                    pe.wait_ge(z_kept, t - 1)
                for k in range(KD):
                    last = nc.tensor.matmul(c.bank[:, t % 2, :], c.x_t[:, k, P * t:P * (t + 1)], wz[:, k, :],
                                            start=k == 0, stop=k == KD - 1)
                last.then_inc(z_done, 1)

            pe.wait_ge(loaded, 32)
            gate_input(0)
            for t in range(NT):
                if t + 1 < NT:
                    gate_input(t + 1)
                pe.wait_ge(gated, t + 1)
                if t >= 2:
                    pe.wait_ge(copied, t - 1)
                for j in range(4):
                    last = nc.tensor.transpose(c.bank[:, 2 + t % 2, P * j:P * (j + 1)],
                                               yz[:, t % 2, P * j:P * (j + 1)], c.ident[:])
                last.then_inc(turned, 1)
                pe.wait_ge(copied, t + 1)
                if t >= 2:
                    pe.wait_ge(added, t - 1)
                for j in range(4):
                    last = nc.tensor.matmul(c.bank[:, 4 + t % 2, 0:D], yz_t[:, t % 2, j, :], wo[:, j, :],
                                            start=j == 0, stop=j == 3)
                last.then_inc(o_done, 1)

        @block.scalar
        def _(act):
            for t in range(NT):
                act.wait_ge(z_done, t + 1)
                if t >= 2:
                    act.wait_ge(gated, t - 1)
                nc.scalar.activation(z[:, t % 2, :], c.bank[:, t % 2, :], ACT.Silu).then_inc(z_kept, 1)

        @block.vector
        def _(dve):
            for t in range(NT):
                dve.wait_ge(z_kept, t + 1)
                if t >= 2:
                    dve.wait_ge(turned, t - 1)
                nc.vector.tensor_tensor(yz[:, t % 2, :], y_tok[:, t, :], z[:, t % 2, :], ALU.mult
                                        ).then_inc(gated, 1)
                dve.wait_ge(turned, t + 1)
                if t >= 2:
                    dve.wait_ge(o_done, t - 1)
                nc.vector.tensor_copy(yz_t[:, t % 2, :, :].rearrange("p j t -> p (j t)"),
                                      c.bank[:, 2 + t % 2, :]).then_inc(copied, 1)
                dve.wait_ge(o_done, t + 1)
                nc.vector.tensor_tensor(c.x_tok[:, t, :], c.x_tok[:, t, :], c.bank[:, 4 + t % 2, 0:D],
                                        ALU.add).then_inc(added, 1)



XH, XD = 16, 128
XP = XH // 2
BIG = 1e30


def cross_attention(c, w, normed):
    nc = c.nc
    own = ExitStack()
    tag = "xn_" if normed else "xm_"

    def sb(name, shape, dt=F32, ctx=own):
        return c.sbuf(tag + name, shape, dt, ctx=ctx)

    kvh = XH if normed else XP
    wq = sb("wq", [P, KD, XH * XD])
    wo = sb("wo", [P, XH, D])
    k_t = sb("k_t", [P, kvh, B * S2])
    v = sb("v", [P, B, XP * XD])
    neg = sb("neg", [P, B * S2])
    with own:
        own_keys = ExitStack()
        wk = sb("wk", [P, kvh * XD], ctx=own_keys)
        wv = sb("wv", [P, 2 if normed else 1, XP * XD], ctx=own_keys)
        ctx_t = sb("ctx_t", [P, B * S2], ctx=own_keys)
        loads = [(ctx_t[:], w["ctx"]), (wk[:], w["k"]), (wv[:], w["v"]), (wq[:], w["q"]), (wo[:], w["o"])]
        if normed:
            small = sb("g", [P, 2], ctx=own_keys)
            loads.append((small[:], w["g"]))
        else:
            small = sb("mask_row", [P, B * S2], U8, own_keys), sb("mask_col", [P, B], U8, own_keys)
            loads += [(small[0][:], w["mask_row"].partition_broadcast(P)), (small[1][:], w["mask_col"])]
        with own_keys:
            yield loads
            cross_keys(c, normed, tag, kvh, ctx_t, wk, wv, small, k_t, v, neg)
        cross_heads(c, normed, tag, kvh, wq, wo, k_t, v, neg)


def cross_keys(c, normed, tag, kvh, ctx_t, wk, wv, small, k_t, v, neg):
    nc = c.nc
    own = ExitStack()

    def sb(name, shape, dt=F32):
        return c.sbuf(tag + name, shape, dt, ctx=own)

    par = 2 if normed else 1
    k_done, k_kept, sq_done, ssq_done, r_done, v_done, v_kept, m_done = (
        c.sem(tag + n) for n in "k_done k_kept sq_done ssq_done r_done v_done v_kept m_done".split())
    if normed:
        g = small
        eps = sb("eps", [P, 1])
        sq = sb("sq", [P, 2, B * S2])
        rms = sb("rms", [P, 2, B * S2])
    else:
        mask_row, mask_col = small
        keep = sb("keep", [P, B])
    with own, nc.Block() as block:

        @block.tensor
        def _(pe):
            for h in range(kvh + 1):
                if h < kvh:
                    if h >= 2:
                        pe.wait_ge(k_kept, h - 1)
                    nc.tensor.matmul(c.bank[:, h % 2, :], wk[:, XD * h:XD * (h + 1)], ctx_t[:], start=True,
                                     stop=True).then_inc(k_done, 1)
                if h and normed:
                    pe.wait_ge(sq_done, h)
                    if h >= 3:
                        pe.wait_ge(r_done, 2 * (h - 2) - 1)
                    nc.tensor.matmul(c.bank[:, 2 + h % 2, :], c.ones[:], sq[:, (h - 1) % 2, :], start=True,
                                     stop=True).then_inc(ssq_done, 1)
            for j in range(2 * B):
                b, half = divmod(j, 2)
                if j >= 2:
                    pe.wait_ge(v_kept, j - 1)
                for parity in range(2):
                    last = nc.tensor.matmul(c.bank[64 * parity:64 * parity + 64, 4 + j % 2, :],
                                            ctx_t[:, S2 * b:S2 * (b + 1)],
                                            wv[:, parity % par, SEG * half:SEG * (half + 1)],
                                            start=True, stop=True)
                last.then_inc(v_done, 1)

        @block.scalar
        def _(act):
            if normed:
                act.wait_ge(m_done, 1)
                for h in range(kvh):
                    act.wait_ge(k_done, h + 1)
                    if h >= 2:
                        act.wait_ge(ssq_done, h - 1)
                    nc.scalar.activation(sq[:, h % 2, :], c.bank[:, h % 2, :], ACT.Square).then_inc(sq_done, 1)
                    act.wait_ge(ssq_done, h + 1)
                    if h >= 2:
                        act.wait_ge(k_kept, h - 1)
                    nc.scalar.activation(rms[:, h % 2, :], c.bank[:, 2 + (h + 1) % 2, :], ACT.Ln, scale=1.0 / XD,
                                         bias=eps[:, 0:1]).then_inc(r_done, 1)
                    act.wait_ge(r_done, 2 * h + 1)
                    nc.scalar.activation(rms[:, h % 2, :], rms[:, h % 2, :], ACT.Exp, scale=-0.5
                                         ).then_inc(r_done, 1)
            if not normed:
                act.wait_ge(m_done, 1)
            for j in range(2 * B):
                b, half = divmod(j, 2)
                act.wait_ge(v_done, j + 1)
                out = v[:, b, SEG * half:SEG * (half + 1)]
                if normed:
                    nc.scalar.activation(out, c.bank[:, 4 + j % 2, :], ACT.Copy).then_inc(v_kept, 1)
                else:
                    nc.scalar.activation(out, c.bank[:, 4 + j % 2, :], ACT.Copy, scale=keep[:, b:b + 1]
                                         ).then_inc(v_kept, 1)

        @block.vector
        def _(dve):
            if normed:
                nc.vector.memset(eps[:], 1e-5).then_inc(m_done, 1)
            if not normed:
                nc.vector.tensor_copy(keep[:], mask_col[:]).then_inc(m_done, 1)
                nc.vector.tensor_scalar(neg[:], mask_row[:], -1.0, BIG, ALU.add, ALU.mult)
            for h in range(kvh):
                if normed:
                    dve.wait_ge(r_done, 2 * h + 2)
                    nc.vector.tensor_tensor(k_t[:, h, :], c.bank[:, h % 2, :], rms[:, h % 2, :], ALU.mult
                                            ).then_inc(k_kept, 1)
                    dve.wait_ge(k_kept, h + 1)
                    nc.vector.tensor_scalar(k_t[:, h, :], k_t[:, h, :], g[:, 0:1], g[:, 1:2], ALU.mult, ALU.mult)
                else:
                    dve.wait_ge(k_done, h + 1)
                    nc.vector.tensor_copy(k_t[:, h, :], c.bank[:, h % 2, :]).then_inc(k_kept, 1)


def cross_heads(c, normed, tag, kvh, wq, wo, k_t, v, neg):
    nc = c.nc
    own = ExitStack()

    def sb(name, shape, dt=F32):
        return c.sbuf(tag + name, shape, dt, ctx=own)

    scale = XD ** -0.5
    q = sb("q", [P, 2, 2, T])
    sc = sb("sc", [P, 8, 4, S2])
    probs = sb("probs", [P, 2, 4, S2])
    top = sb("top", [P, 4, 4])
    total = sb("total", [P, 2, 4])
    p_t = sb("p_t", [P, 2, T])
    o_t = sb("o_t", [P, XH, T])
    vb = sb("vb", [P, XP * XD])
    names = ("q_done q_kept s_done s_used shifted top_done exp_done sums p_done t_done t_kept o_done o_kept v_kept "
             "out_done added sq_done rq_in rq_ln rq_done eps_set").split()
    s = {n: c.sem(tag + "h_" + n) for n in names}
    if normed:
        qsq = sb("qsq", [P, 2, 2, T])
        rq = sb("rq", [P, 4, 4])
        eps = sb("eps_q", [P, 1])
    with own, nc.Block() as block:


        SHIFT, NORMALISE, TURN, VALUES = 2, 3, 4, 5

        def steps(eng, step):
            for at in range(XP):
                step(0, at)
            with eng.Fori(0, B - 2) as r:
                for at in range(XP, 2 * XP):
                    step(r, at)
            for at in range(XP, 2 * XP + VALUES + 2):
                step(B - 2, at)

        def exists(r, at):
            return at >= 0 and not (isinstance(r, int) and r * XP + at >= B * XP)

        @block.tensor
        def _(pe):
            def queries(r, at):
                j = at % XP
                pe.wait_ge(s["q_kept"], r * XP + at + 1)
                for h in range(2):
                    for k in range(KD):
                        last = nc.tensor.matmul(c.bank[:, j % 2, T * h:T * (h + 1)],
                                                wq[:, k, XD * (2 * j + h):XD * (2 * j + h + 1)],
                                                c.x_t[:, k, bass.ds(r * T + at // XP * T, T)],
                                                start=k == 0, stop=k == 1)
                last.then_inc(s["q_done"], 1)

            def scores(r, at):
                j, g = at % XP, r * XP + at
                pe.wait_ge(s["q_kept"], g + 3)
                if normed:
                    pe.wait_ge(s["sq_done"], g + 1)
                pe.wait_ge(s["s_used"], g + 1)
                for t in range(2):
                    for h in range(2):
                        col = (2 * t + h) * S2
                        head = 2 * j + h if normed else j
                        last = nc.tensor.matmul(c.bank[:, 2 + j % 2, col:col + S2],
                                                q[:, j % 2, h, P * t:P * (t + 1)],
                                                k_t[:, head, bass.ds(r * S2 + at // XP * S2, S2)],
                                                start=True, stop=True)
                if normed:
                    for t in range(2):
                        for h in range(2):
                            col = 4 * S2 + 2 * t + h
                            last = nc.tensor.matmul(c.bank[:, 2 + j % 2, col:col + 1],
                                                    qsq[:, j % 2, h, P * t:P * (t + 1)], c.ones[:, 0:1],
                                                    start=True, stop=True)
                last.then_inc(s["s_done"], 1)

            def turn(r, at):
                j = at % XP
                pe.wait_ge(s["p_done"], r * XP + at + 1)
                pe.wait_ge(s["t_kept"], r * XP + at + 1)
                for t in range(2):
                    last = nc.tensor.transpose(c.bank[:, 4, P * t:P * (t + 1)],
                                               probs[:, j % 2, 2 * t:2 * t + 2, :].rearrange("p h s -> p (h s)"),
                                               c.ident[:])
                last.then_inc(s["t_done"], 1)

            def values(r, at):
                j = at % XP
                pe.wait_ge(s["t_kept"], r * XP + at + 2)
                pe.wait_ge(s["o_kept"], r * XP + at + 1)
                if j == 0:
                    pe.wait_ge(s["v_kept"], r + at // XP + 1)
                for h in range(2):
                    rows = slice(64 * h, 64 * h + 64)
                    last = nc.tensor.matmul(c.bank[:, 5 + h, 0:T], vb[rows, XD * j:XD * (j + 1)],
                                            p_t[rows, j % 2, :], start=True, stop=True)
                last.then_inc(s["o_done"], 1)

            def project_out(r, at):
                pe.wait_ge(s["o_kept"], r * XP + at + 1)
                pe.wait_ge(s["added"], r + at // XP)
                for t in range(2):
                    for h in range(XH):
                        last = nc.tensor.matmul(c.bank[:, 7, D * t:D * (t + 1)], o_t[:, h, P * t:P * (t + 1)],
                                                wo[:, h, :], start=h == 0, stop=h == XH - 1)
                last.then_inc(s["out_done"], 1)

            for n, v_ in (("s_done", 2), ("t_done", 2), ("o_done", 2), ("out_done", 1)):
                pe.sem_inc(s[n], v_)
            if normed:
                pe.wait_ge(s["eps_set"], 1)
            queries(0, 0)

            def step(r, at):
                if exists(r, at + 1):
                    queries(r, at + 1)
                if exists(r, at):
                    scores(r, at)
                if exists(r, at - TURN):
                    turn(r, at - TURN)
                if at > VALUES and (at - VALUES) % XP == 0:
                    project_out(r, at - VALUES)
                if exists(r, at - VALUES):
                    values(r, at - VALUES)

            steps(nc.tensor, step)

        @block.scalar
        def _(act):
            act.sem_inc(s["q_kept"], 2)
            act.sem_inc(s["t_kept"], 1)
            act.sem_inc(s["o_kept"], 1)

            def keep_q(r, at):
                act.wait_ge(s["q_done"], r * XP + at + 1)
                act.wait_ge(s["s_done"], r * XP + at + 1)
                nc.scalar.activation(q[:, at % 2].rearrange("p h t -> p (h t)"), c.bank[:, at % 2, :], ACT.Copy
                                     ).then_inc(s["q_kept"], 1)

            def rms(r, at):
                both = rq[:, at % 4 - 1:at % 4 + 1, :]
                act.wait_ge(s["rq_in"], r * XP + at + 1)
                nc.scalar.activation(both, both, ACT.Ln, scale=1.0 / XD, bias=eps[:, 0:1]).then_inc(s["rq_ln"], 2)
                act.wait_ge(s["rq_ln"], r * XP + at + 1)
                nc.scalar.activation(both, both, ACT.Exp, scale=-0.5).then_inc(s["rq_done"], 2)

            def exps(r, at):
                act.wait_ge(s["shifted"], r * XP + at + 1)
                nc.scalar.activation(sc[:, at % 8], sc[:, at % 8], ACT.Exp, scale=scale).then_inc(s["exp_done"], 1)

            def keep_t(r, at):
                act.wait_ge(s["t_done"], r * XP + at + 3)
                act.wait_ge(s["o_done"], r * XP + at + 1)
                nc.scalar.activation(p_t[:, at % 2, :], c.bank[:, 4, 0:T], ACT.Copy).then_inc(s["t_kept"], 1)

            def keep_o(r, at):
                j = at % XP
                act.wait_ge(s["o_done"], r * XP + at + 3)
                if j == 0:
                    act.wait_ge(s["out_done"], r + at // XP + 1)
                nc.scalar.activation(o_t[:, 2 * j:2 * j + 2, :],
                                     c.bank[:, 5:7, 0:T], ACT.Copy
                                     ).then_inc(s["o_kept"], 1)

            if normed:
                act.wait_ge(s["eps_set"], 1)
            keep_q(0, 0)

            def step(r, at):
                if exists(r, at + 1):
                    keep_q(r, at + 1)
                if normed and exists(r, at) and at % 2:
                    rms(r, at)
                if exists(r, at - SHIFT):
                    exps(r, at - SHIFT)
                if exists(r, at - TURN):
                    keep_t(r, at - TURN)
                if exists(r, at - VALUES):
                    keep_o(r, at - VALUES)

            steps(nc.scalar, step)

        @block.vector
        def _(dve):
            dve.sem_inc(s["s_used"], 2)
            dve.sem_inc(s["added"], 1)
            if normed:
                nc.vector.memset(eps[:], 1e-5).then_inc(s["eps_set"], 1)

            def take(r, at):
                g, bank = r * XP + at, 2 + at % 2
                dve.wait_ge(s["s_done"], g + 3)
                scores = c.bank[:, bank, 0:4 * S2].rearrange("p (g s) -> p g s", s=S2)
                if normed:
                    nc.vector.tensor_copy(rq[:, at % 4, :], c.bank[:, bank, 4 * S2:4 * S2 + 4]
                                          ).then_inc(s["rq_in"], 1)
                    nc.vector.tensor_reduce(top[:, at % 4, :], scores, AX.X, ALU.max).then_inc(s["top_done"], 1)
                    dve.wait_ge(s["top_done"], g + 1)
                    nc.vector.tensor_tensor(sc[:, at % 8], scores,
                                            top[:, at % 4, :].unsqueeze(2).broadcast_to([P, 4, S2]),
                                            ALU.subtract).then_inc(s["s_used"], 1)
                else:
                    bias = neg[:, bass.ds(r * S2 + at // XP * S2, S2)].unsqueeze(1).broadcast_to([P, 4, S2])
                    nc.vector.tensor_tensor(sc[:, at % 8], scores, bias, ALU.add).then_inc(s["s_used"], 1)
                    dve.wait_ge(s["s_used"], g + 3)
                    nc.vector.tensor_reduce(top[:, at % 4, :], sc[:, at % 8], AX.X, ALU.max
                                            ).then_inc(s["top_done"], 1)

            def shift(r, at):
                g = r * XP + at
                if normed:
                    dve.wait_ge(s["rq_done"], g + 1)
                    dve.wait_ge(s["s_used"], g + 3)
                    other, op = rq, ALU.mult
                else:
                    dve.wait_ge(s["top_done"], g + 1)
                    other, op = top, ALU.subtract
                nc.vector.tensor_tensor(sc[:, at % 8], sc[:, at % 8],
                                        other[:, at % 4, :].unsqueeze(2).broadcast_to([P, 4, S2]), op
                                        ).then_inc(s["shifted"], 1)

            def normalise(r, at):
                g = r * XP + at
                dve.wait_ge(s["exp_done"], g + 1)
                nc.vector.tensor_reduce(total[:, at % 2, :], sc[:, at % 8], AX.X, ALU.add).then_inc(s["sums"], 1)
                dve.wait_ge(s["sums"], g * 2 + 1)
                nc.vector.reciprocal(total[:, at % 2, :], total[:, at % 2, :]).then_inc(s["sums"], 1)
                dve.wait_ge(s["sums"], g * 2 + 2)
                dve.wait_ge(s["t_done"], g + 1)
                nc.vector.tensor_tensor(probs[:, at % 2], sc[:, at % 8],
                                        total[:, at % 2, :].unsqueeze(2).broadcast_to([P, 4, S2]), ALU.mult
                                        ).then_inc(s["p_done"], 1)

            def add(r, at):
                dve.wait_ge(s["out_done"], r + at // XP + 1)
                x = c.x_tok[:, bass.ds(r * 2 + (at // XP - 1) * 2, 2), :]
                nc.vector.tensor_tensor(x, x, c.bank[:, 7, :].rearrange("p (t d) -> p t d", t=2), ALU.add
                                        ).then_inc(s["added"], 1)

            def step(r, at):
                if exists(r, at):
                    take(r, at)
                if exists(r, at - SHIFT):
                    shift(r, at - SHIFT)
                if exists(r, at - NORMALISE):
                    normalise(r, at - NORMALISE)
                if at > VALUES + 1 and (at - VALUES - 1) % XP == 0:
                    add(r, at - VALUES - 1)

            steps(nc.vector, step)

        @block.gpsimd
        def _(pool):
            def squares(r, at):
                pool.wait_ge(s["q_kept"], r * XP + at + 3)
                pool.wait_ge(s["s_done"], r * XP + at + 1)
                nc.gpsimd.tensor_tensor(qsq[:, at % 2], q[:, at % 2], q[:, at % 2], ALU.mult
                                        ).then_inc(s["sq_done"], 1)

            def place_values(r, at):
                pool.wait_ge(s["o_done"], r * XP + at + 2)
                nc.gpsimd.tensor_copy(vb[:], v[:, bass.ds(r + at // XP, 1), :].rearrange("p o n -> p (o n)")
                                      ).then_inc(s["v_kept"], 1)

            if normed:
                squares(0, 0)

            def step(r, at):
                if exists(r, at - VALUES) and (at - VALUES) % XP == 0:
                    place_values(r, at - VALUES)
                if normed and exists(r, at + 1):
                    squares(r, at + 1)

            steps(nc.gpsimd, step)



def gated_ffn(c, tag, rows, w_in, w_out, scale_gate, scale_up):
    nc = c.nc
    own = ExitStack()
    M = len(rows)
    gate = c.sbuf(tag + "gate_out", [P, 2, SEG], ctx=own)
    hid = c.sbuf(tag + "hid", [P, M, SEG], ctx=own)
    s = {n: c.sem(tag + n) for n in "in_done silu_done hid_done out_done added".split()}
    with own, nc.Block() as block:

        @block.tensor
        def _(pe):
            with nc.tensor.Fori(0, NSEG) as i:
                for m in range(M):
                    r = rows[m]
                    pe.wait_ge(s["hid_done"], i * M + m + 1)
                    for g in range(2):
                        for k in range(KD):
                            last = nc.tensor.matmul(c.bank[:, 2 * (m % 2) + g, :], w_in[:, k, g, P * m:P * (m + 1)],
                                                    c.x_t[:, k, bass.ds(i * SEG, SEG)], start=k == 0, stop=k == 1)
                    last.then_inc(s["in_done"], 1)
                pe.wait_ge(s["hid_done"], i * M + M + 2)
                for half in range(2):
                    pe.wait_ge(s["added"], i * 2 + half + 1)
                    for t in range(2):
                        for m in range(M):
                            r = rows[m]
                            at = P * (2 * half + t)
                            last = nc.tensor.matmul(c.bank[:, 4 + half, D * t:D * (t + 1)], hid[0:r, m, at:at + P],
                                                    w_out[0:r, m, :], start=m == 0, stop=m == M - 1)
                    last.then_inc(s["out_done"], 1)

        @block.scalar
        def _(act):
            with nc.scalar.Fori(0, NSEG) as i:
                for m in range(M):
                    r = rows[m]
                    act.wait_ge(s["in_done"], i * M + m + 1)
                    act.wait_ge(s["hid_done"], i * M + m + 1)
                    nc.scalar.activation(gate[0:r, m % 2, :], c.bank[0:r, 2 * (m % 2), :], ACT.Silu,
                                         scale=scale_gate[0:r, m:m + 1]).then_inc(s["silu_done"], 1)

        @block.vector
        def _(dve):
            dve.sem_inc(s["hid_done"], 2)
            dve.sem_inc(s["added"], 2)
            with nc.vector.Fori(0, NSEG) as i:
                for m in range(M):
                    r = rows[m]
                    dve.wait_ge(s["silu_done"], i * M + m + 1)
                    nc.vector.scalar_tensor_tensor(hid[0:r, m, :], c.bank[0:r, 2 * (m % 2) + 1, :],
                                                   scale_up[0:r, m:m + 1], gate[0:r, m % 2, :], ALU.mult, ALU.mult
                                                   ).then_inc(s["hid_done"], 1)
                for half in range(2):
                    dve.wait_ge(s["out_done"], i * 2 + half + 1)
                    x = c.x_tok[:, bass.ds(i * 4 + 2 * half, 2), :]
                    nc.vector.tensor_tensor(x, x, c.bank[:, 4 + half, :].rearrange("p (t d) -> p t d", t=2),
                                            ALU.add).then_inc(s["added"], 1)


HID0, HSCALE = 1024, 64.0


def hadamard_ffn(c, w):
    nc = c.nc
    own = ExitStack()
    M = HID0 // P
    w_in = c.sbuf("had_in", [P, KD, 2, HID0], ctx=own)
    w_out = c.sbuf("had_out", [P, M, D], ctx=own)
    scales = c.sbuf("had_scales", [P, 2, M], ctx=own)
    with own:
        mine = ExitStack()
        up = c.sbuf("had_rows", [P, 2, 2 * M, D], ctx=mine)
        dn = c.sbuf("had_down_rows", [P, 2, KD, HID0], ctx=mine)
        su_in = c.sbuf("had_su_in", [P, KD], ctx=mine)
        su_out = c.sbuf("had_su_out", [P, M], ctx=mine)
        down_scale = c.sbuf("had_down_scale", [P, KD], ctx=mine)
        yield [(up[:, 0], w["rows"]), (dn[:, 0], w["down"]), (su_in[:], w["su_in"]), (su_out[:], w["su_out"]),
               (down_scale[:], w["down_scale"]), (scales[:], w["scales"])]
        plus, minus, turned, kept, scaled = (c.sem("had_" + n) for n in "plus minus turned kept scaled".split())
        stages_in = D.bit_length() - 1
        stages_out = HID0.bit_length() - 1
        with mine, nc.Block() as block:

            def butterflies(eng, unit, op, mine_done, other_done):
                n = 0
                for buf, stages in ((up, stages_in), (dn, stages_out)):
                    for st in range(stages):
                        if n:
                            eng.wait_ge(mine_done, n)
                            eng.wait_ge(other_done, n)
                        h = 1 << st
                        src, dst = (buf[:, (st + o) % 2].rearrange("p m d -> p (m d)").rearrange(
                            "p (g two h) -> p g two h", two=2, h=h) for o in range(2))
                        which = 0 if op == ALU.add else 1
                        unit.tensor_tensor(dst[:, :, which, :], src[:, :, 0, :], src[:, :, 1, :], op
                                           ).then_inc(mine_done, 1)
                        n += 1

            all_stages = stages_in + stages_out
            up_at, dn_at = stages_in % 2, stages_out % 2

            @block.vector
            def _(dve):
                butterflies(dve, nc.vector, ALU.add, plus, minus)
                dve.wait_ge(plus, all_stages)
                dve.wait_ge(minus, all_stages)
                nc.vector.tensor_scalar(scales[:], scales[:], HSCALE, None, ALU.mult)
                nc.vector.tensor_scalar(down_scale[:], down_scale[:], HSCALE, None, ALU.mult).then_inc(scaled, 1)
                nc.vector.tensor_scalar(su_in[:], su_in[:], D ** -0.5 / HSCALE, None, ALU.mult).then_inc(scaled, 1)
                nc.vector.tensor_scalar(su_out[:], su_out[:], HID0 ** -0.5 / HSCALE, None, ALU.mult
                                        ).then_inc(scaled, 1)
                dve.wait_ge(scaled, 1)
                for k in range(KD):
                    nc.vector.tensor_scalar(dn[:, dn_at, k, :], dn[:, dn_at, k, :], down_scale[:, k:k + 1], None,
                                            ALU.mult).then_inc(scaled, 1)

            @block.gpsimd
            def _(pool):
                butterflies(pool, nc.gpsimd, ALU.subtract, minus, plus)

            @block.tensor
            def _(pe):
                pe.wait_ge(plus, stages_in)
                pe.wait_ge(minus, stages_in)
                n = 0
                for g in range(2):
                    for k in range(KD):
                        for half in range(2):
                            if n >= 4:
                                pe.wait_ge(kept, n - 3)
                            for j in range(4):
                                m = g * M + 4 * half + j
                                last = nc.tensor.transpose(c.bank[:, n % 4, P * j:P * (j + 1)],
                                                           up[:, up_at, m, P * k:P * (k + 1)], c.ident[:])
                            last.then_inc(turned, 1)
                            n += 1
                pe.wait_ge(scaled, 3 + KD)
                for m in range(M):
                    pe.wait_ge(kept, n - 3)
                    for k in range(KD):
                        last = nc.tensor.transpose(c.bank[:, n % 4, P * k:P * (k + 1)],
                                                   dn[:, dn_at, k, P * m:P * (m + 1)], c.ident[:])
                    last.then_inc(turned, 1)
                    n += 1

            @block.scalar
            def _(act):
                act.wait_ge(scaled, 3)
                n = 0
                for g in range(2):
                    for k in range(KD):
                        for half in range(2):
                            act.wait_ge(turned, n + 1)
                            nc.scalar.activation(w_in[:, k, g, SEG * half:SEG * (half + 1)], c.bank[:, n % 4, :],
                                                 ACT.Copy, scale=su_in[:, k:k + 1]).then_inc(kept, 1)
                            n += 1
                for m in range(M):
                    act.wait_ge(turned, n + 1)
                    nc.scalar.activation(w_out[:, m, :], c.bank[:, n % 4, 0:D], ACT.Copy, scale=su_out[:, m:m + 1]
                                         ).then_inc(kept, 1)
                    n += 1

        gated_ffn(c, "had_", [P] * M, w_in, w_out, scales[:, 0, :], scales[:, 1, :])


HID1, ZERO_POINT = 704, 128.0


def dequant_ffn(c, w):
    nc = c.nc
    own = ExitStack()
    M = -(-HID1 // P)
    rows = [min(P, HID1 - P * m) for m in range(M)]
    w_in = c.sbuf("deq_in", [P, KD, 2, P * M], ctx=own)
    w_out = c.sbuf("deq_out", [P, M, D], ctx=own)
    s_gate = c.sbuf("deq_s_gate", [P, M], ctx=own)
    s_up = c.sbuf("deq_s_up", [P, M], ctx=own)
    with own:
        mine = ExitStack()
        q_in = c.sbuf("deq_q_in", [P, KD, 2, HID1], I32, ctx=mine)
        q_out = c.sbuf("deq_q_out", [P, M, D], I32, ctx=mine)
        s_down = c.sbuf("deq_s_down", [P, D], ctx=mine)
        loads = [(q_in[:], w["in"]), (s_down[:], w["s_down"].partition_broadcast(P))]
        for m in range(M):
            tile = slice(P * m, P * m + rows[m])
            loads += [(q_out[0:rows[m], m, :], w["out"][tile, :]), (s_gate[0:rows[m], m:m + 1], w["s_gate"][tile, :]),
                      (s_up[0:rows[m], m:m + 1], w["s_up"][tile, :])]
        yield loads
        centred = c.sem("deq_centred")
        with mine, nc.Block() as block:

            @block.vector
            def _(dve):
                for k in range(KD):
                    nc.vector.memset(w_in[:, k, :, HID1:], 0.0)
                    nc.vector.tensor_scalar(w_in[:, k, :, 0:HID1], q_in[:, k], ZERO_POINT, None, ALU.subtract)
                for m in range(M):
                    r = rows[m]
                    nc.vector.tensor_scalar(w_out[0:r, m, :], q_out[0:r, m, :], ZERO_POINT, None, ALU.subtract
                                            ).then_inc(centred, 1)
                for m in range(M):
                    r = rows[m]
                    dve.wait_ge(centred, m + 1)
                    nc.vector.tensor_tensor(w_out[0:r, m, :], w_out[0:r, m, :], s_down[0:r, :], ALU.mult)

        gated_ffn(c, "deq_", rows, w_in, w_out, s_gate, s_up)



KH, KW = 16, 128
LEVELS = 7
CH = SEG // P


def kda(c, w):
    own = ExitStack()
    xf_t = c.sbuf("xf_t", [P, TOK], ctx=own)
    xg_t = c.sbuf("xg_t", [P, TOK], ctx=own)
    beta = c.sbuf("beta", [KH, TOK], ctx=own)
    neg_a = c.sbuf("kda_neg_a", [P, KH], ctx=own)
    with own:
        own_gates = ExitStack()
        wfg = c.sbuf("wfg", [P, KD, 2, KW], ctx=own_gates)
        wb = c.sbuf("wb", [P, KD, KH], ctx=own_gates)
        with own_gates:
            yield [(wfg[:], w["fg"]), (wb[:], w["b"]), (neg_a[:], w["A_log"].partition_broadcast(P))]
            kda_gates(c, wfg, wb, xf_t, xg_t, beta, neg_a)
        kda_heads(c, w, xf_t, xg_t, beta, neg_a)


def kda_gates(c, wfg, wb, xf_t, xg_t, beta, neg_a):
    nc = c.nc
    done, kept = c.sem("kg_done"), c.sem("kg_kept")
    with nc.Block() as block:

        @block.tensor
        def _(pe):
            for q in range(NSEG):
                if q:
                    pe.wait_ge(kept, 3 * q)
                for g in range(3):
                    for k in range(KD):
                        lhs = wb[:, k, :] if g == 2 else wfg[:, k, g, :]
                        out = c.bank[0:KH, 2, :] if g == 2 else c.bank[:, g, :]
                        last = nc.tensor.matmul(out, lhs, c.x_t[:, k, SEG * q:SEG * (q + 1)], start=k == 0,
                                                stop=k == 1)
                    last.then_inc(done, 1)

        @block.scalar
        def _(act):
            for q in range(NSEG):
                cols = slice(SEG * q, SEG * (q + 1))
                for g, out in enumerate((xf_t, xg_t)):
                    act.wait_ge(done, 3 * q + g + 1)
                    nc.scalar.activation(out[:, cols], c.bank[:, g, :], ACT.Copy).then_inc(kept, 1)
                act.wait_ge(done, 3 * q + 3)
                nc.scalar.activation(beta[:, cols], c.bank[0:KH, 2, :], ACT.Sigmoid).then_inc(kept, 1)
            nc.scalar.activation(neg_a[:], neg_a[:], ACT.Exp).then_inc(kept, 1)

        @block.vector
        def _(dve):
            dve.wait_ge(kept, 3 * NSEG + 1)
            nc.vector.tensor_scalar(neg_a[:], neg_a[:], -1.0, None, ALU.mult)


def halves_of(ap, m, side):
    if len(ap.shape) == 2:
        return ap.rearrange("p (g two m) -> p g two m", two=2, m=m)[:, :, side, :]
    return ap.rearrange("p c (g two m) -> p c g two m", two=2, m=m)[:, :, :, side, :]


def kda_heads(c, w, xf_t, xg_t, beta, neg_a):
    nc = c.nc
    own = ExitStack()

    def sb(name, shape, dt=F32):
        return c.sbuf("k_" + name, shape, dt, ctx=own)

    wqkv = sb("wqkv", [P, 2, KD, 3, KW])
    wfg2 = sb("wfg2", [P, 2, 2, KW])
    wo = sb("wo", [P, 2, D])
    taps = sb("taps", [P, 2, 3, 5])
    dt_bias = sb("dt_bias", [P, 2])
    sel = sb("sel", [KH, 2, P])
    decay = sb("decay", [P, 2])
    o_norm = sb("o_norm", [P, 1])
    masks = sb("masks", [P, LEVELS, P // 2])
    masks_i = sb("masks_i", [P, LEVELS, P // 2], I32)
    eps6 = sb("eps6", [P, 1])
    eps5 = sb("eps5", [P, 1])
    raw = sb("raw", [P, 3, 2, T + 3])
    conv = sb("conv", [P, 3, SEG])
    act_out = sb("act_out", [P, 3, SEG])
    sq = sb("sq", [P, 2, SEG])
    rn = sb("rn", [P, 2, SEG])
    z = sb("z", [P, SEG])
    tail = sb("tail", [P, SEG])
    low = sb("low", [P, SEG])
    kn = sb("kn", [P, SEG])
    vals = sb("vals", [P, 4, CH, KW])
    sgate = sb("sgate", [P, 4, SEG])
    qn = sb("qn", [P, 2, SEG])
    kq = sb("kq", [P, 2, SEG])
    kqp = sb("kqp", [P, 2, 2, SEG])
    e = sb("e", [P, 2, 2 * SEG])
    ct = sb("ct", [P, LEVELS, CH, P])
    ysb = sb("ysb", [P, LEVELS, CH, P])
    bt = sb("bt", [P, 2, CH, P])
    tm = sb("tm", [P, CH, P])
    xm = sb("xm", [P, 2, CH, P])
    cross = sb("cross", [P, 2, 2, P])
    u = sb("u", [P, CH, KW])
    rest = sb("rest", [P, 2, KW])
    o_sb = sb("o_sb", [P, SEG])
    osq = sb("osq", [P, SEG])
    orn = sb("orn", [P, SEG])
    og = sb("og", [P, SEG])
    names = ("const zeroed w_even w_odd decay_set proj_done raw_kept g_done z_done tail_done low_done ln1_done "
             "sp_done a_done gt_done sg_done tap silu_done vt_done v_kept beta_done sq_done ssq_done ln_done "
             "rn_done kn_done kq_done dg_done ab_done ct_done bt_done upq upp e_done y_done yk d_done tx_done t_init x_done x_kept o_kept u_done u_kept "
             "r_done rs_done o_done osq_done oss_done or_ln or_done og_mul og_done out_done xadd").split()
    s = {n: c.sem("kda_" + n) for n in names}
    e_at = [0]
    for lv in range(LEVELS):
        e_at.append(e_at[-1] + (SEG >> lv))

    with own, nc.Block() as block:

        weights = ((wqkv, "qkv", "o p k g m -> p (o k) g m"), (wfg2, "fg2", "o p g m -> p (o g) m"),
                   (wo, "o", "o p m -> p (o m)"), (taps, "taps", "o p g m -> p (o g) m"),
                   (dt_bias, "dt_bias", "o p m -> p (o m)"), (sel, "sel", "o p m -> p (o m)"))

        def load_head(sp, head, e):
            for place, n, how in weights:
                sp.dma_start(place[:, e:e + 1] if place is dt_bias else place[:, e],
                             w[n][bass.ds(head, 1)].rearrange(how)).then_inc(s[("w_even", "w_odd")[e]], 16)

        @block.sync
        def _(sp):
            sp.dma_start(o_norm[:], w["o_norm"]).then_inc(s["const"], 16)
            sp.dma_start(masks[:], w["masks"]).then_inc(s["const"], 16)
            load_head(sp, 0, 0)
            load_head(sp, 1, 1)
            with nc.sync.Fori(0, KH // 2 - 1) as i:
                sp.wait_ge(s["xadd"], i * 16 + 9)
                load_head(sp, i * 2 + 2, 0)
                sp.wait_ge(s["xadd"], i * 16 + 17)
                load_head(sp, i * 2 + 3, 1)

        def head_loaded(eng, i, m):
            if m % 8 == 0:
                eng.wait_ge(s["w_even"], i * 96 + 12 * m + 96)
            elif m % 8 == 4:
                eng.wait_ge(s["w_odd"], i * 96 + 96)

        def segments(eng, front, core, outputs):
            def step(i, m):
                last = isinstance(i, int) and i * 8 + m == KH * NSEG - 1
                core(i * 8 + m, m,
                     lambda piece: None if last else front(i, i * 8 + m + 1, m + 1, piece),
                     lambda piece: behind(i, m, 1 + piece // 7, piece))

            def behind(i, m, back, piece):
                if not (isinstance(i, int) and i * 8 + m < back):
                    outputs(i * 8 + m - back, (m - back) % 8, piece)

            for piece in range(LEVELS):
                front(0, 0, 0, piece)
            for m in range(2):
                step(0, m)
            with eng.Fori(0, KH // 2 - 1) as i:
                for m in range(2, 10):
                    step(i, m)
            for m in range(2, 8):
                step(KH // 2 - 1, m)
            for piece in (7, 8):
                outputs(KH * NSEG - 2, 6, piece)
            for piece in range(9):
                outputs(KH * NSEG - 1, 7, piece)

        def front_pe(pe, i, k, m, piece):
            cols = slice(SEG * (m % 4), SEG * (m % 4 + 1))
            e_ = m // 4 % 2
            if piece == 0:
                head_loaded(pe, i, m)
                pe.wait_ge(s["ln_done"], k + 1)
            if piece < 2:
                if piece == 1:
                    pe.wait_ge(s["kq_done"], k + 1)
                for g in ((0, 1), (2,))[piece]:
                    for j in range(KD):
                        last = nc.tensor.matmul(c.bank[:, g, :], wqkv[:, e_, j, g, :], c.x_t[:, j, cols],
                                                start=j == 0, stop=j == 1)
                last.then_inc(s["proj_done"], 1)
            if piece == 1:
                pe.wait_ge(s["sg_done"], k + 1)
                nc.tensor.matmul(c.bank[:, 3, :], wfg2[:, e_, 0, :], xf_t[:, cols], start=True, stop=True
                                 ).then_inc(s["g_done"], 1)
            elif piece == 2:
                pe.wait_ge(s["z_done"], k + 1)
                nc.tensor.matmul(c.bank[:, 3, :], wfg2[:, e_, 1, :], xg_t[:, cols], start=True, stop=True
                                 ).then_inc(s["gt_done"], 1)
            elif piece == 4:
                pe.wait_ge(s["silu_done"], k * 2 + 3)
                for j in range(CH):
                    last = nc.tensor.transpose(c.bank[:, 2, P * j:P * (j + 1)], act_out[:, 2, P * j:P * (j + 1)],
                                               c.ident[:])
                last.then_inc(s["vt_done"], 1)
                pe.wait_ge(s["sq_done"], k + 1)
                for g in range(2):
                    last = nc.tensor.matmul(c.bank[:, g, :], c.ones[:], sq[:, g, :], start=True, stop=True)
                last.then_inc(s["ssq_done"], 1)
            elif piece == 5:
                pe.wait_ge(s["v_kept"], k + 1)
                nc.tensor.matmul(c.bank[:, 2, :], sel[:, e_, :], beta[:, cols], start=True, stop=True
                                 ).then_inc(s["beta_done"], 1)

        def pairs(pe, k, m, lv):
            pr = m % 2
            if lv:
                pe.wait_ge(s["upq"], k * 7 + lv)
                pe.wait_ge(s["upp"], k * 7 + lv)
                pe.wait_ge(s["bt_done"], k * 8 + lv + 1)
            for ch in range(CH):
                right = halves_of(kqp[:, pr, :, P * ch:P * (ch + 1)], 1 << lv, 1)
                last = nc.tensor.matmul(c.bank[:, 4, P * ch:P * (ch + 1)], kq[:, pr, P * ch:P * (ch + 1)],
                                        right, start=True, stop=True)
            last.then_inc(s["ab_done"], 1)

        def core_pe(pe, k, m, front, outputs):
            pr = m % 2
            x_ = xm[:, pr]
            pe.wait_ge(s["kq_done"], k + 2)
            pairs(pe, k, m, 0)
            pe.wait_ge(s["tx_done"], k * 7 + 1)
            for ch in range(CH):
                last = nc.tensor.matmul(c.bank[:, 7, P * ch:P * (ch + 1)], kq[:, pr, P * ch:P * (ch + 1)],
                                        qn[:, pr, P * ch:P * (ch + 1)], start=True, stop=True)
            last.then_inc(s["dg_done"], 1)
            outputs(7)
            for lv in range(LEVELS):
                if lv + 1 < LEVELS:
                    pairs(pe, k, m, lv + 1)
                if lv == 0:
                    outputs(8)
                    pe.wait_ge(s["x_kept"], k + 1)
                pe.wait_ge(s["ct_done"], k * 7 + lv + 1)
                if lv == LEVELS - 1:
                    front(5)
                if lv:
                    pe.wait_ge(s["tx_done"], k * 7 + lv + 1)
                for ch in range(CH):
                    left = c.ident[:] if lv == 0 else tm[:, ch, :]
                    last = nc.tensor.matmul(c.bank[:, 6, 64 * ch:64 * ch + 64], ct[:, lv, ch, :],
                                            halves_of(left, 1 << lv, 0), start=True, stop=True)
                last.then_inc(s["y_done"], 1)
                outputs(lv)
                if lv != 5:
                    front(lv)
                if lv:
                    pe.wait_ge(s["yk"], k * 6 + lv)
                    for ch in range(CH):
                        if lv + 1 < LEVELS:
                            nc.tensor.matmul(c.bank[:, 7, 64 * ch:64 * ch + 64], x_[:, ch, :],
                                             halves_of(ysb[:, lv, ch, :], 1 << lv, 0), start=True, stop=True)
                        last = nc.tensor.matmul(c.bank[:, 7, 256 + 64 * ch:320 + 64 * ch], ysb[:, lv, ch, :],
                                                halves_of(x_[:, ch, :], 1 << lv, 1), start=True, stop=True)
                    last.then_inc(s["d_done"], 1)
            pe.wait_ge(s["upq"], k * 7 + 7)
            pe.wait_ge(s["upp"], k * 7 + 7)
            pe.wait_ge(s["bt_done"], k * 8 + 8)
            for b in range(2):
                last = nc.tensor.matmul(c.bank[:, 6, 2 * P * b:2 * P * (b + 1)],
                                        kq[:, pr, 2 * P * b:2 * P * b + P],
                                        kqp[:, pr, :, 2 * P * b + P:2 * P * (b + 1)], start=True, stop=True)
            last.then_inc(s["x_done"], 1)

        def outputs_pe(pe, k, m, piece):
            x_, b_, v_ = xm[:, m % 2], bt[:, m % 2], vals[:, m % 4]
            if piece == 0:
                pe.wait_ge(s["tx_done"], k * 7 + 8)
                pe.wait_ge(s["v_kept"], k + 1)
                pe.wait_ge(s["xadd"], k * 2 + 1)
                for b in range(2):
                    last = nc.tensor.matmul(c.bank[:, 5, P * b:P * (b + 1)], x_[:, 2 * b, :], v_[:, 2 * b, :],
                                            start=True, stop=True)
                last.then_inc(s["u_done"], 1)
            elif piece == 1:
                pe.wait_ge(s["x_kept"], k + 2)
                pe.wait_ge(s["u_kept"], k * 2 + 1)
                for b in range(2):
                    last = nc.tensor.matmul(c.bank[:, 5, P * b:P * (b + 1)], cross[:, b, 0, :], u[:, 2 * b, :],
                                            start=True, stop=True)
                last.then_inc(s["r_done"], 1)
            elif piece == 2:
                pe.wait_ge(s["rs_done"], k + 1)
                for b in range(2):
                    last = nc.tensor.matmul(c.bank[:, 5, P * b:P * (b + 1)], x_[:, 2 * b + 1, :], rest[:, b, :],
                                            start=True, stop=True)
                last.then_inc(s["u_done"], 1)
            elif piece == 3:
                pe.wait_ge(s["bt_done"], k * 8 + 8)
                pe.wait_ge(s["u_kept"], k * 2 + 2)
                for b in range(2):
                    nc.tensor.matmul(c.bank[:, 5, 2 * P * b:2 * P * b + P], u[:, 2 * b, :], b_[:, 2 * b, :],
                                     start=True, stop=True)
                    o1 = c.bank[:, 5, 2 * P * b + P:2 * P * (b + 1)]
                    nc.tensor.matmul(o1, u[:, 2 * b, :], cross[:, b, 1, :], start=True, stop=False)
                    last = nc.tensor.matmul(o1, u[:, 2 * b + 1, :], b_[:, 2 * b + 1, :], start=False, stop=True)
                last.then_inc(s["o_done"], 1)
            elif piece == 4:
                pe.wait_ge(s["osq_done"], k + 1)
                pe.wait_ge(s["o_kept"], k + 1)
                nc.tensor.matmul(c.bank[:, 5, :], c.ones[:], osq[:], start=True, stop=True
                                 ).then_inc(s["oss_done"], 1)
            elif piece >= 7:
                if piece == 7:
                    pe.wait_ge(s["og_done"], k + 1)
                else:
                    pe.wait_ge(s["xadd"], k * 2 + 2)
                for ch in range(2 * (piece - 7), 2 * (piece - 7) + 2):
                    last = nc.tensor.matmul(c.bank[:, 5, D * (ch % 2):D * (ch % 2 + 1)],
                                            og[:, P * ch:P * (ch + 1)], wo[:, m // 4 % 2, :],
                                            start=True, stop=True)
                last.then_inc(s["out_done"], 1)

        @block.tensor
        def _(pe):
            pe.wait_ge(s["const"], 32)
            pe.wait_ge(s["zeroed"], 2)
            pe.sem_inc(s["y_done"], 1)
            segments(nc.tensor, lambda *a: front_pe(pe, *a), lambda *a: core_pe(pe, *a),
                     lambda *a: outputs_pe(pe, *a))

        def front_act(act, i, k, m, piece):
            pr = m % 2
            if piece == 0:
                head_loaded(act, i, m)
            if piece < 2:
                g = (slice(0, 2), slice(2, 3))[piece]
                act.wait_ge(s["proj_done"], k * 2 + piece + 1)
                nc.scalar.activation(raw[:, g, :, 3:], c.bank[:, g, :].rearrange("p g (b t) -> p g b t", b=2),
                                     ACT.Copy).then_inc(s["raw_kept"], 1)
            if piece == 1:
                act.wait_ge(s["g_done"], k + 1)
                nc.scalar.activation(z[:], c.bank[:, 3, :], ACT.Identity, bias=dt_bias[:, m // 4 % 2:m // 4 % 2 + 1]
                                     ).then_inc(s["z_done"], 1)
                act.wait_ge(s["z_done"], k + 1)
                nc.scalar.activation(tail[:], z[:], ACT.Abs).then_inc(s["tail_done"], 1)
                act.wait_ge(s["tail_done"], k * 2 + 1)
                nc.scalar.activation(tail[:], tail[:], ACT.Exp, scale=-1.0).then_inc(s["tail_done"], 1)
            elif piece == 2:
                act.wait_ge(s["low_done"], k * 2 + 2)
                nc.scalar.activation(low[:], low[:], ACT.Ln, bias=1.0).then_inc(s["ln1_done"], 1)
            elif piece == 3:
                act.wait_ge(s["tap"], k * 8 + 4)
                act.wait_ge(s["kq_done"], k + 1)
                nc.scalar.activation(act_out[:, 0:2], conv[:, 0:2], ACT.Silu).then_inc(s["silu_done"], 1)
                act.wait_ge(s["silu_done"], k * 2 + 2)
                nc.scalar.activation(sq[:], act_out[:, 0:2, :], ACT.Square).then_inc(s["sq_done"], 1)
                act.wait_ge(s["tap"], k * 8 + 8)
                nc.scalar.activation(act_out[:, 2], conv[:, 2], ACT.Silu).then_inc(s["silu_done"], 1)
            elif piece == 4:
                act.wait_ge(s["vt_done"], k + 1)
                nc.scalar.activation(vals[:, m % 4].rearrange("p c v -> p (c v)"), c.bank[:, 2, :], ACT.Copy
                                     ).then_inc(s["v_kept"], 1)
                act.wait_ge(s["gt_done"], k + 1)
                nc.scalar.activation(sgate[:, m % 4, :], c.bank[:, 3, :], ACT.Sigmoid).then_inc(s["sg_done"], 1)
            elif piece == 5:
                act.wait_ge(s["ssq_done"], k + 1)
                nc.scalar.activation(rn[:], c.bank[:, 0:2, :], ACT.Ln, bias=eps6[:, 0:1]).then_inc(s["ln_done"], 1)
                act.wait_ge(s["ln_done"], k + 2)
                nc.scalar.activation(rn[:], rn[:], ACT.Exp, scale=-0.5).then_inc(s["rn_done"], 1)
            elif piece == 6:
                act.wait_ge(s["sp_done"], k * 2 + 2)
                if m % 4 == 0:
                    act.wait_ge(s["decay_set"], i * 2 + m // 4 + 1)
                nc.scalar.activation(e[:, pr, 0:SEG], z[:], ACT.Exp, scale=decay[:, m // 4 % 2:m // 4 % 2 + 1]
                                     ).then_inc(s["a_done"], 1)

        def core_act(act, k, m, front, outputs):
            for lv in range(LEVELS):
                if lv:
                    act.wait_ge(s["y_done"], k * 7 + lv + 2)
                    nc.scalar.activation(halves_of(ysb[:, lv], 1 << lv, 0),
                                         c.bank[:, 6, 0:256].rearrange("p (c g m) -> p c g m", c=CH, m=1 << lv),
                                         ACT.Copy).then_inc(s["yk"], 1)
                if lv == 6:
                    front(lv)
                    outputs(lv)
                else:
                    outputs(lv)
                    front(lv)
            act.wait_ge(s["x_done"], k + 1)
            nc.scalar.activation(cross[:].rearrange("p b g t -> p (b g t)"), c.bank[:, 6, :], ACT.Copy
                                 ).then_inc(s["x_kept"], 1)

        def outputs_act(act, k, m, piece):
            if piece in (0, 2):
                half = piece // 2
                act.wait_ge(s["u_done"], k * 2 + half + 1)
                nc.scalar.activation(u[:, half:CH:2, :],
                                     c.bank[:, 5, 0:256].rearrange("p (b v) -> p b v", b=2), ACT.Copy
                                     ).then_inc(s["u_kept"], 1)
            elif piece == 3:
                act.wait_ge(s["o_done"], k + 1)
                nc.scalar.activation(osq[:], c.bank[:, 5, :], ACT.Square).then_inc(s["osq_done"], 1)
                nc.scalar.activation(o_sb[:], c.bank[:, 5, :], ACT.Copy).then_inc(s["o_kept"], 1)
            elif piece == 5:
                act.wait_ge(s["oss_done"], k + 1)
                nc.scalar.activation(orn[:], c.bank[:, 5, :], ACT.Ln, scale=1.0 / KW, bias=eps5[:, 0:1]
                                     ).then_inc(s["or_ln"], 1)
            elif piece == 6:
                act.wait_ge(s["or_ln"], k + 1)
                nc.scalar.activation(orn[:], orn[:], ACT.Exp, scale=-0.5).then_inc(s["or_done"], 1)

        @block.scalar
        def _(act):
            act.sem_inc(s["ln_done"], 1)
            act.sem_inc(s["sg_done"], 1)
            act.sem_inc(s["silu_done"], 1)
            act.sem_inc(s["x_kept"], 1)
            act.wait_ge(s["zeroed"], 2)
            segments(nc.scalar, lambda *a: front_act(act, *a), lambda *a: core_act(act, *a),
                     lambda *a: outputs_act(act, *a))

        def convolve(dve, k, m, g, steps, at):
            for count, step in enumerate(steps):
                tap = 3 - step
                if step:
                    dve.wait_ge(s["tap"], k * 8 + at + count)
                for g_ in g:
                    out = conv[:, g_, :].rearrange("p (b t) -> p b t", b=2)
                    src = raw[:, g_, :, tap:tap + T]
                    tp = taps[:, m // 4 % 2, g_]
                    if step == 0:
                        last = nc.vector.tensor_scalar(out, src, tp[:, 3:4], tp[:, 4:5], ALU.mult, ALU.add)
                    else:
                        last = nc.vector.scalar_tensor_tensor(out, src, tp[:, tap:tap + 1], out, ALU.mult, ALU.add)
                last.then_inc(s["tap"], 1)

        def front_dve(dve, i, k, m, piece):
            pr = m % 2
            if piece == 0:
                head_loaded(dve, i, m)
                if m % 4 == 0:
                    nc.vector.tensor_copy(decay[:, m // 4 % 2:m // 4 % 2 + 1], neg_a[:, bass.ds(i * 2 + m // 4, 1)]
                                          ).then_inc(s["decay_set"], 1)
                dve.wait_ge(s["raw_kept"], k * 2 + 1)
                dve.wait_ge(s["silu_done"], k * 2 + 1)
            elif piece == 1:
                convolve(dve, k, m, (0, 1), (0, 1), 0)
            elif piece == 2:
                dve.wait_ge(s["tail_done"], k * 2 + 2)
                nc.vector.tensor_scalar(low[:], tail[:], 1.0, 1.0, ALU.add, ALU.subtract).then_inc(s["low_done"], 1)
                dve.wait_ge(s["low_done"], k * 2 + 1)
                nc.vector.tensor_tensor(tail[:], tail[:], low[:], ALU.subtract).then_inc(s["low_done"], 1)
                convolve(dve, k, m, (0, 1), (2, 3), 2)
            elif piece == 3:
                dve.wait_ge(s["raw_kept"], k * 2 + 2)
                convolve(dve, k, m, (2,), range(4), 4)
            elif piece == 4:
                dve.wait_ge(s["ln1_done"], k + 1)
                nc.vector.scalar_tensor_tensor(z[:], z[:], 0.0, low[:], ALU.max, ALU.add).then_inc(s["sp_done"], 1)
                dve.wait_ge(s["sp_done"], k * 2 + 1)
                nc.vector.tensor_tensor(z[:], z[:], tail[:], ALU.add).then_inc(s["sp_done"], 1)
            elif piece == 6:
                dve.wait_ge(s["rn_done"], k + 1)
                nc.vector.tensor_tensor(kn[:], act_out[:, 1, :], rn[:, 1, :], ALU.mult)
                nc.vector.scalar_tensor_tensor(qn[:, pr, :], act_out[:, 0, :], KW ** -0.5, rn[:, 0, :], ALU.mult,
                                               ALU.mult).then_inc(s["kn_done"], 1)
                dve.wait_ge(s["kn_done"], k + 1)
                dve.wait_ge(s["a_done"], k + 1)
                nc.vector.tensor_tensor(kqp[:, pr, 0, :], kn[:], e[:, pr, 0:SEG], ALU.mult)
                nc.vector.tensor_tensor(kqp[:, pr, 1, :], qn[:, pr, :], e[:, pr, 0:SEG], ALU.mult)
                dve.wait_ge(s["beta_done"], k + 1)
                nc.vector.tensor_tensor(kq[:, pr, :], kn[:], c.bank[:, 2, :], ALU.mult).then_inc(s["kq_done"], 1)

        def level_dve(dve, k, pr, lv):
            m = 1 << lv
            dve.wait_ge(s["bt_done"], k * 8 + lv + 1)
            dve.wait_ge(s["ab_done"], k * 7 + lv + 1)
            ab = c.bank[:, 4, :].rearrange("p (c two g m) -> p c two g m", two=2, c=CH, m=m)
            mask = masks[:, lv, :].unsqueeze(1).broadcast_to([P, CH, 64]).rearrange("p c (g m) -> p c g m", m=m)
            mask_i = masks_i[:, lv, :].unsqueeze(1).broadcast_to([P, CH, 64]).rearrange("p c (g m) -> p c g m", m=m)
            nc.vector.tensor_tensor(halves_of(ct[:, lv], m, 1), ab[:, :, 0], mask, ALU.mult).then_inc(s["ct_done"], 1)
            nc.vector.copy_predicated(halves_of(bt[:, pr], m, 1), mask_i, ab[:, :, 1]).then_inc(s["bt_done"], 1)
            if lv:
                dve.wait_ge(s["e_done"], k * 6 + lv)
                dve.wait_ge(s["upq"], k * 7 + lv)
            g = SEG >> (lv + 1)
            pairs_e = e[:, pr, e_at[lv]:e_at[lv + 1]].rearrange("p (g two) -> p g two", two=2)
            left = halves_of(kq[:, pr, :], m, 0)
            nc.vector.tensor_tensor(left, left, pairs_e[:, :, 1:2].broadcast_to([P, g, m]), ALU.mult
                                    ).then_inc(s["upq"], 1)
            if lv + 1 < LEVELS:
                nc.vector.tensor_tensor(e[:, pr, e_at[lv + 1]:e_at[lv + 1] + g], pairs_e[:, :, 0], pairs_e[:, :, 1],
                                        ALU.mult).then_inc(s["e_done"], 1)

        def inverse_dve(dve, k, pr, lv):
            m = 1 << lv
            eye = c.ident[:].unsqueeze(1).broadcast_to([P, CH, P])
            if lv == 0:
                dve.wait_ge(s["ct_done"], k * 7 + 1)
                nc.vector.tensor_tensor(xm[:, pr], eye, ct[:, 0], ALU.subtract)
                dve.wait_ge(s["t_init"], k + 1)
                dve.wait_ge(s["y_done"], k * 7 + 2)
                left = halves_of(tm[:], m, 0)
                y = c.bank[:, 6, 0:256].rearrange("p (c g m) -> p c g m", c=CH, m=m)
                nc.vector.tensor_tensor(left, left, y, ALU.subtract).then_inc(s["tx_done"], 1)
                return
            dve.wait_ge(s["tx_done"], k * 7 + lv + 1)
            dve.wait_ge(s["d_done"], k * 6 + lv)
            dt_, dx = (c.bank[:, 7, 256 * j:256 * (j + 1)].rearrange("p (c g m) -> p c g m", c=CH, m=m)
                       for j in range(2))
            if lv + 1 < LEVELS:
                left = halves_of(tm[:], m, 0)
                nc.vector.tensor_tensor(left, left, dt_, ALU.subtract)
            right = halves_of(xm[:, pr], m, 1)
            nc.vector.tensor_tensor(right, right, dx, ALU.subtract).then_inc(s["tx_done"], 1)

        def core_dve(dve, k, m, front, outputs):
            pr = m % 2
            dve.wait_ge(s["dg_done"], k + 1)
            nc.vector.tensor_tensor(bt[:, pr], c.bank[:, 7, :].rearrange("p (c t) -> p c t", c=CH),
                                    c.ident[:].unsqueeze(1).broadcast_to([P, CH, P]), ALU.mult
                                    ).then_inc(s["bt_done"], 1)
            level_dve(dve, k, pr, 0)
            outputs(7)
            for lv in range(LEVELS):
                if lv + 1 < LEVELS:
                    level_dve(dve, k, pr, lv + 1)
                if lv == 0:
                    outputs(8)
                else:
                    front(lv)
                outputs(lv)
                inverse_dve(dve, k, pr, lv)
                if lv == 0:
                    front(lv)

        def outputs_dve(dve, k, m, piece):
            if piece == 1:
                dve.wait_ge(s["r_done"], k + 1)
                nc.vector.tensor_tensor(rest[:], vals[:, m % 4, 1:CH:2, :],
                                        c.bank[:, 5, 0:256].rearrange("p (b v) -> p b v", b=2), ALU.subtract
                                        ).then_inc(s["rs_done"], 1)
            elif piece == 6:
                dve.wait_ge(s["or_done"], k + 1)
                nc.vector.tensor_tensor(og[:], o_sb[:], orn[:], ALU.mult).then_inc(s["og_mul"], 1)
                dve.wait_ge(s["og_mul"], k + 1)
                nc.vector.scalar_tensor_tensor(og[:], og[:], o_norm[:, 0:1], sgate[:, m % 4, :], ALU.mult, ALU.mult
                                               ).then_inc(s["og_done"], 1)
            elif piece >= 7:
                half = piece - 7
                dve.wait_ge(s["out_done"], k * 2 + half + 1)
                tile = 4 * (m % 4) + 2 * half
                x = c.x_tok[:, tile:tile + 2, :].rearrange("p t d -> p (t d)")
                nc.vector.tensor_tensor(x, x, c.bank[:, 5, :], ALU.add).then_inc(s["xadd"], 1)

        @block.vector
        def _(dve):
            dve.sem_inc(s["kq_done"], 1)
            dve.sem_inc(s["xadd"], 1)
            dve.sem_inc(s["tx_done"], 1)
            nc.vector.memset(eps6[:], 1e-6)
            nc.vector.memset(eps5[:], 1e-5)
            nc.vector.memset(raw[:, :, :, 0:3], 0.0)
            nc.vector.memset(ct[:], 0.0)
            nc.vector.memset(ysb[:], 0.0).then_inc(s["zeroed"], 1)
            dve.wait_ge(s["const"], 32)
            nc.vector.tensor_copy(masks_i[:], masks[:]).then_inc(s["zeroed"], 1)
            dve.wait_ge(s["zeroed"], 2)
            segments(nc.vector, lambda *a: front_dve(dve, *a), lambda *a: core_dve(dve, *a),
                     lambda *a: outputs_dve(dve, *a))

        def core_pool(pool, k, m_, front, outputs):
            pr = m_ % 2
            pool.wait_ge(s["y_done"], k * 7 + 1)
            nc.gpsimd.tensor_tensor(tm[:], c.ident[:].unsqueeze(1).broadcast_to([P, CH, P]),
                                    c.ident[:].unsqueeze(1).broadcast_to([P, CH, P]), ALU.mult
                                    ).then_inc(s["t_init"], 1)
            for lv in range(LEVELS):
                m = 1 << lv
                if lv:
                    pool.wait_ge(s["e_done"], k * 6 + lv)
                pool.wait_ge(s["ab_done"], k * 7 + lv + 1)
                g = SEG >> (lv + 1)
                factor = e[:, pr, e_at[lv]:e_at[lv + 1]].rearrange("p (g two) -> p g two", two=2)[:, :, 0:1]
                for j in range(2):
                    right = halves_of(kqp[:, pr, j, :], m, 1)
                    last = nc.gpsimd.tensor_tensor(right, right, factor.broadcast_to([P, g, m]), ALU.mult)
                last.then_inc(s["upp"], 1)

        @block.gpsimd
        def _(pool):
            nothing = lambda *a: None
            segments(nc.gpsimd, nothing, lambda *a: core_pool(pool, *a), nothing)


def host_layout(a):
    f = {}

    def cols(m):
        m = np.asarray(m)
        return np.ascontiguousarray(m.reshape(m.shape[0] // P, P, m.shape[1]).transpose(1, 0, 2))

    x = np.asarray(a["x"])
    f["x_tok"] = x.reshape(NT, P, D).transpose(1, 0, 2)
    f["x_t"] = x.reshape(TOK, KD, P).transpose(2, 1, 0)
    f["ident"] = np.eye(P, dtype=np.float32)
    L = {k[8:]: np.asarray(v) for k, v in a.items() if k.startswith("L0_attn_")}
    f["ssm_dt_lam"] = np.stack([cols(L["Wdt"].T), cols(L["Wlam"].T)], axis=2)
    f["ssm_A_log"] = L["A_log"].reshape(SH, 1)
    f["ssm_x"] = cols(L["Wx"].T)
    f["ssm_z"] = cols(L["Wz"].T)
    f["ssm_out"] = cols(L["Wout"].T)

    def pair_rows(m):
        return m.reshape(PAIRS, 2, 64, 2, D).transpose(0, 3, 1, 2, 4).reshape(PAIRS, 2, P, D)

    rows = np.concatenate([L["Wth"].reshape(PAIRS, 1, P, D), pair_rows(L["WB"]), pair_rows(L["WC"])], axis=1)
    f["ssm_pair"] = rows.reshape(PAIRS, 5, P, KD, P).transpose(0, 4, 3, 1, 2)
    b = [L[k].reshape(PAIRS, 2, 64, 2).transpose(0, 3, 1, 2).reshape(PAIRS, 2, P) for k in ("B_bias", "C_bias")]
    f["ssm_bias"] = np.concatenate(b, axis=1).transpose(2, 0, 1)
    f["ssm_norm_w"] = np.stack([np.tile(L[k][j::2], 2) for k in ("Bn_w", "Cn_w") for j in range(2)], axis=1)
    f["ssm_above"] = np.eye(P, P + 1, 1, dtype=np.float32)
    f["ssm_halves"] = np.kron(np.eye(2, dtype=np.float32), np.ones((64, 64), np.float32))
    ctx_t = np.asarray(a["ctx_1024"]).reshape(B * S2, DC).T
    mask = np.asarray(a["mask_BxS2_bf1"]).view(np.uint8)
    for tag, name in (("xm_", "L0_xattn_"), ("xn_", "L1_xattn_")):
        L = {k[len(name):]: np.asarray(v) for k, v in a.items() if k.startswith(name)}
        f[tag + "ctx"] = ctx_t
        f[tag + "q"] = cols(L["Wq"])
        f[tag + "o"] = cols(L["Wo"])
        f[tag + "k"] = L["Wk"]
        f[tag + "v"] = L["Wv"].reshape(DC, 1, -1) if tag == "xm_" else (
            L["Wv"].reshape(DC, XP, 2, XD).transpose(0, 2, 1, 3).reshape(DC, 2, XP * XD))
    f["xn_g"] = np.stack([L["gk"], L["gq"]], axis=1)
    f["xm_mask_row"] = mask.reshape(B * S2)
    f["xm_mask_col"] = np.concatenate([mask.T, mask.T])
    L = {k[7:]: np.asarray(v) for k, v in a.items() if k.startswith("L0_ffn_")}
    f["had_rows"] = np.concatenate([L[k].reshape(HID0 // P, P, D) for k in ("W_gate", "W_up")]).transpose(1, 0, 2)
    f["had_down"] = L["W_down"].reshape(KD, P, HID0).transpose(1, 0, 2)
    f["had_su_in"] = L["SU_ug"].reshape(KD, P).T
    f["had_su_out"] = L["SU_dp"].reshape(HID0 // P, P).T
    f["had_down_scale"] = L["Wscale_dp"].reshape(KD, P).T
    f["had_scales"] = L["Wscale_ug"].reshape(2, HID0 // P, P)[::-1].transpose(2, 0, 1)
    L = {k[7:]: np.asarray(v) for k, v in a.items() if k.startswith("L1_ffn_")}
    f["deq_in"] = np.stack([cols(L["wq_gate"].T), cols(L["wq_up"].T)], axis=2)
    f["deq_out"] = L["wq_down"].T
    f["deq_s_down"] = L["s_down"]
    f["deq_s_gate"] = L["s_gate"].reshape(HID1, 1)
    f["deq_s_up"] = L["s_up"].reshape(HID1, 1)
    L = {k[8:]: np.asarray(v) for k, v in a.items() if k.startswith("L1_attn_")}

    def by_head(m):
        return m.reshape(m.shape[0], KH, KW).transpose(1, 0, 2)

    f["kda_fg"] = np.stack([cols(L["Wfa"]), cols(L["Wga"])], axis=2)
    f["kda_b"] = cols(L["Wb"])
    f["kda_A_log"] = L["A_log"]
    f["kda_o_norm"] = L["o_norm_w"].reshape(KW, 1)
    f["kda_qkv"] = np.stack([by_head(L[k]) for k in ("Wq", "Wk", "Wv")], axis=2).reshape(
        KH, KD, P, 3, KW).transpose(0, 2, 1, 3, 4)
    f["kda_fg2"] = np.stack([by_head(L["Wfb"]), by_head(L["Wgb"])], axis=2)
    f["kda_o"] = L["Wo"].reshape(KH, KW, D)
    f["kda_taps"] = np.stack([np.concatenate([L[f"conv_{g}_w"], L[f"conv_{g}_b"][:, None]], axis=1).reshape(
        KH, KW, 5) for g in "qkv"], axis=2)
    f["kda_dt_bias"] = L["dt_bias"].reshape(KH, KW, 1)
    f["kda_sel"] = np.repeat(np.eye(KH, dtype=np.float32)[:, :, None], P, axis=2)
    masks = np.zeros((P, LEVELS, P // 2), np.float32)
    for lv in range(LEVELS):
        m = 1 << lv
        right = np.arange(P).reshape(-1, 2, m)[:, 1].ravel()
        rows = np.arange(P)
        masks[:, lv] = (rows[:, None] // (2 * m) == right[None, :] // (2 * m)) & ((rows[:, None] // m) % 2 == 0)
    f["kda_masks"] = masks
    return {k: np.ascontiguousarray(v) for k, v in f.items()}


def part(d, prefix):
    return {k[len(prefix):]: v for k, v in d.items() if k.startswith(prefix)}


def program(nc, d, out_d, only=None):
    with ExitStack() as ctx:
        c = Core(nc, ctx)
        layers = [
            (ssm, "ssm_"),
            (lambda c, w: cross_attention(c, w, False), "xm_"),
            (hadamard_ffn, "had_"),
            (kda, "kda_"),
            (lambda c, w: cross_attention(c, w, True), "xn_"),
            (dequant_ffn, "deq_"),
        ]
        chosen = range(len(layers)) if only is None else [only]
        opened = [layer(c, part(d, prefix)) for layer, prefix in (layers[n] for n in chosen)]
        load_start(c, d["x_tok"], d["x_t"], d["ident"], next(opened[0]))
        for n, layer in enumerate(opened):
            for _ in layer:
                pass
            last = n == len(opened) - 1
            layer_norm(c, f"norm{n}", out_d if last else None, () if last else next(opened[n + 1]))
            if not last:
                c.release_sems()
        c.sems.close()


def kernel(**inputs):
    from concourse import bacc
    from concourse.bass_utils import run_bass_kernel_spmd

    nc = bacc.Bacc("TRN2", target_bir_lowering=False, num_devices=1)
    arrays = host_layout(inputs)
    d = {k: nc.dram_tensor("in_" + k, v.shape, mybir.dt.from_np(v.dtype), kind="ExternalInput").ap()
         for k, v in arrays.items()}
    out = nc.dram_tensor("out_x", (P, NT, D), F32, kind="ExternalOutput").ap()
    program(nc, d, out)
    r = run_bass_kernel_spmd(nc, [{"in_" + k: v for k, v in arrays.items()}], core_ids=[0])
    return np.asarray(r.results[0]["out_x"]).transpose(1, 0, 2).reshape(B, T, D)
```
